# Optimizing a Trainium2 kernel written in Bass

```python
import numpy as np
import jax
import jax.numpy as jnp

def _softmax(x, axis=-1):
    return jax.nn.softmax(x, axis=axis)

def _gelu(x):
    return jax.nn.gelu(x, approximate=True)

def _silu(x):
    return jax.nn.silu(x)

def _sigmoid(x):
    return jax.nn.sigmoid(x)

def _layernorm(x, axis=-1, eps=1e-05):
    m = jnp.mean(x, axis=axis, keepdims=True)
    v = jnp.var(x, axis=axis, keepdims=True)
    return (x - m) / jnp.sqrt(v + eps)

def _scatter_add(tgt, idx, src, axis=0):
    return tgt.at[idx].add(src)

def _segment_sum(src, seg, n):
    return jax.ops.segment_sum(src, seg, n)
kernel_name = 'mk_adaln_ffn_d1_seqx_r8_26a2a9'

def setup_inputs(seed: int=0):
    np.random.seed(seed)
    _w = jnp.asarray

    def _rec_inputs():
        import jax
        import jax.numpy as jnp
        _rk = jax.random.key(seed)
        x = -0.0003929 + 0.9999 * jax.random.normal(jax.random.fold_in(_rk, 1), (32, 32, 256), jnp.float32)
        _lenS = 32 - jax.random.randint(jax.random.fold_in(_rk, 7), (32,), 0, max(1, 32 // 4) + 1, jnp.int32)
        _lenS2 = 32 - jax.random.randint(jax.random.fold_in(_rk, 8), (32,), 0, max(1, 32 // 4) + 1, jnp.int32)
        itok_B_0_7 = jax.random.randint(jax.random.fold_in(_rk, 11), (32,), 0, 8, jnp.int32)
        return (x, itok_B_0_7)
    x, itok_B_0_7 = _rec_inputs()

    def _L0_cond_setup():
        import jax, jax.numpy as jnp
        import numpy as np

        def _lora_linear(x, W, A, B, adapter_indices):
            base = jnp.einsum('bsd,df->bsf', x, W)
            Ai = A[adapter_indices]
            Bi = B[adapter_indices]
            lora = jnp.einsum('bsr,brf->bsf', jnp.einsum('bsd,bdr->bsr', x, Ai), Bi)
            return base + lora
        key = jax.random.key(seed)
        ks = jax.random.split(key, 10)
        H, I, N, R = (256, 1024, 8, 16)
        B, S = (4, 256)
        std_h = 1.0 / np.sqrt(H)
        std_i = 1.0 / np.sqrt(I)
        x = jax.random.normal(ks[0], (B, S, H), dtype=jnp.float32)
        adapter_indices = jax.random.randint(ks[1], (B,), 0, N, dtype=jnp.int32)
        Wg = jax.random.normal(ks[2], (H, I), dtype=jnp.float32) * std_h
        Wu = jax.random.normal(ks[3], (H, I), dtype=jnp.float32) * std_h
        Wd = jax.random.normal(ks[4], (I, H), dtype=jnp.float32) * std_i
        Ag = jax.random.normal(ks[5], (N, H, R), dtype=jnp.float32) * std_h
        Bg = jnp.zeros((N, R, I), dtype=jnp.float32) + 0.01
        Au = jax.random.normal(ks[6], (N, H, R), dtype=jnp.float32) * std_h
        Bu = jnp.zeros((N, R, I), dtype=jnp.float32) + 0.01
        Ad = jax.random.normal(ks[7], (N, I, R), dtype=jnp.float32) * std_i
        Bd = jnp.zeros((N, R, H), dtype=jnp.float32) + 0.01
        return {'x': x, 'Wg': Wg, 'Wu': Wu, 'Wd': Wd, 'Ag': Ag, 'Bg': Bg, 'Au': Au, 'Bu': Bu, 'Ad': Ad, 'Bd': Bd, 'adapter_indices': adapter_indices}
    _L0_cond_all = _L0_cond_setup()
    _L0_cond_in = {k: v for k, v in _L0_cond_all.items() if k in ('Wg', 'Wu', 'Wd', 'Ag', 'Bg', 'Au', 'Bu', 'Ad', 'Bd')}
    del _L0_cond_all

    def _L0_ffn_setup():
        import jax, jax.numpy as jnp
        import numpy as np
        EPS = 1e-05
        ROPE_BASE = 150000.0
        NHEADS = 32
        KVHEADS = 8
        HEAD_DIM = 64
        TOP_K = 4

        def _rms(x, w):
            return x * jax.lax.rsqrt(jnp.mean(x * x, -1, keepdims=True) + EPS) * w

        def _rope(q, k):
            S, hd = (q.shape[1], q.shape[-1])
            half = hd // 2
            inv = 1.0 / ROPE_BASE ** (jnp.arange(half, dtype=jnp.float32) / half)
            ang = jnp.arange(S, dtype=jnp.float32)[:, None] * inv
            cos = jnp.concatenate([jnp.cos(ang), jnp.cos(ang)], -1)[None, :, None, :]
            sin = jnp.concatenate([jnp.sin(ang), jnp.sin(ang)], -1)[None, :, None, :]

            def rot(t):
                t1, t2 = (t[..., :half], t[..., half:])
                return jnp.concatenate([-t2, t1], -1)
            return (q * cos + rot(q) * sin, k * cos + rot(k) * sin)
        key = jax.random.key(seed)
        ks = jax.random.split(key, 12)
        B, S, D, H, E = (1, 128, 256, 256, 16)
        s = 0.02
        return {'x': jax.random.normal(ks[0], (B, S, D), jnp.float32), 'ln_w': jnp.ones((D,), jnp.float32), 'ff_ln_w': jnp.ones((D,), jnp.float32), 'wq': jax.random.normal(ks[1], (D, NHEADS * HEAD_DIM), jnp.float32) * s, 'wk': jax.random.normal(ks[2], (D, KVHEADS * HEAD_DIM), jnp.float32) * s, 'wv': jax.random.normal(ks[3], (D, KVHEADS * HEAD_DIM), jnp.float32) * s, 'wo': jax.random.normal(ks[4], (NHEADS * HEAD_DIM, D), jnp.float32) * s, 'wg': jax.random.normal(ks[5], (D, E), jnp.float32) * s, 'w1': jax.random.normal(ks[6], (E, D, H), jnp.float32) * s, 'w3': jax.random.normal(ks[7], (E, D, H), jnp.float32) * s, 'w2': jax.random.normal(ks[8], (E, H, D), jnp.float32) * s}
    _L0_ffn_all = _L0_ffn_setup()
    _L0_ffn_in = {k: v for k, v in _L0_ffn_all.items() if k in ('ln_w', 'ff_ln_w', 'wq', 'wk', 'wv', 'wo', 'wg', 'w1', 'w3', 'w2')}
    del _L0_ffn_all
    return {'x': x, 'itok_B_0_7': itok_B_0_7, 'L0_cond_Wg': _L0_cond_in['Wg'], 'L0_cond_Wu': _L0_cond_in['Wu'], 'L0_cond_Wd': _L0_cond_in['Wd'], 'L0_cond_Ag': _L0_cond_in['Ag'], 'L0_cond_Bg': _L0_cond_in['Bg'], 'L0_cond_Au': _L0_cond_in['Au'], 'L0_cond_Bu': _L0_cond_in['Bu'], 'L0_cond_Ad': _L0_cond_in['Ad'], 'L0_cond_Bd': _L0_cond_in['Bd'], 'L0_ffn_ln_w': _L0_ffn_in['ln_w'], 'L0_ffn_ff_ln_w': _L0_ffn_in['ff_ln_w'], 'L0_ffn_wq': _L0_ffn_in['wq'], 'L0_ffn_wk': _L0_ffn_in['wk'], 'L0_ffn_wv': _L0_ffn_in['wv'], 'L0_ffn_wo': _L0_ffn_in['wo'], 'L0_ffn_wg': _L0_ffn_in['wg'], 'L0_ffn_w1': _L0_ffn_in['w1'], 'L0_ffn_w3': _L0_ffn_in['w3'], 'L0_ffn_w2': _L0_ffn_in['w2']}

def reference(x, itok_B_0_7, L0_cond_Wg, L0_cond_Wu, L0_cond_Wd, L0_cond_Ag, L0_cond_Bg, L0_cond_Au, L0_cond_Bu, L0_cond_Ad, L0_cond_Bd, L0_ffn_ln_w, L0_ffn_ff_ln_w, L0_ffn_wq, L0_ffn_wk, L0_ffn_wv, L0_ffn_wo, L0_ffn_wg, L0_ffn_w1, L0_ffn_w3, L0_ffn_w2):
    import jax
    import jax.numpy as jnp

    def _L0_cond_ref(x, Wg, Wu, Wd, Ag, Bg, Au, Bu, Ad, Bd, adapter_indices):
        import jax, jax.numpy as jnp
        import numpy as np

        def _lora_linear(x, W, A, B, adapter_indices):
            base = jnp.einsum('bsd,df->bsf', x, W)
            Ai = A[adapter_indices]
            Bi = B[adapter_indices]
            lora = jnp.einsum('bsr,brf->bsf', jnp.einsum('bsd,bdr->bsr', x, Ai), Bi)
            return base + lora
        gate = _lora_linear(x, Wg, Ag, Bg, adapter_indices)
        up = _lora_linear(x, Wu, Au, Bu, adapter_indices)
        h = jax.nn.silu(gate) * up
        return _lora_linear(h, Wd, Ad, Bd, adapter_indices)

    def _L0_ffn_ref(x, ln_w, ff_ln_w, wq, wk, wv, wo, wg, w1, w3, w2):
        import jax, jax.numpy as jnp
        import numpy as np
        EPS = 1e-05
        ROPE_BASE = 150000.0
        NHEADS = 32
        KVHEADS = 8
        HEAD_DIM = 64
        TOP_K = 4

        def _rms(x, w):
            return x * jax.lax.rsqrt(jnp.mean(x * x, -1, keepdims=True) + EPS) * w

        def _rope(q, k):
            S, hd = (q.shape[1], q.shape[-1])
            half = hd // 2
            inv = 1.0 / ROPE_BASE ** (jnp.arange(half, dtype=jnp.float32) / half)
            ang = jnp.arange(S, dtype=jnp.float32)[:, None] * inv
            cos = jnp.concatenate([jnp.cos(ang), jnp.cos(ang)], -1)[None, :, None, :]
            sin = jnp.concatenate([jnp.sin(ang), jnp.sin(ang)], -1)[None, :, None, :]

            def rot(t):
                t1, t2 = (t[..., :half], t[..., half:])
                return jnp.concatenate([-t2, t1], -1)
            return (q * cos + rot(q) * sin, k * cos + rot(k) * sin)
        B, S, D = x.shape
        h = _rms(x, ln_w)
        q = (h @ wq).reshape(B, S, NHEADS, HEAD_DIM)
        k = (h @ wk).reshape(B, S, KVHEADS, HEAD_DIM)
        v = (h @ wv).reshape(B, S, KVHEADS, HEAD_DIM)
        q, k = _rope(q, k)
        g = NHEADS // KVHEADS
        k = jnp.repeat(k, g, axis=2)
        v = jnp.repeat(v, g, axis=2)
        scores = jnp.einsum('bqhd,bkhd->bhqk', q, k) / np.float32(np.sqrt(HEAD_DIM))
        causal = jnp.tril(jnp.ones((S, S), bool))
        scores = jnp.where(causal[None, None], scores, jnp.float32(-1e+30))
        attn = jax.nn.softmax(scores, -1)
        o = jnp.einsum('bhqk,bkhd->bqhd', attn, v).reshape(B, S, NHEADS * HEAD_DIM)
        x = x + o @ wo
        h = _rms(x, ff_ln_w)
        logits = h @ wg
        topv, topi = jax.lax.top_k(logits, TOP_K)
        gate = jax.nn.softmax(topv, -1)
        bidx = jnp.arange(B)[:, None, None]
        sidx = jnp.arange(S)[None, :, None]
        weights = jnp.zeros_like(logits).at[bidx, sidx, topi].set(gate)
        a = jax.nn.silu(jnp.einsum('bsd,edh->bseh', h, w1)) * jnp.einsum('bsd,edh->bseh', h, w3)
        y = jnp.einsum('bseh,ehd->bsed', a, w2)
        moe = jnp.einsum('bsed,bse->bsd', y, weights)
        return x + moe
    x = x + _L0_ffn_ref(_L0_cond_ref(x, L0_cond_Wg, L0_cond_Wu, L0_cond_Wd, L0_cond_Ag, L0_cond_Bg, L0_cond_Au, L0_cond_Bu, L0_cond_Ad, L0_cond_Bd, itok_B_0_7), L0_ffn_ln_w, L0_ffn_ff_ln_w, L0_ffn_wq, L0_ffn_wk, L0_ffn_wv, L0_ffn_wo, L0_ffn_wg, L0_ffn_w1, L0_ffn_w3, L0_ffn_w2)
    return x

_drawn_inputs = setup_inputs


def setup_inputs(seed=0):
    import zlib

    import numpy as np

    out = dict(_drawn_inputs(seed))
    spreads = {'L0_cond_Bg': (0.009999999776482582, 0.6),
     'L0_cond_Bu': (0.009999999776482582, 0.6),
     'L0_cond_Bd': (0.009999999776482582, 0.6),
     'L0_ffn_ln_w': (1.0, 0.6),
     'L0_ffn_ff_ln_w': (1.0, 0.6)}
    factors = {'L0_cond_Ag': 2.683,
     'L0_ffn_wq': 7.652,
     'L0_ffn_wk': 7.694,
     'L0_ffn_wg': 8.0,
     'L0_ffn_w1': 7.472,
     'L0_ffn_w3': 7.397,
     'L0_ffn_w2': 7.399}
    for name, (base, spread) in spreads.items():
        noise = np.random.default_rng([zlib.crc32(name.encode()), seed]).standard_normal(out[name].shape)
        drawn = base * np.exp(spread * noise) if base else spread * noise
        out[name] = jnp.asarray(drawn.astype(out[name].dtype))
    for name, factor in factors.items():
        out[name] = (out[name] * factor).astype(out[name].dtype)
    return out
```

```python
from contextlib import ExitStack

import numpy as np

import concourse.bass as bass
from concourse import mybir

ALU = mybir.AluOpType
ACT = mybir.ActivationFunctionType
F32 = mybir.dt.float32
F32R = mybir.dt.float32r
I32 = mybir.dt.int32
U32 = mybir.dt.uint32
AX = mybir.AxisListType

P = 128
SEQ = 32
D = 256
KD = D // P
T = 1024
NT = T // P
SPT = P // SEQ
GROUP = 512
NG = T // GROUP
TPG = GROUP // P
HID = 1024
MH = HID // P
NAD = 8
RANK = 16
HEADS, KVH, HD = 32, 8, 64
QPK = HEADS // KVH
KVP = KVH // 2
QKC = (HEADS + KVH) * HD // GROUP
NE, TOPK = 16, 4
EPS = 1e-5
SCALE = 1.0 / 8.0
WG, WU, BG, BU, WD, AD, MCOLS = 0, 256, 512, 640, 768, 1024, 1152
AG, AU, BD, HCOLS = 0, 256, 512, 768
QCHUNKS = (HEADS + 2 * KVH) * HD // GROUP
OCHUNKS = 4
ECOLS = 3 * KD * D
C_COS, C_SIN, C_MASK, C_LN, C_FF, C_EXP, C_EPS, CCOLS = 0, 64, 128, 160, 162, 164, 165, 166


def build(nc, x, seq_adapter, cond_head, cond_w, qkv_w, wo_w, gate_w, expert_w, norms, consts, out):
    with ExitStack() as ctx:
        cursor = [nc.sbuf_base + 31 & ~31]

        def sb(name, shape, dt=F32):
            size = 4 * int(np.prod(shape[1:]))
            t = nc.alloc_sbuf_tensor_at(name, shape, dt, offset=cursor[0])
            cursor[0] += size + 31 & ~31
            assert cursor[0] <= nc.sbuf_usable_end, (name, cursor[0], nc.sbuf_usable_end)
            return t

        def pair(name, shape):
            return sb(name + "_hi", shape, F32R), sb(name + "_lo", shape, F32R)

        def sem(name):
            return ctx.enter_context(nc.semaphore(name))

        def ps(name, shape):
            return ctx.enter_context(nc.psum_tensor(name, shape, F32))

        x_rows = sb("x_rows", [P, TPG, D])
        resid = sb("resid", [P, NT, D])
        ident = sb("ident", [P, P])
        cst = sb("cst", [P, CCOLS])
        staging = sb("staging", [P, 2, ECOLS])
        seq_ids = sb("seq_ids", [P, NT * SPT], I32)
        part_id = sb("part_id", [P, 1], I32)
        part_f = sb("part_f", [P, 1])
        row_off = sb("row_off", [P, NT * SPT])
        below = sb("below", [P, NT * SPT])
        amask = sb("amask", [P, NT * SPT])
        meansq1 = sb("meansq1", [P, NT])
        shifted1 = sb("shifted1", [P, NT])
        rstd1 = sb("rstd1", [P, NT])
        meansq2 = sb("meansq2", [P, 1])
        shifted2 = sb("shifted2", [P, 1])
        rstd2 = sb("rstd2", [P, 1])
        sq_junk = sb("sq_junk", [P, D])
        wg_hi, wg_lo = pair("wgate", [P, KD, NE])
        qkv_at = cursor[0]
        qkvw_hi, qkvw_lo = pair("qkvw", [P, QCHUNKS, KD, GROUP])
        overlay = cursor[0]
        head_hi, head_lo = pair("head", [P, HCOLS])
        cw_hi, cw_lo = pair("cw", [P, MH, MCOLS])
        xT_hi, xT_lo = pair("xT", [P, KD, GROUP])
        tm = sb("tm", [P, 2, GROUP])
        tm_hi, tm_lo = pair("tmp", [P, 2, GROUP])
        silu_g = sb("silu_g", [P, 2, GROUP])
        act = sb("act", [P, 2, GROUP])
        act_hi, act_lo = pair("actp", [P, 2, GROUP])
        cursor[0] = overlay
        wo_hi, wo_lo = pair("wo", [P, KVP * QPK, D])
        hrow = sb("hrow", [P, 2, D])
        hT_hi, hT_lo = pair("hT", [P, KD, P])
        h2T_hi, h2T_lo = pair("h2T", [P, KD, T])
        qc = sb("qc", [P, 2, GROUP])
        qs = sb("qs", [P, 2, GROUP])
        qr = sb("qr", [P, QKC, GROUP])
        v_hi, v_lo = pair("v", [P, GROUP])
        shared = cursor[0]
        kT_hi, kT_lo = pair("kT", [P, KVP, P])
        cursor[0] = shared
        pT_hi, pT_lo = pair("pT", [P, 2, KVP, P])
        shared = cursor[0]
        qT_hi, qT_lo = pair("qT", [P, KVP, SPT, P])
        after = cursor[0]
        cursor[0] = shared
        o_rows = sb("o_rows", [P, SPT, KVP, P])
        cursor[0] = after
        z = sb("z", [P, 2, KVP * SPT, SEQ])
        prob = sb("prob", [P, 2, KVP * SPT, SEQ])
        zmax = sb("zmax", [P, 2 * KVP * SPT])
        zsum = sb("zsum", [P, 2 * KVP * SPT])
        zinv = sb("zinv", [P, 2, KVP, SPT])
        oT_hi, oT_lo = pair("oT", [P, KVP * QPK, P])
        end_of_attention = cursor[0]
        cursor[0] = qkv_at
        ew_hi, ew_lo = pair("ew", [P, 2, ECOLS])
        wbc = sb("wbc", [P, 2, T])
        wtok = sb("wtok", [P, NT, NE])
        wT = sb("wT", [P, P])
        logit = sb("logit", [P, NT, NE])
        top8 = sb("top8", [P, NT, 8])
        topi = sb("topi", [P, NT, 8], U32)
        topi_f = sb("topi_f", [P, NT, TOPK])
        tope = sb("tope", [P, NT, TOPK])
        gsum = sb("gsum", [P, NT])
        ginv = sb("ginv", [P, NT])
        gate = sb("gate", [P, NT, TOPK])
        eidx = sb("eidx", [P, NE], I32)
        eidx_f = sb("eidx_f", [P, NE])
        hit = sb("hit", [P, NT, TOPK, NE])
        assert cursor[0] <= overlay, (cursor[0], overlay)
        cursor[0] = shared
        x_fin = sb("x_fin", [P, NT, D])
        msilu = sb("msilu", [P, 2, GROUP])
        mgated = sb("mgated", [P, 2, GROUP])
        mact = sb("mact", [P, 2, GROUP])
        mact_hi, mact_lo = pair("mactp", [P, 2, GROUP])
        assert cursor[0] <= end_of_attention

        w_dram = nc.dram_tensor("moe_weights", (NE, NT, P), F32, kind="Internal").ap()

        ringA = ps("ringA", [P, 2, GROUP])
        ringT = ps("ringT", [P, 2, GROUP])
        wide = ps("wide", [P, 4, GROUP])
        gu = [(ringA[:, 0, :], ringA[:, 1, :]), (ringT[:, 0, :], ringT[:, 1, :])]

        x_in = sem("x_in")
        cst_in = sem("cst_in")
        ids_in = sem("ids_in")
        ident_zero, ident_done = sem("ident_zero"), sem("ident_done")
        powers_set = sem("powers_set")
        mask_step, mask_done = sem("mask_step"), sem("mask_done")
        raw_in = [sem(f"raw_in{i}") for i in range(2)]
        NCH = 1 + MH + QCHUNKS + OCHUNKS + 1
        hi_in = [sem(f"hi_in{i}") for i in range(NCH)]
        lo_done = sem("lo_done")
        pair_full = sem("pair_full")
        xT_hi_done, xT_lo_done = sem("xT_hi_done"), sem("xT_lo_done")
        tm_masked = sem("tm_masked")
        tm_hi_done = sem("tm_hi_done")
        tm_lo_done = sem("tm_lo_done")
        silu_done = sem("silu_done")
        act_done = sem("act_done")
        act_hi_done = sem("act_hi_done")
        act_lo_done = sem("act_lo_done")
        act_used = sem("act_used")
        down_a_full = sem("down_a_full")
        c_full = sem("c_full")
        c_copied = sem("c_copied")
        meansq1_done, shifted1_done, rstd1_done = sem("meansq1_done"), sem("shifted1_done"), sem("rstd1_done")

        h_ready = sem("h_ready")
        h2_ready = sem("h2_ready")
        kl_full = sem("kl_full")
        hT_hi_done, hT_lo_done = sem("hT_hi_done"), sem("hT_lo_done")
        h2T_hi_done, h2T_lo_done = sem("h2T_hi_done"), sem("h2T_lo_done")
        qk_full, qk_read, qk_roped = sem("qk_full"), sem("qk_read"), sem("qk_roped")
        v_full, v_hi_done, v_lo_done = sem("v_full"), sem("v_hi_done"), sem("v_lo_done")
        qkT_full, qkT_hi_done, qkT_lo_done = sem("qkT_full"), sem("qkT_hi_done"), sem("qkT_lo_done")
        s_full, z_masked, zmax_done, z_shifted = sem("s_full"), sem("z_masked"), sem("zmax_done"), sem("z_shifted")
        prob_done, zsum_done, zinv_done = sem("prob_done"), sem("zsum_done"), sem("zinv_done")
        pT_full, pT_hi_done, pT_lo_done = sem("pT_full"), sem("pT_hi_done"), sem("pT_lo_done")
        o_full, o_normed = sem("o_full"), sem("o_normed")
        oT_full, oT_hi_done, oT_lo_done = sem("oT_full"), sem("oT_hi_done"), sem("oT_lo_done")
        y_full, x1_done = sem("y_full"), sem("x1_done")
        meansq2_done, shifted2_done, rstd2_done = sem("meansq2_done"), sem("shifted2_done"), sem("rstd2_done")

        logit_full, logit_done = sem("logit_full"), sem("logit_done")
        route_step, top_exp = sem("route_step"), sem("top_exp")
        eidx_done = sem("eidx_done")
        wT_full, wT_done, w_out = sem("wT_full"), sem("wT_done"), sem("w_out")
        seed_done = sem("seed_done")
        ew_hi_in = [sem(f"ew_hi_in{i}") for i in range(2)]
        wbc_in = [sem(f"wbc_in{i}") for i in range(2)]
        x_again = sem("x_again")
        m_full, m_silu, m_gated, m_act = sem("m_full"), sem("m_silu"), sem("m_gated"), sem("m_act")
        m_hi, m_lo, m_used = sem("m_hi"), sem("m_lo"), sem("m_used")
        acc_full = sem("acc_full")
        out_rows, out_done = sem("out_rows"), sem("out_done")

        x_dram = x.rearrange("b s d -> (b s) d").rearrange("(t p) d -> p t d", p=P)
        out_dram = out.rearrange("b s d -> (b s) d").rearrange("(t p) d -> p t d", p=P)

        chunks = [(cond_head, head_hi[:, :], head_lo[:, :])]
        chunks += [(cond_w[:, m, :], cw_hi[:, m, :], cw_lo[:, m, :]) for m in range(MH)]
        FIRST_QKV = len(chunks)
        chunks += [(qkv_w[:, c, :], qkvw_hi[:, c, :, :].rearrange("p k n -> p (k n)"),
                    qkvw_lo[:, c, :, :].rearrange("p k n -> p (k n)")) for c in range(QCHUNKS)]
        FIRST_WO = len(chunks)
        per = KVP * QPK // OCHUNKS
        chunks += [(wo_w[:, c * per:(c + 1) * per, :].rearrange("p k n -> p (k n)"),
                    wo_hi[:, c * per:(c + 1) * per, :].rearrange("p k n -> p (k n)"),
                    wo_lo[:, c * per:(c + 1) * per, :].rearrange("p k n -> p (k n)"))
                   for c in range(OCHUNKS)]
        chunks += [(gate_w, wg_hi[:, :, :].rearrange("p k n -> p (k n)"),
                    wg_lo[:, :, :].rearrange("p k n -> p (k n)"))]
        assert len(chunks) == NCH

        def wait(eng, semaphore, value):
            if isinstance(value, int) and value <= 0:
                return
            eng.wait_ge(semaphore, value)

        def kl_bank(moe):
            return ringT[:, 0, :] if isinstance(moe, int) and moe == NT - 1 else ringT[:, 1, :]

        def turned(c, kT, qT):
            if c == 0:
                return kT[:, :, :].rearrange("p a n -> p (a n)"), ringT[:, 0, :]
            return (qT[:, c - 1, :, :].rearrange("p s (g q) -> p g s q", g=QPK),
                    ringT[:, c % 2, :].rearrange("p (g s q) -> p g s q", g=QPK, s=SPT))

        def lo_part(lo, full, hi):
            return dict(out=lo, in0=full, in1=hi.bitcast(F32), op=ALU.subtract)

        block = ctx.enter_context(nc.Block())

        @block.sync
        def _(sp):
            def raw(n, src, cols):
                wait(sp, lo_done, n - 1)
                sp.dma_start(staging[:, n % 2, 0:cols], src).then_inc(raw_in[n % 2], 16)

            sp.dma_start(x_rows[:, :, :], x_dram[:, 0:TPG, :]).then_inc(x_in, 16)
            raw(0, chunks[0][0], chunks[0][1].shape[-1])
            raw(1, chunks[1][0], chunks[1][1].shape[-1])
            sp.dma_start(seq_ids[:, :], seq_adapter.partition_broadcast(P)).then_inc(ids_in, 16)
            sp.dma_start(cst[:, 0:C_LN], consts).then_inc(cst_in, 16)
            sp.dma_start(cst[:, C_LN:C_EXP], norms).then_inc(cst_in, 16)
            for n in range(2, NCH):
                raw(n, chunks[n][0], chunks[n][1].shape[-1])
                if n == 6:
                    sp.wait_ge(pair_full, 1)
                    sp.dma_start(x_rows[:, :, :], x_dram[:, TPG:NT, :]).then_inc(x_in, 16)

            def expert_loads(e, b, wbc_free):
                wait(sp, lo_done, NCH + e - 1)
                sp.dma_start(staging[:, b, :], expert_w[bass.ds(e, 1), :, :].rearrange("o p n -> (o p) n")
                             ).then_inc(raw_in[b], 16)
                if wbc_free:
                    sp.wait_ge(m_gated, 4 * (e - 1))
                sp.dma_start(wbc[:, b, :], w_dram[bass.ds(e, 1), :, :].rearrange("o t p -> (o t p)").partition_broadcast(P)
                             ).then_inc(wbc_in[b], 16)

            for b in range(2):
                sp.wait_ge(lo_done, NCH + b - 1)
                sp.dma_start(staging[:, b, :], expert_w[b, :, :]).then_inc(raw_in[b], 16)
            sp.wait_ge(wT_done, 1)
            sp.dma_start(w_dram.rearrange("e t p -> t e p"), wT[:, :]).then_inc(w_out, 16)
            sp.wait_ge(w_out, 16)
            for b in range(2):
                sp.dma_start(wbc[:, b, :], w_dram[b, :, :].rearrange("t p -> (t p)").partition_broadcast(P)
                             ).then_inc(wbc_in[b], 16)
            sp.dma_start(x_fin[:, :, :], x_dram).then_inc(x_again, 16)
            with sp.Fori(1, NE // 2) as i:
                for b in range(2):
                    expert_loads(i * 2 + b, b, True)
            for h in range(4):
                sp.wait_ge(out_rows, h + 1)
                sp.dma_start(out_dram[:, 2 * h:2 * h + 2, :], resid[:, 2 * h:2 * h + 2, :]).then_inc(out_done, 16)
            sp.wait_ge(out_done, 16 * 4)

        @block.gpsimd
        def _(pool):
            for n in range(FIRST_WO):
                pool.dma_start(chunks[n][1], chunks[n][0]).then_inc(hi_in[n], 16)
                if n == 0:
                    pool.memset(ident[:, :], 0.0).then_inc(ident_zero, 1)
                    pool.iota(part_id[:, :], pattern=[[0, 1]], base=0, channel_multiplier=1).then_inc(mask_step, 1)
                    pool.memset(cst[:, C_EXP:C_EXP + 1], -0.5).then_inc(powers_set, 1)
                    pool.memset(cst[:, C_EPS:C_EPS + 1], EPS).then_inc(powers_set, 1)
                    pool.wait_ge(ident_zero, 1)
                    pool.affine_select(out=ident[:, :], in_=ident[:, :], compare_op=ALU.not_equal, fill=1.0,
                                       base=0, pattern=[[-1, P]], channel_multiplier=1).then_inc(ident_done, 1)
            pool.dma_start(chunks[NCH - 1][1], chunks[NCH - 1][0]).then_inc(hi_in[NCH - 1], 16)

            def split(n):
                _src, hi, lo = chunks[n]
                pool.wait_ge(raw_in[n % 2], 16 * (n // 2 + 1))
                pool.wait_ge(hi_in[n], 16)
                pool.wait_ge(lo_done, n)
                pool.tensor_tensor(**lo_part(lo, staging[:, n % 2, 0:hi.shape[-1]], hi)).then_inc(lo_done, 1)

            for n in range(2, FIRST_WO):
                split(n)
            pool.wait_ge(powers_set, 2)
            for g in range(NG):
                cols = slice(g * TPG, (g + 1) * TPG)
                pool.wait_ge(meansq1_done, TPG * (g + 1))
                pool.tensor_scalar(shifted1[:, cols], meansq1[:, cols], EPS, None, ALU.add).then_inc(shifted1_done, 1)
                pool.wait_ge(shifted1_done, g + 1)
                pool.tensor_tensor(rstd1[:, cols], shifted1[:, cols],
                                   cst[:, C_EXP:C_EXP + 1].broadcast_to([P, TPG]), ALU.pow).then_inc(rstd1_done, 1)
            pool.wait_ge(rstd1_done, NG)
            pool.wait_ge(c_full, NG)

            def attention_rows(t):
                wait(pool, kl_full, t)
                pool.tensor_tensor(hrow[:, 1, :], resid[:, t, :], rstd1[:, bass.ds(t, 1)].broadcast_to([P, D]),
                                   ALU.mult).then_inc(h_ready, 1)

            def rope_add(t, c):
                pool.wait_ge(qk_read, QKC * t + c + 1)
                wait(pool, qkT_full, QKC * t)
                cos = qc[:, c % 2, :].rearrange("p (h f d) -> p h f d", f=2, d=HD // 2)
                sin = qs[:, c % 2, :].rearrange("p (h f d) -> p h f d", f=2, d=HD // 2)
                rot = qr[:, c, :].rearrange("p (h f d) -> p h f d", f=2, d=HD // 2)
                for f in range(2):
                    last = pool.tensor_tensor(rot[:, :, f, :], cos[:, :, f, :], sin[:, :, 1 - f, :], ALU.add)
                last.then_inc(qk_roped, 1)

            def shift(t):
                pool.wait_ge(zmax_done, t + 1)
                zv = z[:, :, :, :].rearrange("p j n k -> p (j n) k")
                pool.tensor_tensor(zv, zv, zmax[:, :].unsqueeze(2).broadcast_to([P, 2 * KVP * SPT, SEQ]),
                                   ALU.subtract).then_inc(z_shifted, 1)

            def moe_rows(t):
                pool.wait_ge(meansq2_done, t + 1)
                pool.tensor_tensor(shifted2[:, :], meansq2[:, :], cst[:, C_EPS:C_EPS + 1], ALU.add).then_inc(shifted2_done, 1)
                pool.wait_ge(shifted2_done, t + 1)
                pool.tensor_tensor(rstd2[:, :], shifted2[:, :], cst[:, C_EXP:C_EXP + 1], ALU.pow).then_inc(rstd2_done, 1)
                pool.wait_ge(rstd2_done, t + 1)
                if not (isinstance(t, int) and t == 0):
                    pool.wait_ge(kl_full, t + 3)
                pool.tensor_tensor(hrow[:, 0, :], resid[:, t, :], rstd2[:, 0:1].broadcast_to([P, D]),
                                   ALU.mult).then_inc(h2_ready, 1)

            attention_rows(0)
            for n in range(FIRST_WO, FIRST_WO + OCHUNKS):
                pool.dma_start(chunks[n][1], chunks[n][0]).then_inc(hi_in[n], 16)
            for c in range(QKC):
                rope_add(0, c)
            attention_rows(1)
            for n in range(FIRST_WO, NCH):
                split(n)

            def attend(t, first=False, last=False, rows_left=True):
                shift(t)
                if not last:
                    for c in range(QKC):
                        rope_add(t + 1, c)
                if not first:
                    moe_rows(t - 1)
                if rows_left:
                    attention_rows(t + 2)

            attend(0, first=True)
            attend(1)
            with pool.Fori(2, NT - 2) as t:
                attend(t)
            attend(NT - 2, rows_left=False)
            attend(NT - 1, last=True, rows_left=False)
            moe_rows(NT - 1)

            def expert_split(e, b, first=False):
                if not first:
                    pool.wait_ge(m_used, 4 * (e - 1))
                pool.dma_start(ew_hi[:, b, :], expert_w[bass.ds(e, 1), :, :].rearrange("o p n -> (o p) n")
                               ).then_inc(ew_hi_in[b], 16)

            def expert_lo(e, b, i):
                pool.wait_ge(ew_hi_in[b], 16 * (i + 1))
                pool.wait_ge(raw_in[b], 16 * (NCH // 2 + i + 1))
                pool.wait_ge(lo_done, NCH + e)
                pool.tensor_tensor(**lo_part(ew_lo[:, b, :], staging[:, b, :], ew_hi[:, b, :])).then_inc(lo_done, 1)

            def gated(e, b, i, n, j):
                step = 4 * e + 2 * n + j
                pool.wait_ge(m_silu, step + 1)
                if n == 0 and j == 0:
                    pool.wait_ge(wbc_in[b], 16 * (i + 1))
                wait(pool, m_act, step - 1)
                pool.tensor_tensor(mgated[:, j, :], msilu[:, j, :], wbc[:, b, n * GROUP:(n + 1) * GROUP],
                                   ALU.mult).then_inc(m_gated, 1)

            def experts(i, first=False, last=False):
                for b in range(2):
                    e = 2 * i + b if isinstance(i, int) else i * 2 + b
                    more = not (last and b == 1)
                    if more:
                        expert_split(e + 1, 1 - b, first and b == 0)
                    gated(e, b, i, 0, 0)
                    if more:
                        expert_lo(e + 1, 1 - b, i + b)
                    gated(e, b, i, 0, 1)
                    gated(e, b, i, 1, 0)
                    gated(e, b, i, 1, 1)

            pool.wait_ge(v_full, NT)
            pool.iota(eidx[:, :], pattern=[[1, NE]], base=0, channel_multiplier=0).then_inc(eidx_done, 1)
            expert_split(0, 0, True)
            expert_lo(0, 0, 0)
            experts(0, first=True)
            with pool.Fori(1, NE // 2 - 1) as i:
                experts(i)
            experts(NE // 2 - 1, last=True)

        @block.scalar
        def _(act_e):
            def copy(out, in_, scale=None):
                if scale is None:
                    return act_e.activation(out, in_, ACT.Copy)
                return act_e.activation(out, in_, ACT.Copy, scale=scale)

            for g in range(NG):
                act_e.wait_ge(pair_full, (MH + 2) * g + 1)
                for k in range(KD):
                    copy(xT_hi[:, k, :], gu[0][k]).then_inc(xT_hi_done, 1)
                for i in range(2):
                    act_e.wait_ge(tm_masked, 3 * g + i + 1)
                    copy(tm_hi[:, i, :], tm[:, i, :]).then_inc(tm_hi_done, 1)
                for m in range(MH):
                    act_e.wait_ge(pair_full, (MH + 2) * g + 3 + m)
                    wait(act_e, act_done, MH * g + m - 1)
                    act_e.activation(silu_g[:, m % 2, :], gu[m % 2][0], ACT.Silu).then_inc(silu_done, 1)
                    act_e.wait_ge(act_done, MH * g + m + 1)
                    wait(act_e, act_used, MH * g + m - 1)
                    copy(act_hi[:, m % 2, :], act[:, m % 2, :]).then_inc(act_hi_done, 1)
                act_e.wait_ge(tm_masked, 3 * g + 3)
                copy(tm_hi[:, 0, :], tm[:, 0, :]).then_inc(tm_hi_done, 1)
                act_e.wait_ge(c_full, g + 1)
                for i in range(TPG):
                    rows = wide[:, i // 2, (i % 2) * D:(i % 2 + 1) * D]
                    copy(resid[:, g * TPG + i, :], rows)
                    wait(act_e, meansq1_done, g * TPG + i)
                    act_e.activation(sq_junk[:, :], rows, ACT.Square, scale=D ** -0.5,
                                     accum_out=meansq1[:, g * TPG + i:g * TPG + i + 1]).then_inc(meansq1_done, 1)

            def kl_hi(moe, attn):
                if moe is not None:
                    for k in range(KD):
                        last = copy(h2T_hi[:, k, bass.ds(moe * P, P)], kl_bank(moe)[:, k * P:(k + 1) * P],
                                    cst[:, C_FF + k:C_FF + k + 1])
                    last.then_inc(h2T_hi_done, 1)
                if attn is not None:
                    for k in range(KD):
                        last = copy(hT_hi[:, k, :], ringT[:, 1, (KD + k) * P:(KD + k + 1) * P],
                                    cst[:, C_LN + k:C_LN + k + 1])
                    last.then_inc(hT_hi_done, 1)

            def v_part(t):
                act_e.wait_ge(v_full, t + 1)
                wait(act_e, o_full, t)
                copy(v_hi[:, :], ringA[:, 1, :]).then_inc(v_hi_done, 1)

            def residual_square(t):
                act_e.wait_ge(x1_done, t + 1)
                wait(act_e, shifted2_done, t)
                act_e.wait_ge(meansq1_done, NT) if isinstance(t, int) and t == 0 else wait(act_e, meansq2_done, t)
                act_e.activation(sq_junk[:, :], resid[:, t, :], ACT.Square, scale=D ** -0.5,
                                 accum_out=meansq2[:, :]).then_inc(meansq2_done, 1)

            act_e.wait_ge(cst_in, 32)
            act_e.wait_ge(kl_full, 1)
            kl_hi(None, 0)
            v_part(0)

            def attend(t, moe=True, attn=True, square=True):
                for c in range(QKC):
                    act_e.wait_ge(qkT_full, QKC * t + c + 1)
                    dst, src = turned(c, kT_hi, qT_hi)
                    copy(dst, src).then_inc(qkT_hi_done, 1)
                if moe or attn:
                    act_e.wait_ge(kl_full, t + 2)
                    kl_hi(t - 2 if moe else None, t + 1 if attn else None)
                act_e.wait_ge(z_shifted, t + 1)
                wait(act_e, pT_full, 2 * t)
                act_e.activation(prob[:, :, :, :].rearrange("p j n k -> p (j n k)"),
                                 z[:, :, :, :].rearrange("p j n k -> p (j n k)"), ACT.Exp).then_inc(prob_done, 1)
                for j in range(2):
                    act_e.wait_ge(pT_full, 2 * t + j + 1)
                    copy(pT_hi[:, j, :, :].rearrange("p a n -> p (a n)"), ringT[:, j, :]).then_inc(pT_hi_done, 1)
                if attn:
                    v_part(t + 1)
                if square:
                    residual_square(t - 1)
                for s in range(SPT):
                    act_e.wait_ge(oT_full, SPT * t + s + 1)
                    copy(oT_hi[:, :, s * SEQ:(s + 1) * SEQ], ringT[:, s % 2, :].rearrange("p (n q) -> p n q", q=SEQ)
                         ).then_inc(oT_hi_done, 1)

            attend(0, moe=False, square=False)
            attend(1, moe=False)
            with act_e.Fori(2, NT - 1) as t:
                attend(t)
            attend(NT - 1, attn=False)
            act_e.wait_ge(kl_full, NT + 2)
            kl_hi(NT - 2, None)
            residual_square(NT - 1)
            act_e.wait_ge(kl_full, NT + 3)
            kl_hi(NT - 1, None)

            act_e.wait_ge(route_step, 3)
            act_e.activation(tope[:, :, :].rearrange("p t k -> p (t k)"), gate[:, :, :].rearrange("p t k -> p (t k)"),
                             ACT.Exp).then_inc(top_exp, 1)
            act_e.wait_ge(wT_full, 1)
            copy(wT[:, :], wide[:, 3, 0:P]).then_inc(wT_done, 1)

            def experts(i):
                for b in range(2):
                    for s in range(4):
                        step = i * 8 + (4 * b + s)
                        act_e.wait_ge(m_full, step + 1)
                        wait(act_e, m_gated, step - 1)
                        act_e.activation(msilu[:, s % 2, :], gu[1 - s % 2][0], ACT.Silu).then_inc(m_silu, 1)
                        act_e.wait_ge(m_act, step + 1)
                        wait(act_e, m_used, step - 1)
                        copy(mact_hi[:, s % 2, :], mact[:, s % 2, :]).then_inc(m_hi, 1)

            experts(0)
            with act_e.Fori(1, NE // 2) as i:
                experts(i)

        @block.vector
        def _(dve):
            for n in range(2):
                _src, hi, lo = chunks[n]
                dve.wait_ge(raw_in[n], 16)
                dve.wait_ge(hi_in[n], 16)
                dve.tensor_tensor(**lo_part(lo, staging[:, n, 0:hi.shape[-1]], hi)).then_inc(lo_done, 1)
            dve.wait_ge(ids_in, 16)
            dve.wait_ge(mask_step, 1)
            dve.tensor_copy(part_f[:, :], part_id[:, :]).then_inc(mask_done, 1)
            dve.wait_ge(mask_done, 1)
            dve.tensor_scalar(row_off[:, :], seq_ids[:, :], -float(RANK), part_f[:, 0:1], ALU.mult, ALU.add).then_inc(mask_done, 1)
            dve.wait_ge(mask_done, 2)
            dve.tensor_scalar(below[:, :], row_off[:, :], RANK - 0.5, None, ALU.is_le).then_inc(mask_done, 1)
            dve.wait_ge(mask_done, 3)
            dve.scalar_tensor_tensor(out=amask[:, :], in0=row_off[:, :], scalar=0.0, in1=below[:, :],
                                     op0=ALU.is_ge, op1=ALU.mult).then_inc(mask_done, 1)
            dve.wait_ge(mask_done, 4)

            def masked(g, i, src):
                picked = amask[:, g * TPG * SPT:(g + 1) * TPG * SPT].unsqueeze(2).broadcast_to([P, TPG * SPT, SEQ])
                dve.tensor_tensor(tm[:, i, :].rearrange("p (s n) -> p s n", n=SEQ), src.rearrange("p (s n) -> p s n", n=SEQ),
                                  picked, ALU.mult).then_inc(tm_masked, 1)

            def tm_low(g, i, count):
                dve.wait_ge(tm_hi_done, 3 * g + count)
                dve.tensor_tensor(**lo_part(tm_lo[:, i, :], tm[:, i, :], tm_hi[:, i, :])).then_inc(tm_lo_done, 1)

            for g in range(NG):
                for k in range(KD):
                    dve.wait_ge(xT_hi_done, KD * g + k + 1)
                    dve.tensor_tensor(**lo_part(xT_lo[:, k, :], gu[0][k], xT_hi[:, k, :])).then_inc(xT_lo_done, 1)
                dve.wait_ge(pair_full, (MH + 2) * g + 2)
                for i in range(2):
                    masked(g, i, gu[1][i])
                for i in range(2):
                    tm_low(g, i, i + 1)
                for m in range(MH):
                    dve.wait_ge(silu_done, MH * g + m + 1)
                    dve.tensor_tensor(act[:, m % 2, :], silu_g[:, m % 2, :], gu[m % 2][1], ALU.mult).then_inc(act_done, 1)
                    dve.wait_ge(act_hi_done, MH * g + m + 1)
                    dve.tensor_tensor(**lo_part(act_lo[:, m % 2, :], act[:, m % 2, :], act_hi[:, m % 2, :])).then_inc(act_lo_done, 1)
                dve.wait_ge(down_a_full, g + 1)
                masked(g, 0, wide[:, 2, :])
                tm_low(g, 0, 3)

            dve.wait_ge(cst_in, 32)
            dve.wait_ge(meansq1_done, NT)

            def kl_lo(moe, attn):
                if moe is not None:
                    for k in range(KD):
                        last = dve.scalar_tensor_tensor(
                            out=h2T_lo[:, k, bass.ds(moe * P, P)], in0=kl_bank(moe)[:, k * P:(k + 1) * P],
                            scalar=cst[:, C_FF + k:C_FF + k + 1], in1=h2T_hi[:, k, bass.ds(moe * P, P)].bitcast(F32),
                            op0=ALU.mult, op1=ALU.subtract)
                    last.then_inc(h2T_lo_done, 1)
                if attn is not None:
                    for k in range(KD):
                        last = dve.scalar_tensor_tensor(
                            out=hT_lo[:, k, :], in0=ringT[:, 1, (KD + k) * P:(KD + k + 1) * P],
                            scalar=cst[:, C_LN + k:C_LN + k + 1], in1=hT_hi[:, k, :].bitcast(F32),
                            op0=ALU.mult, op1=ALU.subtract)
                    last.then_inc(hT_lo_done, 1)

            def rope_products(t, c):
                dve.wait_ge(qk_full, QKC * t + c + 1)
                wait(dve, qk_roped, QKC * t + c - 1)
                heads = GROUP // HD
                src = ringA[:, c % 2, :].rearrange("p (h d) -> p h d", d=HD)
                for dst, col in ((qc, C_COS), (qs, C_SIN)):
                    table = cst[:, col:col + HD].unsqueeze(1).broadcast_to([P, heads, HD])
                    last = dve.tensor_tensor(dst[:, c % 2, :].rearrange("p (h d) -> p h d", d=HD), src, table, ALU.mult)
                last.then_inc(qk_read, 1)

            def v_low(t):
                dve.wait_ge(v_hi_done, t + 1)
                dve.tensor_tensor(**lo_part(v_lo[:, :], ringA[:, 1, :], v_hi[:, :])).then_inc(v_lo_done, 1)

            def residual(t):
                dve.wait_ge(y_full, t + 1)
                dve.tensor_tensor(resid[:, t, :], ringA[:, 0, 0:D], resid[:, t, :], ALU.add).then_inc(x1_done, 1)

            dve.wait_ge(hT_hi_done, 1)
            kl_lo(None, 0)
            for c in range(QKC):
                rope_products(0, c)
            v_low(0)

            def attend(t, moe=True, attn=True, res=True):
                for c in range(QKC):
                    dve.wait_ge(qkT_hi_done, QKC * t + c + 1)
                    hi, src = turned(c, kT_hi, qT_hi)
                    dve.tensor_tensor(**lo_part(turned(c, kT_lo, qT_lo)[0], src, hi)).then_inc(qkT_lo_done, 1)
                if moe:
                    dve.wait_ge(h2T_hi_done, t - 1)
                if attn:
                    dve.wait_ge(hT_hi_done, t + 2)
                kl_lo(t - 2 if moe else None, t + 1 if attn else None)
                dve.wait_ge(s_full, t + 1)
                wait(dve, prob_done, t)
                for j in range(2):
                    mask = cst[:, C_MASK:C_MASK + SEQ].unsqueeze(1).broadcast_to([P, KVP * SPT, SEQ])
                    dve.scalar_tensor_tensor(out=z[:, j, :, :], in0=wide[:, j, :].rearrange("p (n k) -> p n k", k=SEQ),
                                             scalar=SCALE, in1=mask, op0=ALU.mult, op1=ALU.add).then_inc(z_masked, 1)
                dve.wait_ge(z_masked, 2 * t + 2)
                dve.tensor_reduce(zmax[:, :], z[:, :, :, :].rearrange("p j n k -> p (j n) k"), AX.X, ALU.max).then_inc(zmax_done, 1)
                if attn:
                    rope_products(t + 1, 0)
                    rope_products(t + 1, 1)
                dve.wait_ge(prob_done, t + 1)
                dve.tensor_reduce(zsum[:, :], prob[:, :, :, :].rearrange("p j n k -> p (j n) k"), AX.X, ALU.add).then_inc(zsum_done, 1)
                dve.wait_ge(zsum_done, t + 1)
                dve.reciprocal(zinv[:, :, :, :].rearrange("p j a s -> p (j a s)"), zsum[:, :]).then_inc(zinv_done, 1)
                if attn:
                    rope_products(t + 1, 2)
                    rope_products(t + 1, 3)
                for j in range(2):
                    dve.wait_ge(pT_hi_done, 2 * t + j + 1)
                    dve.tensor_tensor(**lo_part(pT_lo[:, j, :, :].rearrange("p a n -> p (a n)"), ringT[:, j, :],
                                                pT_hi[:, j, :, :].rearrange("p a n -> p (a n)"))).then_inc(pT_lo_done, 1)
                if attn:
                    rope_products(t + 1, 4)
                dve.wait_ge(o_full, t + 1)
                dve.wait_ge(zinv_done, t + 1)
                for s in range(SPT):
                    inv = zinv[:, :, :, s].rearrange("p j a -> p a j").unsqueeze(3).broadcast_to([P, KVP, 2, HD])
                    dve.tensor_tensor(o_rows[:, s, :, :].rearrange("p a (j d) -> p a j d", j=2),
                                      wide[:, s, :].rearrange("p (a j d) -> p a j d", a=KVP, j=2), inv, ALU.mult).then_inc(o_normed, 1)
                if attn:
                    v_low(t + 1)
                if res:
                    residual(t - 1)
                for s in range(SPT):
                    dve.wait_ge(oT_hi_done, SPT * t + s + 1)
                    dve.tensor_tensor(**lo_part(oT_lo[:, :, s * SEQ:(s + 1) * SEQ],
                                                ringT[:, s % 2, :].rearrange("p (n q) -> p n q", q=SEQ),
                                                oT_hi[:, :, s * SEQ:(s + 1) * SEQ])).then_inc(oT_lo_done, 1)

            attend(0, moe=False, res=False)
            attend(1, moe=False)
            with dve.Fori(2, NT - 1) as t:
                attend(t)
            attend(NT - 1, attn=False)
            dve.wait_ge(h2T_hi_done, NT - 1)
            kl_lo(NT - 2, None)
            residual(NT - 1)
            dve.wait_ge(h2T_hi_done, NT)
            kl_lo(NT - 1, None)

            dve.wait_ge(logit_full, 1)
            dve.tensor_copy(logit[:, :, :].rearrange("p t e -> p (t e)"), ringA[:, 1, 0:NT * NE]).then_inc(logit_done, 1)
            dve.wait_ge(logit_done, 1)
            for t in range(NT):
                last = dve.max(top8[:, t, :], logit[:, t, :])
            last.then_inc(route_step, 1)
            dve.wait_ge(route_step, 1)
            for t in range(NT):
                last = dve.max_index(topi[:, t, :], top8[:, t, :], logit[:, t, :])
            last.then_inc(route_step, 1)
            dve.tensor_tensor(gate[:, :, :], top8[:, :, 0:TOPK], top8[:, :, 0:1].broadcast_to([P, NT, TOPK]),
                              ALU.subtract).then_inc(route_step, 1)
            dve.wait_ge(route_step, 3)
            dve.tensor_copy(topi_f[:, :, :], topi[:, :, 0:TOPK]).then_inc(route_step, 1)
            dve.wait_ge(eidx_done, 1)
            dve.tensor_copy(eidx_f[:, :], eidx[:, :]).then_inc(route_step, 1)
            dve.wait_ge(route_step, 5)
            dve.tensor_tensor(hit[:, :, :, :].rearrange("p t k e -> p (t k) e"),
                              topi_f[:, :, :].rearrange("p t k -> p (t k)").unsqueeze(2).broadcast_to([P, NT * TOPK, NE]),
                              eidx_f[:, :].unsqueeze(1).broadcast_to([P, NT * TOPK, NE]), ALU.is_equal).then_inc(route_step, 1)
            dve.wait_ge(top_exp, 1)
            dve.tensor_reduce(gsum[:, :], tope[:, :, :], AX.X, ALU.add).then_inc(route_step, 1)
            dve.wait_ge(route_step, 7)
            dve.reciprocal(ginv[:, :], gsum[:, :]).then_inc(route_step, 1)
            dve.wait_ge(route_step, 8)
            dve.tensor_tensor(gate[:, :, :], tope[:, :, :], ginv[:, :].unsqueeze(2).broadcast_to([P, NT, TOPK]),
                              ALU.mult).then_inc(route_step, 1)
            dve.wait_ge(route_step, 9)
            hits = hit[:, :, :, :].rearrange("p t k e -> p (t k) e")
            dve.tensor_tensor(hits, hits, gate[:, :, :].rearrange("p t k -> p (t k)").unsqueeze(2).broadcast_to(
                [P, NT * TOPK, NE]), ALU.mult).then_inc(route_step, 1)
            dve.wait_ge(route_step, 10)
            dve.tensor_reduce(wtok[:, :, :], hit[:, :, :, :].rearrange("p t k e -> p t e k"), AX.X, ALU.add).then_inc(route_step, 1)

            def experts(i):
                for b in range(2):
                    for s in range(4):
                        step = i * 8 + (4 * b + s)
                        dve.wait_ge(m_gated, step + 1)
                        dve.tensor_tensor(mact[:, s % 2, :], mgated[:, s % 2, :], gu[1 - s % 2][1], ALU.mult).then_inc(m_act, 1)
                        dve.wait_ge(m_hi, step + 1)
                        dve.tensor_tensor(**lo_part(mact_lo[:, s % 2, :], mact[:, s % 2, :], mact_hi[:, s % 2, :])).then_inc(m_lo, 1)

            experts(0)
            with dve.Fori(1, NE // 2) as i:
                experts(i)
            dve.wait_ge(x_again, 16)
            dve.wait_ge(acc_full, 1)
            for h in range(4):
                dve.tensor_tensor(resid[:, 2 * h:2 * h + 2, :].rearrange("p t d -> p (t d)"), wide[:, h, :],
                                  x_fin[:, 2 * h:2 * h + 2, :].rearrange("p t d -> p (t d)"), ALU.add).then_inc(out_rows, 1)

        @block.tensor
        def _(pe):
            def product(out, st, mv, first, last):
                terms = ((st[0], mv[0]), (st[0], mv[1]), (st[1], mv[0]))
                for i, (a, b) in enumerate(terms):
                    mm = pe.matmul(out, a, b, start=first and i == 0, stop=last and i == 2, skip_group_check=True)
                return mm

            pe.wait_ge(ident_done, 1)
            for g in range(NG):
                pe.wait_ge(x_in, 16 * (g + 1))
                wait(pe, act_done, MH * g - 1)
                for k in range(KD):
                    for i in range(TPG):
                        mm = pe.transpose(gu[0][k][:, i * P:(i + 1) * P], x_rows[:, i, k * P:(k + 1) * P], ident[:, :])
                mm.then_inc(pair_full, 1)
                pe.wait_ge(xT_lo_done, KD * (g + 1))
                pe.wait_ge(lo_done, 1)
                wait(pe, act_done, MH * g)
                for i, col in enumerate((AG, AU)):
                    for k in range(KD):
                        c = col + k * P
                        mm = product(gu[1][i], (head_hi[:, c:c + P], head_lo[:, c:c + P]), (xT_hi[:, k, :], xT_lo[:, k, :]),
                                     k == 0, k == KD - 1)
                mm.then_inc(pair_full, 1)

                def gate_up(m):
                    pe.wait_ge(lo_done, 2 + m)
                    if m == 0:
                        pe.wait_ge(tm_lo_done, 3 * g + 2)
                    elif m > 1:
                        pe.wait_ge(act_done, MH * g + m - 1)
                    for i, (w, bcol) in enumerate(((WG, BG), (WU, BU))):
                        for k in range(KD):
                            c = w + k * P
                            product(gu[m % 2][i], (cw_hi[:, m, c:c + P], cw_lo[:, m, c:c + P]),
                                    (xT_hi[:, k, :], xT_lo[:, k, :]), k == 0, False)
                        mm = product(gu[m % 2][i], (cw_hi[:, m, bcol:bcol + P], cw_lo[:, m, bcol:bcol + P]),
                                     (tm_hi[:, i, :], tm_lo[:, i, :]), False, True)
                    mm.then_inc(pair_full, 1)

                def down(m):
                    pe.wait_ge(act_lo_done, MH * g + m + 1)
                    if m == 0:
                        wait(pe, meansq1_done, TPG * g)
                    h = m % 2
                    for i in range(TPG):
                        tok = slice(i * P, (i + 1) * P)
                        product(wide[:, i // 2, (i % 2) * D:(i % 2 + 1) * D], (act_hi[:, h, tok], act_lo[:, h, tok]),
                                (cw_hi[:, m, WD:WD + D], cw_lo[:, m, WD:WD + D]), m == 0 and i % 2 == 0, False)
                    mm = product(wide[:, 2, :], (cw_hi[:, m, AD:AD + P], cw_lo[:, m, AD:AD + P]),
                                 (act_hi[:, h, :], act_lo[:, h, :]), m == 0, m == MH - 1)
                    mm.then_inc(act_used, 1)

                for m in range(MH):
                    gate_up(m)
                    if m >= 1:
                        down(m - 1)
                down(MH - 1)
                pe.wait_ge(act_used, MH * (g + 1))
                pe.nop().then_inc(down_a_full, 1)
                pe.wait_ge(tm_lo_done, 3 * g + 3)
                for i in range(TPG):
                    tok = slice(i * P, (i + 1) * P)
                    mm = product(wide[:, i // 2, (i % 2) * D:(i % 2 + 1) * D], (tm_hi[:, 0, tok], tm_lo[:, 0, tok]),
                                 (head_hi[:, BD:BD + D], head_lo[:, BD:BD + D]), False, i % 2 == 1)
                mm.then_inc(c_full, 1)

            def rows_turned(moe, attn):
                if moe is not None:
                    pe.wait_ge(h2_ready, moe + 1)
                    for k in range(KD):
                        mm = pe.transpose(kl_bank(moe)[:, k * P:(k + 1) * P], hrow[:, 0, k * P:(k + 1) * P], ident[:, :])
                if attn is not None:
                    pe.wait_ge(h_ready, attn + 1)
                    for k in range(KD):
                        mm = pe.transpose(ringT[:, 1, (KD + k) * P:(KD + k + 1) * P], hrow[:, 1, k * P:(k + 1) * P], ident[:, :])
                mm.then_inc(kl_full, 1)

            def project(t, c):
                if isinstance(t, int) and t == 0:
                    pe.wait_ge(lo_done, FIRST_QKV + c + 1)
                if c == 0:
                    pe.wait_ge(hT_lo_done, t + 1)
                    wait(pe, x1_done, t - 2)
                elif c == 1:
                    wait(pe, v_lo_done, t)
                else:
                    pe.wait_ge(qk_read, QKC * t + c - 1)
                for k in range(KD):
                    mm = product(ringA[:, c % 2, :], (hT_hi[:, k, :], hT_lo[:, k, :]),
                                 (qkvw_hi[:, c, k, :], qkvw_lo[:, c, k, :]), k == 0, k == KD - 1)
                mm.then_inc(qk_full if c < QKC else v_full, 1)

            def turn_qk(t):
                pe.wait_ge(qk_roped, QKC * t + 1)
                for c in range(QKC):
                    pe.wait_ge(qk_roped, QKC * t + c + 1)
                    if c < 2:
                        wait(pe, oT_lo_done, SPT * t - 1 + c)
                    else:
                        pe.wait_ge(qkT_lo_done, QKC * t + c - 1)
                    for n in range(GROUP // P):
                        mm = pe.transpose(ringT[:, c % 2, n * P:(n + 1) * P], qr[:, c, n * P:(n + 1) * P], ident[:, :])
                    mm.then_inc(qkT_full, 1)

            def scores(t):
                pe.wait_ge(qkT_lo_done, QKC * (t + 1))
                wait(pe, o_normed, SPT * t)
                for a in range(KVP):
                    for s in range(SPT):
                        tok = slice(s * SEQ, (s + 1) * SEQ)
                        n = (a * SPT + s) * SEQ
                        for i, (q, k) in enumerate(((qT_hi, kT_hi), (qT_hi, kT_lo), (qT_lo, kT_hi))):
                            for j in range(2):
                                row = slice(j * HD, (j + 1) * HD)
                                mm = pe.matmul(wide[:, j, n:n + SEQ], q[row, a, s, :], k[row, a, tok],
                                               start=i == 0, stop=i == 2, skip_group_check=True)
                mm.then_inc(s_full, 1)

            def turn_p(t, attn, moe):
                pe.wait_ge(prob_done, t + 1)
                for j in range(2):
                    if j == 0:
                        pe.wait_ge(qkT_lo_done, QKC * (t + 1))
                    else:
                        if attn:
                            pe.wait_ge(hT_lo_done, t + 2)
                        if moe:
                            pe.wait_ge(h2T_lo_done, t - 1)
                    for a in range(KVP):
                        rows = prob[:, j, a * SPT:(a + 1) * SPT, :].rearrange("p s k -> p (s k)")
                        mm = pe.transpose(ringT[:, j, a * P:(a + 1) * P], rows, ident[:, :])
                    mm.then_inc(pT_full, 1)

            def heads_out(t):
                pe.wait_ge(pT_lo_done, 2 * t + 2)
                pe.wait_ge(v_lo_done, t + 1)
                for a in range(KVP):
                    for j in range(2):
                        n = (a * 2 + j) * HD
                        for i, (p_, v_) in enumerate(((pT_hi, v_hi), (pT_hi, v_lo), (pT_lo, v_hi))):
                            for s in range(SPT):
                                row = slice(s * SEQ, (s + 1) * SEQ)
                                mm = pe.matmul(wide[:, s, n:n + HD], p_[row, j, a, :], v_[row, n:n + HD],
                                               start=i == 0, stop=i == 2, skip_group_check=True)
                mm.then_inc(o_full, 1)

            def turn_o(t):
                for s in range(SPT):
                    pe.wait_ge(o_normed, SPT * t + s + 1)
                    if s < 2:
                        pe.wait_ge(pT_lo_done, 2 * t + s + 1)
                    else:
                        pe.wait_ge(oT_lo_done, SPT * t + s - 1)
                    for a in range(KVP):
                        mm = pe.transpose(ringT[:, s % 2, a * P:(a + 1) * P], o_rows[:, s, a, :], ident[:, :])
                    mm.then_inc(oT_full, 1)

            def attention_out(t, read):
                pe.wait_ge(oT_lo_done, SPT * (t + 1))
                if isinstance(t, int) and t == 0:
                    pe.wait_ge(lo_done, FIRST_WO + OCHUNKS)
                pe.wait_ge(qk_read, read)
                if isinstance(t, int) and t >= NT - 2:
                    pe.wait_ge(x1_done, t)
                for n in range(KVP * QPK):
                    mm = product(ringA[:, 0, 0:D], (oT_hi[:, n, :], oT_lo[:, n, :]), (wo_hi[:, n, :], wo_lo[:, n, :]),
                                 n == 0, n == KVP * QPK - 1)
                mm.then_inc(y_full, 1)

            pe.wait_ge(meansq1_done, NT)
            rows_turned(None, 0)
            for c in range(QCHUNKS):
                project(0, c)

            def attend(t, moe=True, attn=True, res=True):
                turn_qk(t)
                if moe or attn:
                    pe.wait_ge(qkT_lo_done, QKC * t + 4)
                    rows_turned(t - 2 if moe else None, t + 1 if attn else None)
                scores(t)
                if attn:
                    for c in range(QKC):
                        project(t + 1, c)
                turn_p(t, attn, moe)
                heads_out(t)
                if attn:
                    project(t + 1, QKC)
                if res:
                    attention_out(t - 1, QKC * (t + 2) if attn else QKC * NT)
                turn_o(t)

            attend(0, moe=False, res=False)
            attend(1, moe=False)
            with pe.Fori(2, NT - 1) as t:
                attend(t)
            attend(NT - 1, attn=False)
            pe.wait_ge(oT_lo_done, SPT * NT)
            rows_turned(NT - 2, None)
            attention_out(NT - 1, QKC * NT)
            rows_turned(NT - 1, None)

            pe.wait_ge(h2T_lo_done, NT)
            pe.wait_ge(lo_done, NCH)
            for t in range(NT):
                for k in range(KD):
                    tok = slice(t * P, (t + 1) * P)
                    mm = product(ringA[:, 1, t * NE:(t + 1) * NE], (h2T_hi[:, k, tok], h2T_lo[:, k, tok]),
                                 (wg_hi[:, k, :], wg_lo[:, k, :]), k == 0, k == KD - 1)
            mm.then_inc(logit_full, 1)

            def gate_up_e(e, b, n, j):
                step = e * 4 + (2 * n + j)
                if n == 0 and j == 0:
                    pe.wait_ge(lo_done, NCH + 1 + e)
                wait(pe, m_act, step - 1)
                for i in range(2):
                    for k in range(KD):
                        c = (i * KD + k) * D + j * P
                        tok = slice(n * GROUP, (n + 1) * GROUP)
                        mm = product(gu[1 - j][i], (ew_hi[:, b, c:c + P], ew_lo[:, b, c:c + P]),
                                     (h2T_hi[:, k, tok], h2T_lo[:, k, tok]), k == 0, k == KD - 1)
                mm.then_inc(m_full, 1)

            def down_e(e, b, n, j, last=False):
                pe.wait_ge(m_lo, e * 4 + (2 * n + j + 1))
                c = (2 * KD + j) * D
                for i in range(TPG):
                    tile = n * TPG + i
                    tok = slice(i * P, (i + 1) * P)
                    mm = product(wide[:, tile // 2, (tile % 2) * D:(tile % 2 + 1) * D], (mact_hi[:, j, tok], mact_lo[:, j, tok]),
                                 (ew_hi[:, b, c:c + D], ew_lo[:, b, c:c + D]), False, last)
                mm.then_inc(m_used, 1)

            def seed(tiles):
                for tile in tiles:
                    pe.matmul(wide[:, tile // 2, (tile % 2) * D:(tile % 2 + 1) * D], ident[:, :], resid[:, tile, :],
                              start=tile % 2 == 0, stop=False, skip_group_check=True)

            gate_up_e(0, 0, 0, 0)
            pe.wait_ge(logit_done, 1)
            pe.wait_ge(o_normed, SPT * NT)
            pe.wait_ge(x1_done, NT)
            seed(range(NT - 2))
            pe.wait_ge(route_step, 11)
            pe.transpose(wide[:, 3, 0:P], wtok[:, :, :].rearrange("p t e -> p (t e)"), ident[:, :]).then_inc(wT_full, 1)
            pe.wait_ge(wT_done, 1)
            seed(range(NT - 2, NT))

            STEPS = [(b, n, j) for b in range(2) for n in range(2) for j in range(2)]

            def experts(i, last=False):
                for s, (b, n, j) in enumerate(STEPS):
                    if s + 1 < len(STEPS):
                        b2, n2, j2 = STEPS[s + 1]
                        gate_up_e(i * 2 + b2, b2, n2, j2)
                    elif not last:
                        gate_up_e(i * 2 + 2, *STEPS[0])
                    down_e(i * 2 + b, b, n, j, last and b == 1)

            experts(0)
            with pe.Fori(1, NE // 2 - 1) as i:
                experts(i)
            experts(NE // 2 - 1, last=True)
            pe.wait_ge(m_used, 4 * NE)
            pe.nop().then_inc(acc_full, 1)


_INPUTS = ["x", "seq_adapter", "cond_head", "cond_w", "qkv_w", "wo_w", "gate_w", "expert_w", "norms", "consts"]


def lay_out(inputs):
    def ktiles(w):
        return w.reshape(-1, P, w.shape[-1]).transpose(1, 0, 2)

    i = {k: np.asarray(v) for k, v in inputs.items()}

    def adapters(w):
        return w.transpose(1, 0, 2).reshape(w.shape[1], NAD * RANK)

    ag, au, ad = (ktiles(adapters(i["L0_cond_A" + c])) for c in "gud")
    bg, bu, bd = (i["L0_cond_B" + c].reshape(NAD * RANK, -1) for c in "gud")
    wg, wu, wd = (ktiles(i["L0_cond_W" + c]) for c in "gud")
    head = np.concatenate([ag.reshape(P, -1), au.reshape(P, -1), bd], 1)

    def hid(w):
        return w.reshape(P, KD, MH, P).transpose(0, 2, 1, 3).reshape(P, MH, KD * P)

    cond = np.concatenate([hid(wg), hid(wu), bg.reshape(P, MH, P), bu.reshape(P, MH, P), wd, ad], 2)
    q = ktiles(i["L0_ffn_wq"]).reshape(P, KD, KVP, 2, QPK, HD).transpose(0, 1, 2, 4, 3, 5).reshape(P, KD, KVP, GROUP)
    k, v = (ktiles(i["L0_ffn_w" + c])[:, :, None, :] for c in "kv")
    qkv = np.concatenate([k, q, v], 2).transpose(0, 2, 1, 3).reshape(P, QCHUNKS, KD * GROUP)
    wo = i["L0_ffn_wo"].reshape(KVP, 2, QPK, HD, D).transpose(1, 3, 0, 2, 4).reshape(P, KVP * QPK, D)
    gate = ktiles(i["L0_ffn_wg"]).reshape(P, KD * NE)
    ew = np.stack([i["L0_ffn_" + n].reshape(NE, KD, P, D) for n in ("w1", "w3", "w2")], 1)
    ew = ew.transpose(0, 3, 1, 2, 4).reshape(NE, P, ECOLS)
    norms = np.concatenate([i["L0_ffn_ln_w"].reshape(KD, P).T, i["L0_ffn_ff_ln_w"].reshape(KD, P).T], 1)
    half = HD // 2
    inv = (1.0 / np.float32(150000.0) ** (np.arange(half, dtype=np.float32) / np.float32(half))).astype(np.float32)
    ang = (np.arange(SEQ, dtype=np.float32)[:, None] * inv).astype(np.float32)
    cos, sin = np.cos(ang), np.sin(ang)
    rope = np.tile(np.concatenate([cos, cos, sin, -sin], 1), (SPT, 1))
    pos = np.arange(P) % SEQ
    mask = np.where(np.arange(SEQ)[None, :] <= pos[:, None], 0.0, -1e30).astype(np.float32)
    consts = np.concatenate([rope, mask], 1).astype(np.float32)
    arrays = dict(x=i["x"], seq_adapter=i["itok_B_0_7"], cond_head=head, cond_w=cond, qkv_w=qkv, wo_w=wo,
                  gate_w=gate, expert_w=ew, norms=norms, consts=consts)
    return {k: np.ascontiguousarray(v) for k, v in arrays.items()}


def kernel(**inputs):
    import concourse.bacc as bacc
    from concourse.bass_utils import run_bass_kernel_spmd

    nc = bacc.Bacc("TRN2", target_bir_lowering=False, num_devices=1)
    laid = lay_out(inputs)
    args = [nc.dram_tensor(f"in_{n}", laid[n].shape, mybir.dt.from_np(laid[n].dtype), kind="ExternalInput").ap() for n in _INPUTS]
    out = nc.dram_tensor("out_0", inputs["x"].shape, F32, kind="ExternalOutput").ap()
    build(nc, *args, out)
    result = run_bass_kernel_spmd(nc, [{f"in_{n}": laid[n] for n in _INPUTS}], core_ids=[0])
    return result.results[0]["out_0"]
```

```python
from contextlib import ExitStack

import numpy as np

import concourse.bass as bass
from concourse import mybir

ALU = mybir.AluOpType
ACT = mybir.ActivationFunctionType
F32 = mybir.dt.float32
F32R = mybir.dt.float32r
I32 = mybir.dt.int32
U32 = mybir.dt.uint32
AX = mybir.AxisListType

P = 128
SEQ = 32
D = 256
KD = D // P
T = 1024
NT = T // P
SPT = P // SEQ
GROUP = 512
NG = T // GROUP
TPG = GROUP // P
HID = 1024
MH = HID // P
NAD = 8
RANK = 16
HEADS, KVH, HD = 32, 8, 64
QPK = HEADS // KVH
KVP = KVH // 2
QKC = (HEADS + KVH) * HD // GROUP
NE, TOPK = 16, 4
EPS = 1e-5
SCALE = 1.0 / 8.0
WG, WU, BG, BU, WD, AD, MCOLS = 0, 256, 512, 640, 768, 1024, 1152
AG, AU, BD, HCOLS = 0, 256, 512, 768
QCHUNKS = (HEADS + 2 * KVH) * HD // GROUP
OCHUNKS = 4
ECOLS = 3 * KD * D
C_COS, C_SIN, C_MASK, C_LN, C_FF, C_EXP, C_EPS, CCOLS = 0, 64, 128, 384, 386, 388, 389, 390


def build(nc, x, seq_adapter, cond_head, cond_w, qkv_w, wo_w, gate_w, expert_w, norms, consts, out):
    with ExitStack() as ctx:
        cursor = [nc.sbuf_base + 31 & ~31]

        def sb(name, shape, dt=F32):
            size = 4 * int(np.prod(shape[1:]))
            t = nc.alloc_sbuf_tensor_at(name, shape, dt, offset=cursor[0])
            cursor[0] += size + 31 & ~31
            assert cursor[0] <= nc.sbuf_usable_end, (name, cursor[0], nc.sbuf_usable_end)
            return t

        def pair(name, shape):
            return sb(name + "_hi", shape, F32R), sb(name + "_lo", shape, F32R)

        def sem(name):
            return ctx.enter_context(nc.semaphore(name))

        def ps(name, shape):
            return ctx.enter_context(nc.psum_tensor(name, shape, F32))

        resid = sb("resid", [P, NT, D])
        ident = sb("ident", [P, P])
        cst = sb("cst", [P, CCOLS])
        staging = sb("staging", [P, 2, MCOLS])
        seq_ids = sb("seq_ids", [P, NT * SPT], I32)
        part_id = sb("part_id", [P, 1], I32)
        part_f = sb("part_f", [P, 1])
        row_off = sb("row_off", [P, NT * SPT])
        below = sb("below", [P, NT * SPT])
        amask = sb("amask", [P, NT * SPT])
        meansq1 = sb("meansq1", [P, NT])
        shifted1 = sb("shifted1", [P, NT])
        rstd1 = sb("rstd1", [P, NT])
        meansq2 = sb("meansq2", [P, 1])
        shifted2 = sb("shifted2", [P, 1])
        rstd2 = sb("rstd2", [P, 1])
        wg_hi, wg_lo = pair("wgate", [P, KD, NE])
        qkv_at = cursor[0]
        qkvw_hi, qkvw_lo = pair("qkvw", [P, QCHUNKS, KD, GROUP])
        overlay = cursor[0]
        x_rows = sb("x_rows", [P, TPG, D])
        head_hi, head_lo = pair("head", [P, HCOLS])
        cw_hi, cw_lo = pair("cw", [P, MH, MCOLS])
        xT_hi, xT_lo = pair("xT", [P, KD, GROUP])
        tm = sb("tm", [P, 2, GROUP])
        tm_hi, tm_lo = pair("tmp", [P, 2, GROUP])
        silu_g = sb("silu_g", [P, 2, GROUP])
        act = sb("act", [P, 2, GROUP])
        act_hi, act_lo = pair("actp", [P, 2, GROUP])
        cursor[0] = overlay
        wo_hi, wo_lo = pair("wo", [P, KVP * QPK, D])
        hrow = sb("hrow", [P, 2, D])
        hT_hi, hT_lo = pair("hT", [P, KD, P])
        h2T_hi, h2T_lo = pair("h2T", [P, KD, T])
        qc = sb("qc", [P, 2, GROUP])
        qs = sb("qs", [P, 2, GROUP])
        qr = sb("qr", [P, QKC, GROUP])
        kT_blk = sb("kT_blk", [P, KVP, SPT, 2, 2, SEQ], F32R)
        v_blk_hi, v_blk_lo = pair("v_blk", [P, KVH, SPT, HD])
        pT_hi, pT_lo = pair("pT", [P, KVH, P])
        shared = cursor[0]
        qT_hi, qT_lo = pair("qT", [P, KVP, SPT, P])
        after = cursor[0]
        cursor[0] = shared
        o_rows = sb("o_rows", [P, SPT, KVP, P])
        cursor[0] = after
        after = cursor[0]
        z = sb("z", [P, KVP, 2 * SPT, SEQ])
        cursor[0] = after
        v_hi, v_lo = pair("v", [P, GROUP])
        zmax = sb("zmax", [P, KVH * SPT])
        zsum = sb("zsum", [P, KVH * SPT])
        zinv = sb("zinv", [P, KVP, 2, SPT])
        oT_hi, oT_lo = pair("oT", [P, KVP * QPK, P])
        end_of_attention = cursor[0]
        cursor[0] = qkv_at
        ew_hi, ew_lo = pair("ew", [P, 2, ECOLS])
        ew_raw = sb("ew_raw", [P, 2, ECOLS])
        wbc = sb("wbc", [P, 2, T])
        assert cursor[0] <= overlay, (cursor[0], overlay)
        cursor[0] = shared
        wtok = sb("wtok", [P, NT, NE])
        wT = sb("wT", [P, P])
        logit = sb("logit", [P, NT, NE])
        top8 = sb("top8", [P, NT, 8])
        topi = sb("topi", [P, NT, 8], U32)
        topi_f = sb("topi_f", [P, NT, TOPK])
        tope = sb("tope", [P, NT, TOPK])
        gsum = sb("gsum", [P, NT])
        ginv = sb("ginv", [P, NT])
        gate = sb("gate", [P, NT, TOPK])
        eidx = sb("eidx", [P, NE], I32)
        eidx_f = sb("eidx_f", [P, NE])
        hit = sb("hit", [P, NT, TOPK, NE])
        x_fin = sb("x_fin", [P, NT, D])
        msilu = sb("msilu", [P, 2, GROUP])
        mgated = sb("mgated", [P, 2, GROUP])
        mact = sb("mact", [P, 2, GROUP])
        mact_hi, mact_lo = pair("mactp", [P, 2, GROUP])
        assert cursor[0] <= end_of_attention

        w_dram = nc.dram_tensor("moe_weights", (NE, NT, P), F32, kind="Internal").ap()

        ringA = ps("ringA", [P, 2, GROUP])
        ringT = ps("ringT", [P, 2, GROUP])
        wide = ps("wide", [P, 4, GROUP])
        gu = [(ringA[:, 0, :], ringA[:, 1, :]), (ringT[:, 0, :], ringT[:, 1, :])]

        x_in = sem("x_in")
        cst_in = sem("cst_in")
        ids_in = sem("ids_in")
        ident_zero, ident_done = sem("ident_zero"), sem("ident_done")
        powers_set = sem("powers_set")
        mask_step, mask_done = sem("mask_step"), sem("mask_done")
        raw_in = [sem(f"raw_in{i}") for i in range(2)]
        NCH = 1 + MH + QCHUNKS + OCHUNKS + 1
        hi_in = [sem(f"hi_in{i}") for i in range(NCH)]
        lo_done = sem("lo_done")
        pair_full = sem("pair_full")
        xT_hi_done, xT_lo_done = sem("xT_hi_done"), sem("xT_lo_done")
        tm_masked = sem("tm_masked")
        tm_hi_done = sem("tm_hi_done")
        tm_lo_done = sem("tm_lo_done")
        silu_done = sem("silu_done")
        act_done = sem("act_done")
        act_hi_done = sem("act_hi_done")
        act_lo_done = sem("act_lo_done")
        act_used = sem("act_used")
        down_a_full = sem("down_a_full")
        c_full = sem("c_full")
        c_copied = sem("c_copied")
        meansq1_done, shifted1_done, rstd1_done = sem("meansq1_done"), sem("shifted1_done"), sem("rstd1_done")

        h_ready = sem("h_ready")
        h2_ready = sem("h2_ready")
        kl_full = sem("kl_full")
        hT_hi_done, hT_lo_done = sem("hT_hi_done"), sem("hT_lo_done")
        h2T_hi_done, h2T_lo_done = sem("h2T_hi_done"), sem("h2T_lo_done")
        qk_full, qk_read, qk_roped = sem("qk_full"), sem("qk_read"), sem("qk_roped")
        blocks_zero, v_spread = sem("blocks_zero"), sem("v_spread")
        v_full, v_hi_done, v_lo_done = sem("v_full"), sem("v_hi_done"), sem("v_lo_done")
        qkT_full, qkT_hi_done, qkT_lo_done = sem("qkT_full"), sem("qkT_hi_done"), sem("qkT_lo_done")
        s_full, z_masked, zmax_done, z_shifted = sem("s_full"), sem("z_masked"), sem("zmax_done"), sem("z_shifted")
        prob_done, zsum_done, zinv_done = sem("prob_done"), sem("zsum_done"), sem("zinv_done")
        pT_full, pT_hi_done, pT_lo_done = sem("pT_full"), sem("pT_hi_done"), sem("pT_lo_done")
        o_full, o_normed = sem("o_full"), sem("o_normed")
        oT_full, oT_hi_done, oT_lo_done = sem("oT_full"), sem("oT_hi_done"), sem("oT_lo_done")
        y_full, x1_done = sem("y_full"), sem("x1_done")
        meansq2_done, shifted2_done, rstd2_done = sem("meansq2_done"), sem("shifted2_done"), sem("rstd2_done")

        logit_full, logit_done = sem("logit_full"), sem("logit_done")
        route_step, top_exp = sem("route_step"), sem("top_exp")
        eidx_done = sem("eidx_done")
        wT_full, wT_done, w_out = sem("wT_full"), sem("wT_done"), sem("w_out")
        seed_done = sem("seed_done")
        ew_raw_in = [sem(f"ew_raw_in{i}") for i in range(2)]
        ew_lo_done = sem("ew_lo_done")
        ew_hi_in = [sem(f"ew_hi_in{i}") for i in range(2)]
        wbc_in = [sem(f"wbc_in{i}") for i in range(2)]
        x_again = sem("x_again")
        m_full, m_silu, m_gated, m_act = sem("m_full"), sem("m_silu"), sem("m_gated"), sem("m_act")
        m_hi, m_lo, m_used = sem("m_hi"), sem("m_lo"), sem("m_used")
        acc_full = sem("acc_full")
        out_rows, out_done = sem("out_rows"), sem("out_done")

        x_dram = x.rearrange("b s d -> (b s) d").rearrange("(t p) d -> p t d", p=P)
        out_dram = out.rearrange("b s d -> (b s) d").rearrange("(t p) d -> p t d", p=P)

        chunks = [(cond_head, head_hi[:, :], head_lo[:, :])]
        chunks += [(cond_w[:, m, :], cw_hi[:, m, :], cw_lo[:, m, :]) for m in range(MH)]
        FIRST_QKV = len(chunks)
        chunks += [(qkv_w[:, c, :], qkvw_hi[:, c, :, :].rearrange("p k n -> p (k n)"),
                    qkvw_lo[:, c, :, :].rearrange("p k n -> p (k n)")) for c in range(QCHUNKS)]
        FIRST_WO = len(chunks)
        per = KVP * QPK // OCHUNKS
        chunks += [(wo_w[:, c * per:(c + 1) * per, :].rearrange("p k n -> p (k n)"),
                    wo_hi[:, c * per:(c + 1) * per, :].rearrange("p k n -> p (k n)"),
                    wo_lo[:, c * per:(c + 1) * per, :].rearrange("p k n -> p (k n)"))
                   for c in range(OCHUNKS)]
        chunks += [(gate_w, wg_hi[:, :, :].rearrange("p k n -> p (k n)"),
                    wg_lo[:, :, :].rearrange("p k n -> p (k n)"))]
        assert len(chunks) == NCH

        def wait(eng, semaphore, value):
            if isinstance(value, int) and value <= 0:
                return
            eng.wait_ge(semaphore, value)

        def kl_bank(moe):
            return ringT[:, 0, :] if isinstance(moe, int) and moe == NT - 1 else ringT[:, 1, :]

        def turned(c, part, qT):
            if c > 0:
                return [(qT[:, c - 1, :, :].rearrange("p s (g q) -> p g s q", g=QPK),
                         ringT[:, c % 2, :].rearrange("p (g s q) -> p g s q", g=QPK, s=SPT))]
            bank = ringT[:, 0, :].rearrange("p (a s k) -> p a s k", a=KVP, s=SPT)
            rows = [slice(j * HD, (j + 1) * HD) for j in range(2)]
            return [(kT_blk[row, :, :, part, j, :], bank[row, :, :, :]) for j, row in enumerate(rows)]

        def o_turned(a, oT):
            return (oT[:, a * QPK:(a + 1) * QPK, :].rearrange("p g (s q) -> p g s q", s=SPT),
                    ringT[:, a % 2, :].rearrange("p (s g q) -> p g s q", s=SPT, g=QPK))

        def lo_part(lo, full, hi):
            return dict(out=lo, in0=full, in1=hi.bitcast(F32), op=ALU.subtract)

        block = ctx.enter_context(nc.Block())

        @block.sync
        def _(sp):
            def raw(n, src, cols):
                wait(sp, lo_done, n - 1)
                sp.dma_start(staging[:, n % 2, 0:cols], src).then_inc(raw_in[n % 2], 16)

            sp.dma_start(x_rows[:, :, :], x_dram[:, 0:TPG, :]).then_inc(x_in, 16)
            raw(0, chunks[0][0], chunks[0][1].shape[-1])
            raw(1, chunks[1][0], chunks[1][1].shape[-1])
            sp.dma_start(seq_ids[:, :], seq_adapter.partition_broadcast(P)).then_inc(ids_in, 16)
            sp.dma_start(cst[:, 0:C_LN], consts).then_inc(cst_in, 16)
            sp.dma_start(cst[:, C_LN:C_EXP], norms).then_inc(cst_in, 16)
            for n in range(2, FIRST_WO + 2):
                raw(n, chunks[n][0], chunks[n][1].shape[-1])
                if n == 6:
                    sp.wait_ge(pair_full, 1)
                    sp.dma_start(x_rows[:, :, :], x_dram[:, TPG:NT, :]).then_inc(x_in, 16)

            def spread_v(t):
                sp.wait_ge(v_lo_done, t + 1)
                for src, dst in ((v_hi, v_blk_hi), (v_lo, v_blk_lo)):
                    for q in range(SPT):
                        row = slice(q * SEQ, (q + 1) * SEQ)
                        sp.dma_start(dst[row, :, q, :].bitcast(F32), src[row, :].bitcast(F32).rearrange("p (h d) -> p h d", d=HD)).then_inc(v_spread, 16)

            sp.wait_ge(blocks_zero, 3)
            spread_v(0)
            for n in range(FIRST_WO + 2, NCH):
                raw(n, chunks[n][0], chunks[n][1].shape[-1])
            with sp.Fori(1, NT) as t:
                spread_v(t)

            sp.wait_ge(v_full, NT)
            for b in range(2):
                sp.dma_start(ew_raw[:, b, :], expert_w[b, :, :]).then_inc(ew_raw_in[b], 16)
            sp.wait_ge(wT_done, 1)
            sp.dma_start(w_dram.rearrange("e t p -> t e p"), wT[:, :]).then_inc(w_out, 16)
            sp.wait_ge(w_out, 16)
            for b in range(2):
                sp.dma_start(wbc[:, b, :], w_dram[b, :, :].rearrange("t p -> (t p)").partition_broadcast(P)
                             ).then_inc(wbc_in[b], 16)
            sp.dma_start(x_fin[:, :, :], x_dram).then_inc(x_again, 16)
            with sp.Fori(1, NE // 2) as i:
                for b in range(2):
                    e = i * 2 + b
                    sp.wait_ge(ew_lo_done, e - 1)
                    sp.dma_start(ew_raw[:, b, :], expert_w[bass.ds(e, 1), :, :].rearrange("o p n -> (o p) n")
                                 ).then_inc(ew_raw_in[b], 16)
                    sp.wait_ge(m_gated, (e - 1) * 4)
                    sp.dma_start(wbc[:, b, :], w_dram[bass.ds(e, 1), :, :].rearrange("o t p -> (o t p)").partition_broadcast(P)
                                 ).then_inc(wbc_in[b], 16)
            for h in range(4):
                sp.wait_ge(out_rows, h + 1)
                sp.dma_start(out_dram[:, 2 * h:2 * h + 2, :], resid[:, 2 * h:2 * h + 2, :]).then_inc(out_done, 16)
            sp.wait_ge(out_done, 16 * 4)

        @block.gpsimd
        def _(pool):
            for n in range(FIRST_WO):
                pool.dma_start(chunks[n][1], chunks[n][0]).then_inc(hi_in[n], 16)
                if n == 0:
                    pool.memset(ident[:, :], 0.0).then_inc(ident_zero, 1)
                    pool.iota(part_id[:, :], pattern=[[0, 1]], base=0, channel_multiplier=1).then_inc(mask_step, 1)
                    pool.memset(cst[:, C_EXP:C_EXP + 1], -0.5).then_inc(powers_set, 1)
                    pool.memset(cst[:, C_EPS:C_EPS + 1], EPS).then_inc(powers_set, 1)
                    pool.wait_ge(ident_zero, 1)
                    pool.affine_select(out=ident[:, :], in_=ident[:, :], compare_op=ALU.not_equal, fill=1.0,
                                       base=0, pattern=[[-1, P]], channel_multiplier=1).then_inc(ident_done, 1)
            pool.dma_start(chunks[NCH - 1][1], chunks[NCH - 1][0]).then_inc(hi_in[NCH - 1], 16)

            def split(n):
                _src, hi, lo = chunks[n]
                pool.wait_ge(raw_in[n % 2], 16 * (n // 2 + 1))
                pool.wait_ge(hi_in[n], 16)
                pool.wait_ge(lo_done, n)
                pool.tensor_tensor(**lo_part(lo, staging[:, n % 2, 0:hi.shape[-1]], hi)).then_inc(lo_done, 1)

            for n in range(2, FIRST_WO):
                split(n)
            pool.wait_ge(powers_set, 2)
            for g in range(NG):
                cols = slice(g * TPG, (g + 1) * TPG)
                pool.wait_ge(meansq1_done, TPG * (g + 1))
                pool.tensor_scalar(shifted1[:, cols], meansq1[:, cols], EPS, None, ALU.add).then_inc(shifted1_done, 1)
                pool.wait_ge(shifted1_done, g + 1)
                pool.tensor_tensor(rstd1[:, cols], shifted1[:, cols],
                                   cst[:, C_EXP:C_EXP + 1].broadcast_to([P, TPG]), ALU.pow).then_inc(rstd1_done, 1)
            pool.wait_ge(rstd1_done, NG)
            pool.wait_ge(c_full, NG)

            def attention_rows(t):
                wait(pool, kl_full, t)
                pool.tensor_tensor(hrow[:, 1, :], resid[:, t, :], rstd1[:, bass.ds(t, 1)].broadcast_to([P, D]),
                                   ALU.mult).then_inc(h_ready, 1)

            def rope_add(t, c):
                pool.wait_ge(qk_read, QKC * t + c + 1)
                wait(pool, qkT_full, QKC * t)
                cos = qc[:, c % 2, :].rearrange("p (h f d) -> p h f d", f=2, d=HD // 2)
                sin = qs[:, c % 2, :].rearrange("p (h f d) -> p h f d", f=2, d=HD // 2)
                rot = qr[:, c, :].rearrange("p (h f d) -> p h f d", f=2, d=HD // 2)
                for f in range(2):
                    last = pool.tensor_tensor(rot[:, :, f, :], cos[:, :, f, :], sin[:, :, 1 - f, :], ALU.add)
                last.then_inc(qk_roped, 1)

            def shift(t):
                pool.wait_ge(zmax_done, t + 1)
                zv = z[:, :, :, :].rearrange("p a n k -> p (a n) k")
                pool.tensor_tensor(zv, zv, zmax[:, :].unsqueeze(2).broadcast_to([P, KVH * SPT, SEQ]),
                                   ALU.subtract).then_inc(z_shifted, 1)

            def moe_rows(t):
                pool.wait_ge(meansq2_done, t + 1)
                pool.tensor_tensor(shifted2[:, :], meansq2[:, :], cst[:, C_EPS:C_EPS + 1], ALU.add).then_inc(shifted2_done, 1)
                pool.wait_ge(shifted2_done, t + 1)
                pool.tensor_tensor(rstd2[:, :], shifted2[:, :], cst[:, C_EXP:C_EXP + 1], ALU.pow).then_inc(rstd2_done, 1)
                pool.wait_ge(rstd2_done, t + 1)
                if not (isinstance(t, int) and t == 0):
                    pool.wait_ge(kl_full, t + 3)
                pool.tensor_tensor(hrow[:, 0, :], resid[:, t, :], rstd2[:, 0:1].broadcast_to([P, D]),
                                   ALU.mult).then_inc(h2_ready, 1)

            attention_rows(0)
            pool.memset(kT_blk[:, :, :, :, :, :].rearrange("p a s x j k -> p (a s x j k)").bitcast(F32), 0.0).then_inc(blocks_zero, 1)
            for n in range(FIRST_WO, FIRST_WO + OCHUNKS):
                pool.dma_start(chunks[n][1], chunks[n][0]).then_inc(hi_in[n], 16)
            for c in range(QKC):
                rope_add(0, c)
            attention_rows(1)

            def attend(t, first=False, last=False, rows_left=True):
                shift(t)
                if not last:
                    for c in range(QKC):
                        rope_add(t + 1, c)
                if not first:
                    moe_rows(t - 1)
                if rows_left:
                    attention_rows(t + 2)

            attend(0, first=True)
            for n in range(FIRST_WO, NCH):
                split(n)
            attend(1)
            with pool.Fori(2, NT - 2) as t:
                attend(t)
            attend(NT - 2, rows_left=False)
            attend(NT - 1, last=True, rows_left=False)
            moe_rows(NT - 1)

            def expert_split(e, b, first=False):
                if not first:
                    pool.wait_ge(m_used, 4 * (e - 1))
                pool.dma_start(ew_hi[:, b, :], expert_w[bass.ds(e, 1), :, :].rearrange("o p n -> (o p) n")
                               ).then_inc(ew_hi_in[b], 16)

            def expert_lo(e, b, i):
                pool.wait_ge(ew_hi_in[b], 16 * (i + 1))
                pool.wait_ge(ew_raw_in[b], 16 * (i + 1))
                pool.tensor_tensor(**lo_part(ew_lo[:, b, :], ew_raw[:, b, :], ew_hi[:, b, :])).then_inc(ew_lo_done, 1)

            def experts(i, first=False, last=False):
                for b in range(2):
                    e = i * 2 + b
                    if not (last and b == 1):
                        expert_split(e + 1, 1 - b, first and b == 0)
                        expert_lo(e + 1, 1 - b, i + b)

            pool.wait_ge(v_full, NT)
            pool.iota(eidx[:, :], pattern=[[1, NE]], base=0, channel_multiplier=0).then_inc(eidx_done, 1)
            expert_split(0, 0, True)
            expert_lo(0, 0, 0)
            experts(0, first=True)
            with pool.Fori(1, NE // 2 - 1) as i:
                experts(i)
            experts(NE // 2 - 1, last=True)

        @block.scalar
        def _(act_e):
            def copy(out, in_, scale=None):
                if scale is None:
                    return act_e.activation(out, in_, ACT.Copy)
                return act_e.activation(out, in_, ACT.Copy, scale=scale)

            for g in range(NG):
                act_e.wait_ge(pair_full, (MH + 2) * g + 1)
                for k in range(KD):
                    copy(xT_hi[:, k, :], gu[0][k]).then_inc(xT_hi_done, 1)
                for i in range(2):
                    act_e.wait_ge(tm_masked, 3 * g + i + 1)
                    copy(tm_hi[:, i, :], tm[:, i, :]).then_inc(tm_hi_done, 1)
                for m in range(MH):
                    act_e.wait_ge(pair_full, (MH + 2) * g + 3 + m)
                    wait(act_e, act_done, MH * g + m - 1)
                    act_e.activation(silu_g[:, m % 2, :], gu[m % 2][0], ACT.Silu).then_inc(silu_done, 1)
                    act_e.wait_ge(act_done, MH * g + m + 1)
                    wait(act_e, act_used, MH * g + m - 1)
                    copy(act_hi[:, m % 2, :], act[:, m % 2, :]).then_inc(act_hi_done, 1)
                act_e.wait_ge(tm_masked, 3 * g + 3)
                copy(tm_hi[:, 0, :], tm[:, 0, :]).then_inc(tm_hi_done, 1)
                act_e.wait_ge(c_full, g + 1)
                for i in range(TPG):
                    rows = wide[:, i // 2, (i % 2) * D:(i % 2 + 1) * D]
                    copy(resid[:, g * TPG + i, :], rows)
                    wait(act_e, meansq1_done, g * TPG + i)
                    act_e.activation(act[:, 0, 0:D], rows, ACT.Square, scale=D ** -0.5,
                                     accum_out=meansq1[:, g * TPG + i:g * TPG + i + 1]).then_inc(meansq1_done, 1)

            def kl_hi(moe, attn):
                if moe is not None:
                    for k in range(KD):
                        last = copy(h2T_hi[:, k, bass.ds(moe * P, P)], kl_bank(moe)[:, k * P:(k + 1) * P],
                                    cst[:, C_FF + k:C_FF + k + 1])
                    last.then_inc(h2T_hi_done, 1)
                if attn is not None:
                    for k in range(KD):
                        last = copy(hT_hi[:, k, :], ringT[:, 1, (KD + k) * P:(KD + k + 1) * P],
                                    cst[:, C_LN + k:C_LN + k + 1])
                    last.then_inc(hT_hi_done, 1)

            def v_part(t):
                act_e.wait_ge(v_full, t + 1)
                wait(act_e, v_spread, 16 * 2 * SPT * t)
                copy(v_hi[:, :], ringA[:, 1, :]).then_inc(v_hi_done, 1)

            def residual_square(t):
                act_e.wait_ge(x1_done, t + 1)
                wait(act_e, shifted2_done, t)
                act_e.wait_ge(meansq1_done, NT) if isinstance(t, int) and t == 0 else wait(act_e, meansq2_done, t)
                act_e.activation(hrow[:, 0, :], resid[:, t, :], ACT.Square, scale=D ** -0.5,
                                 accum_out=meansq2[:, :]).then_inc(meansq2_done, 1)

            act_e.wait_ge(cst_in, 32)
            act_e.wait_ge(blocks_zero, 3)
            act_e.wait_ge(kl_full, 1)
            kl_hi(None, 0)
            v_part(0)

            def attend(t, moe=True, attn=True, square=True):
                for c in range(QKC):
                    act_e.wait_ge(qkT_full, QKC * t + c + 1)
                    for dst, src in turned(c, 0, qT_hi):
                        last = copy(dst, src)
                    last.then_inc(qkT_hi_done, 1)
                if moe or attn:
                    act_e.wait_ge(kl_full, t + 2)
                    kl_hi(t - 2 if moe else None, t + 1 if attn else None)
                act_e.wait_ge(z_shifted, t + 1)
                zv = z[:, :, :, :].rearrange("p a n k -> p (a n k)")
                act_e.activation(zv, zv, ACT.Exp).then_inc(prob_done, 1)
                for j in range(2):
                    act_e.wait_ge(pT_full, 2 * t + j + 1)
                    copy(pT_hi[:, j * 4:(j + 1) * 4, :].rearrange("p a n -> p (a n)"), ringT[:, j, :]).then_inc(pT_hi_done, 1)
                if attn:
                    v_part(t + 1)
                if square:
                    residual_square(t - 1)
                for s in range(SPT):
                    act_e.wait_ge(oT_full, SPT * t + s + 1)
                    copy(*o_turned(s, oT_hi)).then_inc(oT_hi_done, 1)

            attend(0, moe=False, square=False)
            attend(1, moe=False)
            with act_e.Fori(2, NT - 1) as t:
                attend(t)
            attend(NT - 1, attn=False)
            act_e.wait_ge(kl_full, NT + 2)
            kl_hi(NT - 2, None)
            residual_square(NT - 1)
            act_e.wait_ge(kl_full, NT + 3)
            kl_hi(NT - 1, None)

            act_e.wait_ge(route_step, 3)
            act_e.activation(tope[:, :, :].rearrange("p t k -> p (t k)"), gate[:, :, :].rearrange("p t k -> p (t k)"),
                             ACT.Exp).then_inc(top_exp, 1)
            act_e.wait_ge(wT_full, 1)
            copy(wT[:, :], wide[:, 3, 0:P]).then_inc(wT_done, 1)

            def experts(i):
                for b in range(2):
                    for s in range(4):
                        step = i * 8 + (4 * b + s)
                        act_e.wait_ge(m_full, step + 1)
                        wait(act_e, m_gated, step - 1)
                        act_e.activation(msilu[:, s % 2, :], gu[1 - s % 2][0], ACT.Silu).then_inc(m_silu, 1)
                        act_e.wait_ge(m_act, step + 1)
                        wait(act_e, m_used, step - 1)
                        copy(mact_hi[:, s % 2, :], mact[:, s % 2, :]).then_inc(m_hi, 1)

            experts(0)
            with act_e.Fori(1, NE // 2) as i:
                experts(i)

        @block.vector
        def _(dve):
            for n in range(2):
                _src, hi, lo = chunks[n]
                dve.wait_ge(raw_in[n], 16)
                dve.wait_ge(hi_in[n], 16)
                dve.tensor_tensor(**lo_part(lo, staging[:, n, 0:hi.shape[-1]], hi)).then_inc(lo_done, 1)
            dve.wait_ge(ids_in, 16)
            dve.wait_ge(mask_step, 1)
            dve.tensor_copy(part_f[:, :], part_id[:, :]).then_inc(mask_done, 1)
            dve.wait_ge(mask_done, 1)
            dve.tensor_scalar(row_off[:, :], seq_ids[:, :], -float(RANK), part_f[:, 0:1], ALU.mult, ALU.add).then_inc(mask_done, 1)
            dve.wait_ge(mask_done, 2)
            dve.tensor_scalar(below[:, :], row_off[:, :], RANK - 0.5, None, ALU.is_le).then_inc(mask_done, 1)
            dve.wait_ge(mask_done, 3)
            dve.scalar_tensor_tensor(out=amask[:, :], in0=row_off[:, :], scalar=0.0, in1=below[:, :],
                                     op0=ALU.is_ge, op1=ALU.mult).then_inc(mask_done, 1)
            dve.wait_ge(mask_done, 4)

            def masked(g, i, src):
                picked = amask[:, g * TPG * SPT:(g + 1) * TPG * SPT].unsqueeze(2).broadcast_to([P, TPG * SPT, SEQ])
                dve.tensor_tensor(tm[:, i, :].rearrange("p (s n) -> p s n", n=SEQ), src.rearrange("p (s n) -> p s n", n=SEQ),
                                  picked, ALU.mult).then_inc(tm_masked, 1)

            def tm_low(g, i, count):
                dve.wait_ge(tm_hi_done, 3 * g + count)
                dve.tensor_tensor(**lo_part(tm_lo[:, i, :], tm[:, i, :], tm_hi[:, i, :])).then_inc(tm_lo_done, 1)

            for g in range(NG):
                for k in range(KD):
                    dve.wait_ge(xT_hi_done, KD * g + k + 1)
                    dve.tensor_tensor(**lo_part(xT_lo[:, k, :], gu[0][k], xT_hi[:, k, :])).then_inc(xT_lo_done, 1)
                dve.wait_ge(pair_full, (MH + 2) * g + 2)
                for i in range(2):
                    masked(g, i, gu[1][i])
                for i in range(2):
                    tm_low(g, i, i + 1)
                for m in range(MH):
                    dve.wait_ge(silu_done, MH * g + m + 1)
                    dve.tensor_tensor(act[:, m % 2, :], silu_g[:, m % 2, :], gu[m % 2][1], ALU.mult).then_inc(act_done, 1)
                    dve.wait_ge(act_hi_done, MH * g + m + 1)
                    dve.tensor_tensor(**lo_part(act_lo[:, m % 2, :], act[:, m % 2, :], act_hi[:, m % 2, :])).then_inc(act_lo_done, 1)
                dve.wait_ge(down_a_full, g + 1)
                masked(g, 0, wide[:, 2, :])
                tm_low(g, 0, 3)

            dve.wait_ge(cst_in, 32)
            dve.wait_ge(meansq1_done, NT)

            def kl_lo(moe, attn):
                if moe is not None:
                    for k in range(KD):
                        last = dve.scalar_tensor_tensor(
                            out=h2T_lo[:, k, bass.ds(moe * P, P)], in0=kl_bank(moe)[:, k * P:(k + 1) * P],
                            scalar=cst[:, C_FF + k:C_FF + k + 1], in1=h2T_hi[:, k, bass.ds(moe * P, P)].bitcast(F32),
                            op0=ALU.mult, op1=ALU.subtract)
                    last.then_inc(h2T_lo_done, 1)
                if attn is not None:
                    for k in range(KD):
                        last = dve.scalar_tensor_tensor(
                            out=hT_lo[:, k, :], in0=ringT[:, 1, (KD + k) * P:(KD + k + 1) * P],
                            scalar=cst[:, C_LN + k:C_LN + k + 1], in1=hT_hi[:, k, :].bitcast(F32),
                            op0=ALU.mult, op1=ALU.subtract)
                    last.then_inc(hT_lo_done, 1)

            def rope_products(t, c):
                dve.wait_ge(qk_full, QKC * t + c + 1)
                wait(dve, qk_roped, QKC * t + c - 1)
                heads = GROUP // HD
                src = ringA[:, c % 2, :].rearrange("p (h d) -> p h d", d=HD)
                for dst, col in ((qc, C_COS), (qs, C_SIN)):
                    table = cst[:, col:col + HD].unsqueeze(1).broadcast_to([P, heads, HD])
                    last = dve.tensor_tensor(dst[:, c % 2, :].rearrange("p (h d) -> p h d", d=HD), src, table, ALU.mult)
                last.then_inc(qk_read, 1)

            def v_low(t):
                dve.wait_ge(v_hi_done, t + 1)
                dve.tensor_tensor(**lo_part(v_lo[:, :], ringA[:, 1, :], v_hi[:, :])).then_inc(v_lo_done, 1)

            def residual(t):
                dve.wait_ge(y_full, t + 1)
                dve.tensor_tensor(resid[:, t, :], ringA[:, 0, 0:D], resid[:, t, :], ALU.add).then_inc(x1_done, 1)

            dve.wait_ge(c_full, NG)
            for blk in (v_blk_hi, v_blk_lo):
                dve.memset(blk[:, :, :, :].rearrange("p h s d -> p (h s d)").bitcast(F32), 0.0).then_inc(blocks_zero, 1)
            dve.wait_ge(hT_hi_done, 1)
            kl_lo(None, 0)
            for c in range(QKC):
                rope_products(0, c)
            v_low(0)

            def attend(t, moe=True, attn=True, res=True):
                for c in range(QKC):
                    dve.wait_ge(qkT_hi_done, QKC * t + c + 1)
                    for (hi, src), (lo, _src) in zip(turned(c, 0, qT_hi), turned(c, 1, qT_lo)):
                        last = dve.tensor_tensor(**lo_part(lo, src, hi))
                    last.then_inc(qkT_lo_done, 1)
                if moe:
                    dve.wait_ge(h2T_hi_done, t - 1)
                if attn:
                    dve.wait_ge(hT_hi_done, t + 2)
                kl_lo(t - 2 if moe else None, t + 1 if attn else None)
                dve.wait_ge(s_full, t + 1)
                dve.wait_ge(v_spread, 16 * 2 * SPT * (t + 1))
                mask = cst[:, C_MASK:C_MASK + 2 * P].unsqueeze(1).broadcast_to([P, KVP, 2 * P])
                zv = z[:, :, :, :].rearrange("p a n k -> p a (n k)")
                for part, more in ((0, mask), (1, zv)):
                    if part:
                        dve.wait_ge(z_masked, 2 * t + 1)
                    src = wide[:, :, part * 2 * P:(part + 1) * 2 * P]
                    dve.scalar_tensor_tensor(out=zv, in0=src, scalar=SCALE, in1=more,
                                             op0=ALU.mult, op1=ALU.add).then_inc(z_masked, 1)
                dve.wait_ge(z_masked, 2 * t + 2)
                dve.tensor_reduce(zmax[:, :], z[:, :, :, :].rearrange("p a n k -> p (a n) k"), AX.X, ALU.max).then_inc(zmax_done, 1)
                if attn:
                    rope_products(t + 1, 0)
                    rope_products(t + 1, 1)
                dve.wait_ge(prob_done, t + 1)
                dve.tensor_reduce(zsum[:, :], z[:, :, :, :].rearrange("p a n k -> p (a n) k"), AX.X, ALU.add).then_inc(zsum_done, 1)
                dve.wait_ge(zsum_done, t + 1)
                dve.reciprocal(zinv[:, :, :, :].rearrange("p a j s -> p (a j s)"), zsum[:, :]).then_inc(zinv_done, 1)
                if attn:
                    rope_products(t + 1, 2)
                    rope_products(t + 1, 3)
                for j in range(2):
                    dve.wait_ge(pT_hi_done, 2 * t + j + 1)
                    half = slice(j * 4, (j + 1) * 4)
                    dve.tensor_tensor(**lo_part(pT_lo[:, half, :].rearrange("p a n -> p (a n)"), ringT[:, j, :],
                                                pT_hi[:, half, :].rearrange("p a n -> p (a n)"))).then_inc(pT_lo_done, 1)
                if attn:
                    rope_products(t + 1, 4)
                dve.wait_ge(o_full, t + 1)
                dve.wait_ge(zinv_done, t + 1)
                for a in range(KVP):
                    inv = zinv[:, a, :, :].unsqueeze(3).broadcast_to([P, 2, SPT, HD])
                    dve.tensor_tensor(o_rows[:, :, a, :].rearrange("p s (j d) -> p j s d", j=2),
                                      wide[:, a, :].rearrange("p (j s d) -> p j s d", j=2, s=SPT), inv, ALU.mult).then_inc(o_normed, 1)
                if attn:
                    v_low(t + 1)
                if res:
                    residual(t - 1)
                for s in range(SPT):
                    dve.wait_ge(oT_hi_done, SPT * t + s + 1)
                    dve.tensor_tensor(**lo_part(o_turned(s, oT_lo)[0], o_turned(s, oT_hi)[1], o_turned(s, oT_hi)[0])
                                      ).then_inc(oT_lo_done, 1)

            attend(0, moe=False, res=False)
            attend(1, moe=False)
            with dve.Fori(2, NT - 1) as t:
                attend(t)
            attend(NT - 1, attn=False)
            dve.wait_ge(h2T_hi_done, NT - 1)
            kl_lo(NT - 2, None)
            residual(NT - 1)
            dve.wait_ge(h2T_hi_done, NT)
            kl_lo(NT - 1, None)

            dve.wait_ge(logit_full, 1)
            dve.tensor_copy(logit[:, :, :].rearrange("p t e -> p (t e)"), ringA[:, 1, 0:NT * NE]).then_inc(logit_done, 1)
            dve.wait_ge(logit_done, 1)
            for t in range(NT):
                last = dve.max(top8[:, t, :], logit[:, t, :])
            last.then_inc(route_step, 1)
            dve.wait_ge(route_step, 1)
            for t in range(NT):
                last = dve.max_index(topi[:, t, :], top8[:, t, :], logit[:, t, :])
            last.then_inc(route_step, 1)
            dve.tensor_tensor(gate[:, :, :], top8[:, :, 0:TOPK], top8[:, :, 0:1].broadcast_to([P, NT, TOPK]),
                              ALU.subtract).then_inc(route_step, 1)
            dve.wait_ge(route_step, 3)
            dve.tensor_copy(topi_f[:, :, :], topi[:, :, 0:TOPK]).then_inc(route_step, 1)
            dve.wait_ge(eidx_done, 1)
            dve.tensor_copy(eidx_f[:, :], eidx[:, :]).then_inc(route_step, 1)
            dve.wait_ge(route_step, 5)
            dve.tensor_tensor(hit[:, :, :, :].rearrange("p t k e -> p (t k) e"),
                              topi_f[:, :, :].rearrange("p t k -> p (t k)").unsqueeze(2).broadcast_to([P, NT * TOPK, NE]),
                              eidx_f[:, :].unsqueeze(1).broadcast_to([P, NT * TOPK, NE]), ALU.is_equal).then_inc(route_step, 1)
            dve.wait_ge(top_exp, 1)
            dve.tensor_reduce(gsum[:, :], tope[:, :, :], AX.X, ALU.add).then_inc(route_step, 1)
            dve.wait_ge(route_step, 7)
            dve.reciprocal(ginv[:, :], gsum[:, :]).then_inc(route_step, 1)
            dve.wait_ge(route_step, 8)
            dve.tensor_tensor(gate[:, :, :], tope[:, :, :], ginv[:, :].unsqueeze(2).broadcast_to([P, NT, TOPK]),
                              ALU.mult).then_inc(route_step, 1)
            dve.wait_ge(route_step, 9)
            hits = hit[:, :, :, :].rearrange("p t k e -> p (t k) e")
            dve.tensor_tensor(hits, hits, gate[:, :, :].rearrange("p t k -> p (t k)").unsqueeze(2).broadcast_to(
                [P, NT * TOPK, NE]), ALU.mult).then_inc(route_step, 1)
            dve.wait_ge(route_step, 10)
            dve.tensor_reduce(wtok[:, :, :], hit[:, :, :, :].rearrange("p t k e -> p t e k"), AX.X, ALU.add).then_inc(route_step, 1)

            def experts(i):
                for b in range(2):
                    for s in range(4):
                        step = i * 8 + (4 * b + s)
                        dve.wait_ge(m_silu, step + 1)
                        if s == 0:
                            dve.wait_ge(wbc_in[b], (i + 1) * 16)
                        n = s // 2
                        dve.tensor_tensor(mgated[:, s % 2, :], msilu[:, s % 2, :], wbc[:, b, n * GROUP:(n + 1) * GROUP],
                                          ALU.mult).then_inc(m_gated, 1)
                        dve.wait_ge(m_gated, step + 1)
                        dve.tensor_tensor(mact[:, s % 2, :], mgated[:, s % 2, :], gu[1 - s % 2][1], ALU.mult).then_inc(m_act, 1)
                        dve.wait_ge(m_hi, step + 1)
                        dve.tensor_tensor(**lo_part(mact_lo[:, s % 2, :], mact[:, s % 2, :], mact_hi[:, s % 2, :])).then_inc(m_lo, 1)

            experts(0)
            with dve.Fori(1, NE // 2) as i:
                experts(i)
            dve.wait_ge(x_again, 16)
            dve.wait_ge(acc_full, 1)
            for h in range(4):
                dve.tensor_tensor(resid[:, 2 * h:2 * h + 2, :].rearrange("p t d -> p (t d)"), wide[:, h, :],
                                  x_fin[:, 2 * h:2 * h + 2, :].rearrange("p t d -> p (t d)"), ALU.add).then_inc(out_rows, 1)

        @block.tensor
        def _(pe):
            def product(out, st, mv, first, last):
                terms = ((st[0], mv[0]), (st[0], mv[1]), (st[1], mv[0]))
                for i, (a, b) in enumerate(terms):
                    mm = pe.matmul(out, a, b, start=first and i == 0, stop=last and i == 2, skip_group_check=True)
                return mm

            pe.wait_ge(ident_done, 1)
            for g in range(NG):
                pe.wait_ge(x_in, 16 * (g + 1))
                wait(pe, act_done, MH * g - 1)
                for k in range(KD):
                    for i in range(TPG):
                        mm = pe.transpose(gu[0][k][:, i * P:(i + 1) * P], x_rows[:, i, k * P:(k + 1) * P], ident[:, :])
                mm.then_inc(pair_full, 1)
                pe.wait_ge(xT_lo_done, KD * (g + 1))
                pe.wait_ge(lo_done, 1)
                wait(pe, act_done, MH * g)
                for i, col in enumerate((AG, AU)):
                    for k in range(KD):
                        c = col + k * P
                        mm = product(gu[1][i], (head_hi[:, c:c + P], head_lo[:, c:c + P]), (xT_hi[:, k, :], xT_lo[:, k, :]),
                                     k == 0, k == KD - 1)
                mm.then_inc(pair_full, 1)

                def gate_up(m):
                    pe.wait_ge(lo_done, 2 + m)
                    if m == 0:
                        pe.wait_ge(tm_lo_done, 3 * g + 2)
                    elif m > 1:
                        pe.wait_ge(act_done, MH * g + m - 1)
                    for i, (w, bcol) in enumerate(((WG, BG), (WU, BU))):
                        for k in range(KD):
                            c = w + k * P
                            product(gu[m % 2][i], (cw_hi[:, m, c:c + P], cw_lo[:, m, c:c + P]),
                                    (xT_hi[:, k, :], xT_lo[:, k, :]), k == 0, False)
                        mm = product(gu[m % 2][i], (cw_hi[:, m, bcol:bcol + P], cw_lo[:, m, bcol:bcol + P]),
                                     (tm_hi[:, i, :], tm_lo[:, i, :]), False, True)
                    mm.then_inc(pair_full, 1)

                def down(m):
                    pe.wait_ge(act_lo_done, MH * g + m + 1)
                    if m == 0:
                        wait(pe, meansq1_done, TPG * g)
                    h = m % 2
                    for i in range(TPG):
                        tok = slice(i * P, (i + 1) * P)
                        product(wide[:, i // 2, (i % 2) * D:(i % 2 + 1) * D], (act_hi[:, h, tok], act_lo[:, h, tok]),
                                (cw_hi[:, m, WD:WD + D], cw_lo[:, m, WD:WD + D]), m == 0 and i % 2 == 0, False)
                    mm = product(wide[:, 2, :], (cw_hi[:, m, AD:AD + P], cw_lo[:, m, AD:AD + P]),
                                 (act_hi[:, h, :], act_lo[:, h, :]), m == 0, m == MH - 1)
                    mm.then_inc(act_used, 1)

                for m in range(MH):
                    gate_up(m)
                    if m >= 1:
                        down(m - 1)
                down(MH - 1)
                pe.wait_ge(act_used, MH * (g + 1))
                pe.nop().then_inc(down_a_full, 1)
                pe.wait_ge(tm_lo_done, 3 * g + 3)
                for i in range(TPG):
                    tok = slice(i * P, (i + 1) * P)
                    mm = product(wide[:, i // 2, (i % 2) * D:(i % 2 + 1) * D], (tm_hi[:, 0, tok], tm_lo[:, 0, tok]),
                                 (head_hi[:, BD:BD + D], head_lo[:, BD:BD + D]), False, i % 2 == 1)
                mm.then_inc(c_full, 1)

            def rows_turned(moe, attn):
                if moe is not None:
                    pe.wait_ge(h2_ready, moe + 1)
                    for k in range(KD):
                        mm = pe.transpose(kl_bank(moe)[:, k * P:(k + 1) * P], hrow[:, 0, k * P:(k + 1) * P], ident[:, :])
                if attn is not None:
                    pe.wait_ge(h_ready, attn + 1)
                    for k in range(KD):
                        mm = pe.transpose(ringT[:, 1, (KD + k) * P:(KD + k + 1) * P], hrow[:, 1, k * P:(k + 1) * P], ident[:, :])
                mm.then_inc(kl_full, 1)

            def project(t, c):
                if isinstance(t, int) and t == 0:
                    pe.wait_ge(lo_done, FIRST_QKV + c + 1)
                if c == 0:
                    pe.wait_ge(hT_lo_done, t + 1)
                    wait(pe, x1_done, t - 2)
                elif c == 1:
                    wait(pe, v_lo_done, t)
                else:
                    pe.wait_ge(qk_read, QKC * t + c - 1)
                for k in range(KD):
                    mm = product(ringA[:, c % 2, :], (hT_hi[:, k, :], hT_lo[:, k, :]),
                                 (qkvw_hi[:, c, k, :], qkvw_lo[:, c, k, :]), k == 0, k == KD - 1)
                mm.then_inc(qk_full if c < QKC else v_full, 1)

            def turn_qk(t):
                pe.wait_ge(qk_roped, QKC * t + 1)
                for c in range(QKC):
                    pe.wait_ge(qk_roped, QKC * t + c + 1)
                    if c < 2:
                        wait(pe, oT_lo_done, SPT * t - 1 + c)
                    else:
                        pe.wait_ge(qkT_lo_done, QKC * t + c - 1)
                    for n in range(GROUP // P):
                        mm = pe.transpose(ringT[:, c % 2, n * P:(n + 1) * P], qr[:, c, n * P:(n + 1) * P], ident[:, :])
                    mm.then_inc(qkT_full, 1)

            def scores(t):
                pe.wait_ge(qkT_lo_done, QKC * (t + 1))
                wait(pe, o_normed, SPT * t)
                for a in range(KVP):
                    bank = wide[:, a, :].rearrange("p (x s k) -> p x s k", x=4, s=SPT)
                    for s in range(SPT):
                        pe.matmul(bank[:, :, s, :], qT_hi[:, a, s, :], kT_blk[:, a, s, :, :, :].rearrange("p x j k -> p (x j k)"),
                                  start=True, stop=False, skip_group_check=True)
                        mm = pe.matmul(bank[:, 0:2, s, :], qT_lo[:, a, s, :], kT_blk[:, a, s, 0, :, :].rearrange("p j k -> p (j k)"),
                                       start=False, stop=True, skip_group_check=True)
                mm.then_inc(s_full, 1)

            def turn_p(t, attn, moe):
                pe.wait_ge(prob_done, t + 1)
                for j in range(2):
                    if j == 0:
                        pe.wait_ge(qkT_lo_done, QKC * (t + 1))
                    else:
                        if attn:
                            pe.wait_ge(hT_lo_done, t + 2)
                        if moe:
                            pe.wait_ge(h2T_lo_done, t - 1)
                    for a in range(KVP):
                        n = j * 4 + a
                        rows = z[:, n // 2, (n % 2) * SPT:(n % 2 + 1) * SPT, :].rearrange("p s k -> p (s k)")
                        mm = pe.transpose(ringT[:, j, a * P:(a + 1) * P], rows, ident[:, :])
                    mm.then_inc(pT_full, 1)

            def heads_out(t):
                pe.wait_ge(pT_lo_done, 2 * t + 2)
                pe.wait_ge(v_lo_done, t + 1)
                pe.wait_ge(v_spread, 16 * 2 * SPT * (t + 1))
                for h in range(KVH):
                    v_ = [blk[:, h, :, :].rearrange("p s d -> p (s d)") for blk in (v_blk_hi, v_blk_lo)]
                    mm = product(wide[:, h // 2, (h % 2) * D:(h % 2 + 1) * D], (pT_hi[:, h, :], pT_lo[:, h, :]), v_, True, True)
                mm.then_inc(o_full, 1)

            def turn_o(t):
                for s in range(SPT):
                    pe.wait_ge(o_normed, SPT * t + s + 1)
                    if s < 2:
                        pe.wait_ge(pT_lo_done, 2 * t + s + 1)
                    else:
                        pe.wait_ge(oT_lo_done, SPT * t + s - 1)
                    for a in range(KVP):
                        mm = pe.transpose(ringT[:, s % 2, a * P:(a + 1) * P], o_rows[:, a, s, :], ident[:, :])
                    mm.then_inc(oT_full, 1)

            def attention_out(t, read):
                pe.wait_ge(oT_lo_done, SPT * (t + 1))
                if isinstance(t, int) and t == 0:
                    pe.wait_ge(lo_done, FIRST_WO + OCHUNKS)
                pe.wait_ge(qk_read, read)
                if isinstance(t, int) and t >= NT - 2:
                    pe.wait_ge(x1_done, t)
                for n in range(KVP * QPK):
                    mm = product(ringA[:, 0, 0:D], (oT_hi[:, n, :], oT_lo[:, n, :]), (wo_hi[:, n, :], wo_lo[:, n, :]),
                                 n == 0, n == KVP * QPK - 1)
                mm.then_inc(y_full, 1)

            pe.wait_ge(meansq1_done, NT)
            rows_turned(None, 0)
            for c in range(QCHUNKS):
                project(0, c)

            def attend(t, moe=True, attn=True, res=True):
                turn_qk(t)
                if moe or attn:
                    pe.wait_ge(qkT_lo_done, QKC * t + 4)
                    rows_turned(t - 2 if moe else None, t + 1 if attn else None)
                scores(t)
                if attn:
                    for c in range(QKC):
                        project(t + 1, c)
                turn_p(t, attn, moe)
                heads_out(t)
                if attn:
                    project(t + 1, QKC)
                if res:
                    attention_out(t - 1, QKC * (t + 2) if attn else QKC * NT)
                turn_o(t)

            attend(0, moe=False, res=False)
            attend(1, moe=False)
            with pe.Fori(2, NT - 1) as t:
                attend(t)
            attend(NT - 1, attn=False)
            pe.wait_ge(oT_lo_done, SPT * NT)
            rows_turned(NT - 2, None)
            attention_out(NT - 1, QKC * NT)
            rows_turned(NT - 1, None)

            pe.wait_ge(h2T_lo_done, NT)
            pe.wait_ge(lo_done, NCH)
            for t in range(NT):
                for k in range(KD):
                    tok = slice(t * P, (t + 1) * P)
                    mm = product(ringA[:, 1, t * NE:(t + 1) * NE], (h2T_hi[:, k, tok], h2T_lo[:, k, tok]),
                                 (wg_hi[:, k, :], wg_lo[:, k, :]), k == 0, k == KD - 1)
            mm.then_inc(logit_full, 1)

            def gate_up_e(e, b, n, j):
                step = e * 4 + (2 * n + j)
                if n == 0 and j == 0:
                    pe.wait_ge(ew_lo_done, e + 1)
                wait(pe, m_act, step - 1)
                for i in range(2):
                    for k in range(KD):
                        c = (i * KD + k) * D + j * P
                        tok = slice(n * GROUP, (n + 1) * GROUP)
                        mm = product(gu[1 - j][i], (ew_hi[:, b, c:c + P], ew_lo[:, b, c:c + P]),
                                     (h2T_hi[:, k, tok], h2T_lo[:, k, tok]), k == 0, k == KD - 1)
                mm.then_inc(m_full, 1)

            def down_e(e, b, n, j, last=False):
                pe.wait_ge(m_lo, e * 4 + (2 * n + j + 1))
                c = (2 * KD + j) * D
                for i in range(TPG):
                    tile = n * TPG + i
                    tok = slice(i * P, (i + 1) * P)
                    mm = product(wide[:, tile // 2, (tile % 2) * D:(tile % 2 + 1) * D], (mact_hi[:, j, tok], mact_lo[:, j, tok]),
                                 (ew_hi[:, b, c:c + D], ew_lo[:, b, c:c + D]), False, last)
                mm.then_inc(m_used, 1)

            def seed(tiles):
                for tile in tiles:
                    pe.matmul(wide[:, tile // 2, (tile % 2) * D:(tile % 2 + 1) * D], ident[:, :], resid[:, tile, :],
                              start=tile % 2 == 0, stop=False, skip_group_check=True)

            gate_up_e(0, 0, 0, 0)
            pe.wait_ge(logit_done, 1)
            pe.wait_ge(o_normed, SPT * NT)
            pe.wait_ge(x1_done, NT)
            seed(range(NT - 2))
            pe.wait_ge(route_step, 11)
            pe.transpose(wide[:, 3, 0:P], wtok[:, :, :].rearrange("p t e -> p (t e)"), ident[:, :]).then_inc(wT_full, 1)
            pe.wait_ge(wT_done, 1)
            seed(range(NT - 2, NT))

            STEPS = [(b, n, j) for b in range(2) for n in range(2) for j in range(2)]

            def experts(i, last=False):
                for s, (b, n, j) in enumerate(STEPS):
                    if s + 2 < len(STEPS):
                        b2, n2, j2 = STEPS[s + 2]
                        gate_up_e(i * 2 + b2, b2, n2, j2)
                    elif not last:
                        gate_up_e(i * 2 + 2, *STEPS[s + 2 - len(STEPS)])
                    down_e(i * 2 + b, b, n, j, last and b == 1)

            gate_up_e(0, *STEPS[1])
            experts(0)
            with pe.Fori(1, NE // 2 - 1) as i:
                experts(i)
            experts(NE // 2 - 1, last=True)
            pe.wait_ge(m_used, 4 * NE)
            pe.nop().then_inc(acc_full, 1)


_INPUTS = ["x", "seq_adapter", "cond_head", "cond_w", "qkv_w", "wo_w", "gate_w", "expert_w", "norms", "consts"]


def lay_out(inputs):
    def ktiles(w):
        return w.reshape(-1, P, w.shape[-1]).transpose(1, 0, 2)

    i = {k: np.asarray(v) for k, v in inputs.items()}

    def adapters(w):
        return w.transpose(1, 0, 2).reshape(w.shape[1], NAD * RANK)

    ag, au, ad = (ktiles(adapters(i["L0_cond_A" + c])) for c in "gud")
    bg, bu, bd = (i["L0_cond_B" + c].reshape(NAD * RANK, -1) for c in "gud")
    wg, wu, wd = (ktiles(i["L0_cond_W" + c]) for c in "gud")
    head = np.concatenate([ag.reshape(P, -1), au.reshape(P, -1), bd], 1)

    def hid(w):
        return w.reshape(P, KD, MH, P).transpose(0, 2, 1, 3).reshape(P, MH, KD * P)

    cond = np.concatenate([hid(wg), hid(wu), bg.reshape(P, MH, P), bu.reshape(P, MH, P), wd, ad], 2)
    q = ktiles(i["L0_ffn_wq"]).reshape(P, KD, KVP, 2, QPK, HD).transpose(0, 1, 2, 4, 3, 5).reshape(P, KD, KVP, GROUP)
    k, v = (ktiles(i["L0_ffn_w" + c])[:, :, None, :] for c in "kv")
    qkv = np.concatenate([k, q, v], 2).transpose(0, 2, 1, 3).reshape(P, QCHUNKS, KD * GROUP)
    wo = i["L0_ffn_wo"].reshape(KVP, 2, QPK, HD, D).transpose(1, 3, 0, 2, 4).reshape(P, KVP * QPK, D)
    gate = ktiles(i["L0_ffn_wg"]).reshape(P, KD * NE)
    ew = np.stack([i["L0_ffn_" + n].reshape(NE, KD, P, D) for n in ("w1", "w3", "w2")], 1)
    ew = ew.transpose(0, 3, 1, 2, 4).reshape(NE, P, ECOLS)
    norms = np.concatenate([i["L0_ffn_ln_w"].reshape(KD, P).T, i["L0_ffn_ff_ln_w"].reshape(KD, P).T], 1)
    half = HD // 2
    inv = (1.0 / np.float32(150000.0) ** (np.arange(half, dtype=np.float32) / np.float32(half))).astype(np.float32)
    ang = (np.arange(SEQ, dtype=np.float32)[:, None] * inv).astype(np.float32)
    cos, sin = np.cos(ang), np.sin(ang)
    rope = np.tile(np.concatenate([cos, cos, sin, -sin], 1), (SPT, 1))
    pos = np.arange(P) % SEQ
    mask = np.tile(np.where(np.arange(SEQ)[None, :] <= pos[:, None], 0.0, -1e30), (1, 2 * SPT)).astype(np.float32)
    consts = np.concatenate([rope, mask], 1).astype(np.float32)
    arrays = dict(x=i["x"], seq_adapter=i["itok_B_0_7"], cond_head=head, cond_w=cond, qkv_w=qkv, wo_w=wo,
                  gate_w=gate, expert_w=ew, norms=norms, consts=consts)
    return {k: np.ascontiguousarray(v) for k, v in arrays.items()}


def kernel(**inputs):
    import concourse.bacc as bacc
    from concourse.bass_utils import run_bass_kernel_spmd

    nc = bacc.Bacc("TRN2", target_bir_lowering=False, num_devices=1)
    laid = lay_out(inputs)
    args = [nc.dram_tensor(f"in_{n}", laid[n].shape, mybir.dt.from_np(laid[n].dtype), kind="ExternalInput").ap() for n in _INPUTS]
    out = nc.dram_tensor("out_0", inputs["x"].shape, F32, kind="ExternalOutput").ap()
    build(nc, *args, out)
    result = run_bass_kernel_spmd(nc, [{f"in_{n}": laid[n] for n in _INPUTS}], core_ids=[0])
    return result.results[0]["out_0"]
```

```python
from contextlib import ExitStack

import numpy as np

import concourse.bass as bass
from concourse import mybir

ALU = mybir.AluOpType
ACT = mybir.ActivationFunctionType
F32 = mybir.dt.float32
F32R = mybir.dt.float32r
I32 = mybir.dt.int32
U32 = mybir.dt.uint32
AX = mybir.AxisListType

P = 128
SEQ = 32
D = 256
KD = D // P
T = 1024
NT = T // P
SPT = P // SEQ
GROUP = 512
NG = T // GROUP
TPG = GROUP // P
X_STEP, XA_STEP, ROWS_STEP = 2, 4, 12
ROUTE = (0, NT - 2, NT)
ROUTE_STEPS = 10
HID = 1024
MH = HID // P
NAD = 8
RANK = 16
HEADS, KVH, HD = 32, 8, 64
QPK = HEADS // KVH
KVP = KVH // 2
HALF = KVH * SPT // 2
QKC = (HEADS + KVH) * HD // GROUP
NE, TOPK = 16, 4
EPS = 1e-5
SCALE = 1.0 / 8.0
WG, WU, BG, BU, WD, AD, MCOLS = 0, 256, 512, 640, 768, 1024, 1152
AG, AU, BD, HCOLS = 0, 256, 512, 768
QCHUNKS = (HEADS + 2 * KVH) * HD // GROUP
OCHUNKS = 4
OPARTS = KVP * QPK // 2
ECOLS = 3 * KD * D
EPARTS = (slice(0, 2 * KD * D), slice(2 * KD * D, ECOLS))
C_COS, C_SIN, C_MASK, C_LN, C_FF, C_EXP, C_EPS, CCOLS = 0, 64, 128, 384, 386, 388, 389, 390


def build(nc, x, seq_adapter, cond_head, cond_w, qkv_w, wo_w, gate_w, expert_w, norms, consts, out):
    with ExitStack() as ctx:
        cursor = [nc.sbuf_base + 31 & ~31]

        def sb(name, shape, dt=F32):
            size = 4 * int(np.prod(shape[1:]))
            t = nc.alloc_sbuf_tensor_at(name, shape, dt, offset=cursor[0])
            cursor[0] += size + 31 & ~31
            assert cursor[0] <= nc.sbuf_usable_end, (name, cursor[0], nc.sbuf_usable_end)
            return t

        def pair(name, shape):
            return sb(name + "_hi", shape, F32R), sb(name + "_lo", shape, F32R)

        def sem(name):
            return ctx.enter_context(nc.semaphore(name))

        def ps(name, shape):
            return ctx.enter_context(nc.psum_tensor(name, shape, F32))

        resid = sb("resid", [P, NT, D])
        ident = sb("ident", [P, P])
        cst = sb("cst", [P, CCOLS])
        staging = sb("staging", [P, 2, MCOLS])
        seq_ids = sb("seq_ids", [P, NT * SPT], I32)
        part_id = sb("part_id", [P, 1], I32)
        part_f = sb("part_f", [P, 1])
        row_off = sb("row_off", [P, NT * SPT])
        below = sb("below", [P, NT * SPT])
        amask = sb("amask", [P, NT * SPT])
        meansq1 = sb("meansq1", [P, NT])
        shifted1 = sb("shifted1", [P, NT])
        rstd1 = sb("rstd1", [P, NT])
        meansq2 = sb("meansq2", [P, 1])
        shifted2 = sb("shifted2", [P, 1])
        rstd2 = sb("rstd2", [P, 1])
        eidx = sb("eidx", [P, NE], I32)
        eidx_f = sb("eidx_f", [P, NE])
        wg_hi, wg_lo = pair("wgate", [P, KD, NE])
        qkv_at = cursor[0]
        qkvw_hi, qkvw_lo = pair("qkvw", [P, QCHUNKS, KD, GROUP])
        overlay = cursor[0]
        x_rows = sb("x_rows", [P, TPG, D])
        head_hi, head_lo = pair("head", [P, HCOLS])
        cw_hi, cw_lo = pair("cw", [P, MH, MCOLS])
        xT = [pair("xT0", [P, KD, GROUP]), None]
        xa_parts = [pair("xa0", [P, 2, GROUP]), None]
        xa = sb("xa", [P, 2, GROUP])
        xT[1] = pair("xT1", [P, KD, GROUP])
        xa_parts[1] = pair("xa1", [P, 2, GROUP])
        da_hi, da_lo = pair("da", [P, GROUP])
        silu_g = sb("silu_g", [P, 2, GROUP])
        act = sb("act", [P, 2, GROUP])
        act_hi, act_lo = pair("actp", [P, 2, GROUP])
        cursor[0] = overlay
        hrow = sb("hrow", [P, 2, D])
        hT_hi, hT_lo = pair("hT", [P, KD, P])
        wo_hi, wo_lo = pair("wo", [P, KVP * QPK, D])
        h2T_hi, h2T_lo = pair("h2T", [P, KD, T])
        kT_blk = sb("kT_blk", [P, KVP, SPT, 2, 2, SEQ], F32R)
        v_blk = sb("v_blk", [P, 2, KVH, SPT, HD], F32R)
        probs_at = cursor[0]
        pT_hi, pT_lo = pair("pT", [P, KVH, P])
        shared = cursor[0]
        cursor[0] = probs_at
        o_rows = sb("o_rows", [P, SPT, KVP, P])
        assert cursor[0] == shared
        qc = sb("qc", [P, 2, GROUP])
        qs = sb("qs", [P, 2, GROUP])
        qr = sb("qr", [P, QKC, GROUP])
        shared = cursor[0]
        qT_hi, qT_lo = pair("qT", [P, KVP, SPT, P])
        after = cursor[0]
        z = sb("z", [P, KVP, 2 * SPT, SEQ])
        cursor[0] = after
        v = sb("v", [P, 2, GROUP], F32R)
        zmax = sb("zmax", [P, KVH * SPT])
        zsum = sb("zsum", [P, KVH * SPT])
        zinv = sb("zinv", [P, KVP, 2, SPT])
        oT_hi, oT_lo = pair("oT", [P, KVP * QPK, P])
        end_of_attention = cursor[0]
        cursor[0] = qkv_at
        ew_hi, ew_lo = pair("ew", [P, 2, ECOLS])
        ew_raw = sb("ew_raw", [P, 2, ECOLS])
        wbc = sb("wbc", [P, 2, T])
        assert cursor[0] <= overlay, (cursor[0], overlay)
        cursor[0] = shared
        wtok = sb("wtok", [P, NT, NE])
        wT = sb("wT", [P, P])
        logit = sb("logit", [P, NT, NE])
        top8 = sb("top8", [P, NT, 8])
        topi = sb("topi", [P, NT, 8], U32)
        topi_f = sb("topi_f", [P, NT, TOPK])
        tope = sb("tope", [P, NT, TOPK])
        gsum = sb("gsum", [P, NT])
        ginv = sb("ginv", [P, NT])
        gate = sb("gate", [P, NT, TOPK])
        hit = sb("hit", [P, NT, TOPK, NE])
        x_fin = sb("x_fin", [P, NT, D])
        msilu = sb("msilu", [P, 2, GROUP])
        mgated = sb("mgated", [P, 2, GROUP])
        mact = sb("mact", [P, 2, GROUP])
        mact_hi, mact_lo = pair("mactp", [P, 2, GROUP])
        assert cursor[0] <= end_of_attention

        w_dram = nc.dram_tensor("moe_weights", (NE, NT, P), F32, kind="Internal").ap()

        ringA = ps("ringA", [P, 2, GROUP])
        ringT = ps("ringT", [P, 2, GROUP])
        wide = ps("wide", [P, 4, GROUP])
        gu = [(ringA[:, 0, :], ringA[:, 1, :]), (ringT[:, 0, :], ringT[:, 1, :])]

        x_in = sem("x_in")
        cst_in = sem("cst_in")
        ids_in = sem("ids_in")
        ident_zero, ident_done = sem("ident_zero"), sem("ident_done")
        powers_set = sem("powers_set")
        mask_step, mask_done = sem("mask_step"), sem("mask_done")
        raw_in = [sem(f"raw_in{i}") for i in range(2)]
        NCH = 1 + MH + QCHUNKS + OCHUNKS + 1
        hi_in = [sem(f"hi_in{i}") for i in range(NCH)]
        lo_done = sem("lo_done")
        pair_full = sem("pair_full")
        xT_full, xT_hi_done, xT_lo_done = sem("xT_full"), sem("xT_hi_done"), sem("xT_lo_done")
        xa_full, xa_masked = sem("xa_full"), sem("xa_masked")
        xa_hi_done, xa_lo_done = sem("xa_hi_done"), sem("xa_lo_done")
        da_masked, da_hi_done, da_lo_done = sem("da_masked"), sem("da_hi_done"), sem("da_lo_done")
        silu_done = sem("silu_done")
        act_done = sem("act_done")
        act_hi_done = sem("act_hi_done")
        act_lo_done = sem("act_lo_done")
        act_used = sem("act_used")
        c_full = sem("c_full")
        meansq1_done, shifted1_done, rstd1_done = sem("meansq1_done"), sem("shifted1_done"), sem("rstd1_done")

        h_ready = sem("h_ready")
        h2_ready = sem("h2_ready")
        kl_full = sem("kl_full")
        hT_hi_done, hT_lo_done = sem("hT_hi_done"), sem("hT_lo_done")
        h2T_hi_done, h2T_lo_done = sem("h2T_hi_done"), sem("h2T_lo_done")
        qk_full, qk_read, qk_roped = sem("qk_full"), sem("qk_read"), sem("qk_roped")
        kT_zero, blocks_zero, v_spread = sem("kT_zero"), sem("blocks_zero"), sem("v_spread")
        v_full, v_hi_done, v_lo_done = sem("v_full"), sem("v_hi_done"), sem("v_lo_done")
        qkT_full, qkT_hi_done, qkT_lo_done = sem("qkT_full"), sem("qkT_hi_done"), sem("qkT_lo_done")
        s_full, z_masked, zmax_done, z_shifted = sem("s_full"), sem("z_masked"), sem("zmax_done"), sem("z_shifted")
        prob_done, zsum_done, zinv_done = sem("prob_done"), sem("zsum_done"), sem("zinv_done")
        pT_full, pT_hi_done, pT_lo_done = sem("pT_full"), sem("pT_hi_done"), sem("pT_lo_done")
        o_full, o_normed = sem("o_full"), sem("o_normed")
        oT_full, oT_hi_done, oT_lo_done = sem("oT_full"), sem("oT_hi_done"), sem("oT_lo_done")
        y_full, x1_done = sem("y_full"), sem("x1_done")
        meansq2_done, shifted2_done, rstd2_done = sem("meansq2_done"), sem("shifted2_done"), sem("rstd2_done")

        logit_full, logit_done = sem("logit_full"), sem("logit_done")
        route_step, top_exp = sem("route_step"), sem("top_exp")
        eidx_done, eidx_f_done = sem("eidx_done"), sem("eidx_f_done")
        wT_full, wT_done, w_out = sem("wT_full"), sem("wT_done"), sem("w_out")
        w0_full, w0_done = sem("w0_full"), sem("w0_done")
        ew_raw_in = [sem(f"ew_raw_in{i}") for i in range(2)]
        ew_lo_done = sem("ew_lo_done")
        ew_hi_in = [[sem(f"ew_hi_in{i}_{part}") for part in range(2)] for i in range(2)]
        wbc_in = [sem(f"wbc_in{i}") for i in range(2)]
        x_again = sem("x_again")
        m_full, m_silu, m_gated, m_act = sem("m_full"), sem("m_silu"), sem("m_gated"), sem("m_act")
        m_hi, m_lo, m_used = sem("m_hi"), sem("m_lo"), sem("m_used")
        out_rows, out_done = sem("out_rows"), sem("out_done")

        x_dram = x.rearrange("b s d -> (b s) d").rearrange("(t p) d -> p t d", p=P)
        out_dram = out.rearrange("b s d -> (b s) d").rearrange("(t p) d -> p t d", p=P)

        chunks = [(cond_head, head_hi[:, :], head_lo[:, :])]
        chunks += [(cond_w[:, m, :], cw_hi[:, m, :], cw_lo[:, m, :]) for m in range(MH)]
        FIRST_QKV = len(chunks)
        chunks += [(qkv_w[:, c, :], qkvw_hi[:, c, :, :].rearrange("p k n -> p (k n)"),
                    qkvw_lo[:, c, :, :].rearrange("p k n -> p (k n)")) for c in range(QCHUNKS)]
        FIRST_WO = len(chunks)
        per = KVP * QPK // OCHUNKS
        chunks += [(wo_w[:, c * per:(c + 1) * per, :].rearrange("p k n -> p (k n)"),
                    wo_hi[:, c * per:(c + 1) * per, :].rearrange("p k n -> p (k n)"),
                    wo_lo[:, c * per:(c + 1) * per, :].rearrange("p k n -> p (k n)"))
                   for c in range(OCHUNKS)]
        chunks += [(gate_w, wg_hi[:, :, :].rearrange("p k n -> p (k n)"),
                    wg_lo[:, :, :].rearrange("p k n -> p (k n)"))]
        assert len(chunks) == NCH

        def wait(eng, semaphore, value):
            if isinstance(value, int) and value <= 0:
                return
            eng.wait_ge(semaphore, value)

        def xT_bank(g, k):
            return gu[0][k] if g == 0 else wide[:, 3, :]

        def xa_bank(g, i):
            return gu[1][i] if g == 0 else wide[:, 3, :]

        def attn_bank(t):
            return wide[:, 3, D:2 * D] if isinstance(t, int) and t == 0 else ringT[:, 1, D:2 * D]

        def kl_bank(moe):
            return wide[:, 3 - (moe - (NT - 2)), :] if isinstance(moe, int) and moe >= NT - 2 else ringT[:, 1, :]

        def logit_bank(t):
            return ringA[:, 1, :] if t < ROUTE[1] else wide[:, 2, D:2 * D]

        def turned(c, part, qT):
            if c > 0:
                return [(qT[:, c - 1, :, :].rearrange("p s (g q) -> p g s q", g=QPK),
                         ringT[:, c % 2, :].rearrange("p (g s q) -> p g s q", g=QPK, s=SPT))]
            bank = ringT[:, 0, :].rearrange("p (a s k) -> p a s k", a=KVP, s=SPT)
            rows = [slice(j * HD, (j + 1) * HD) for j in range(2)]
            return [(kT_blk[row, :, :, part, j, :], bank[row, :, :, :]) for j, row in enumerate(rows)]

        def o_turned(a, oT):
            return (oT[:, a * QPK:(a + 1) * QPK, :].rearrange("p g (s q) -> p g s q", s=SPT),
                    ringT[:, a % 2, :].rearrange("p (s g q) -> p g s q", s=SPT, g=QPK))

        def lo_part(lo, full, hi):
            return dict(out=lo, in0=full, in1=hi.bitcast(F32), op=ALU.subtract)

        block = ctx.enter_context(nc.Block())

        @block.sync
        def _(sp):
            def raw(n, src, cols):
                wait(sp, lo_done, n - 1)
                sp.dma_start(staging[:, n % 2, 0:cols], src).then_inc(raw_in[n % 2], 16)

            sp.dma_start(x_rows[:, :, :], x_dram[:, 0:TPG, :]).then_inc(x_in, 16)
            raw(0, chunks[0][0], chunks[0][1].shape[-1])
            raw(1, chunks[1][0], chunks[1][1].shape[-1])
            sp.dma_start(seq_ids[:, :], seq_adapter.partition_broadcast(P)).then_inc(ids_in, 16)
            sp.dma_start(cst[:, 0:C_LN], consts).then_inc(cst_in, 16)
            sp.dma_start(cst[:, C_LN:C_EXP], norms).then_inc(cst_in, 16)
            for n in range(2, FIRST_WO + 2):
                raw(n, chunks[n][0], chunks[n][1].shape[-1])
                if n == 3:
                    sp.wait_ge(xT_full, KD)
                    sp.dma_start(x_rows[:, :, :], x_dram[:, TPG:NT, :]).then_inc(x_in, 16)

            def spread_v(t):
                sp.wait_ge(v_lo_done, t + 1)
                wait(sp, o_full, t)
                for q in range(SPT):
                    row = slice(q * SEQ, (q + 1) * SEQ)
                    sp.dma_start(v_blk[row, :, :, q, :].rearrange("p x h d -> p (x h) d").bitcast(F32),
                                 v[row, :, :].bitcast(F32).rearrange("p x (h d) -> p (x h) d", d=HD)).then_inc(v_spread, 16)

            sp.wait_ge(blocks_zero, 2)
            spread_v(0)
            spread_v(1)
            for n in range(FIRST_WO + 2, NCH):
                raw(n, chunks[n][0], chunks[n][1].shape[-1])
            with sp.Fori(2, NT) as t:
                spread_v(t)

            sp.wait_ge(v_full, NT)
            for b in range(2):
                sp.dma_start(ew_raw[:, b, :], expert_w[b, :, :]).then_inc(ew_raw_in[b], 16)
            sp.wait_ge(wT_done, 1)
            sp.dma_start(w_dram.rearrange("e t p -> t e p"), wT[:, :]).then_inc(w_out, 16)
            sp.wait_ge(w_out, 16)
            sp.dma_start(wbc[:, 1, :], w_dram[1, :, :].rearrange("t p -> (t p)").partition_broadcast(P)).then_inc(wbc_in[1], 16)
            sp.dma_start(x_fin[:, :, :], x_dram).then_inc(x_again, 16)
            with sp.Fori(1, NE // 2) as i:
                for b in range(2):
                    e = i * 2 + b
                    sp.wait_ge(ew_lo_done, 2 * (e - 1))
                    sp.dma_start(ew_raw[:, b, :], expert_w[bass.ds(e, 1), :, :].rearrange("o p n -> (o p) n")
                                 ).then_inc(ew_raw_in[b], 16)
                    sp.wait_ge(m_gated, (e - 1) * 4)
                    sp.dma_start(wbc[:, b, :], w_dram[bass.ds(e, 1), :, :].rearrange("o t p -> (o t p)").partition_broadcast(P)
                                 ).then_inc(wbc_in[b], 16)
            for h in range(4):
                sp.wait_ge(out_rows, h + 1)
                sp.dma_start(out_dram[:, 2 * h:2 * h + 2, :], resid[:, 2 * h:2 * h + 2, :]).then_inc(out_done, 16)
            sp.wait_ge(out_done, 16 * 4)

        @block.gpsimd
        def _(pool):
            def load_hi(n):
                pool.dma_start(chunks[n][1], chunks[n][0]).then_inc(hi_in[n], 16)

            for n in range(4):
                load_hi(n)
                if n == 0:
                    pool.memset(ident[:, :], 0.0).then_inc(ident_zero, 1)
                    pool.iota(eidx[:, :], pattern=[[1, NE]], base=0, channel_multiplier=0).then_inc(eidx_done, 1)
                    pool.iota(part_id[:, :], pattern=[[0, 1]], base=0, channel_multiplier=1).then_inc(mask_step, 1)
                    pool.memset(cst[:, C_EXP:C_EXP + 1], -0.5).then_inc(powers_set, 1)
                    pool.memset(cst[:, C_EPS:C_EPS + 1], EPS).then_inc(powers_set, 1)
                    pool.wait_ge(ident_zero, 1)
                    pool.affine_select(out=ident[:, :], in_=ident[:, :], compare_op=ALU.not_equal, fill=1.0,
                                       base=0, pattern=[[-1, P]], channel_multiplier=1).then_inc(ident_done, 1)

            def split(n):
                _src, hi, lo = chunks[n]
                pool.wait_ge(raw_in[n % 2], 16 * (n // 2 + 1))
                pool.wait_ge(hi_in[n], 16)
                pool.wait_ge(lo_done, n)
                pool.tensor_tensor(**lo_part(lo, staging[:, n % 2, 0:hi.shape[-1]], hi)).then_inc(lo_done, 1)

            for n in range(2, FIRST_WO):
                split(n)
                if n + 2 < FIRST_WO:
                    load_hi(n + 2)
            load_hi(NCH - 1)

            def row_scales(g):
                cols = slice(g * TPG, (g + 1) * TPG)
                pool.wait_ge(meansq1_done, TPG * (g + 1))
                pool.tensor_scalar(shifted1[:, cols], meansq1[:, cols], EPS, None, ALU.add).then_inc(shifted1_done, 1)
                pool.wait_ge(shifted1_done, g + 1)
                pool.tensor_tensor(rstd1[:, cols], shifted1[:, cols],
                                   cst[:, C_EXP:C_EXP + 1].broadcast_to([P, TPG]), ALU.pow).then_inc(rstd1_done, 1)

            pool.wait_ge(powers_set, 2)
            row_scales(0)
            pool.wait_ge(rstd1_done, 1)

            def attention_rows(t):
                wait(pool, kl_full, t)
                pool.tensor_tensor(hrow[:, 1, :], resid[:, t, :], rstd1[:, bass.ds(t, 1)].broadcast_to([P, D]),
                                   ALU.mult).then_inc(h_ready, 1)

            def rope_add(t, c):
                pool.wait_ge(qk_read, QKC * t + c + 1)
                wait(pool, qkT_full, QKC * t)
                cos = qc[:, c % 2, :].rearrange("p (h f d) -> p h f d", f=2, d=HD // 2)
                sin = qs[:, c % 2, :].rearrange("p (h f d) -> p h f d", f=2, d=HD // 2)
                rot = qr[:, c, :].rearrange("p (h f d) -> p h f d", f=2, d=HD // 2)
                for f in range(2):
                    last = pool.tensor_tensor(rot[:, :, f, :], cos[:, :, f, :], sin[:, :, 1 - f, :], ALU.add)
                last.then_inc(qk_roped, 1)

            def shift(t, half):
                pool.wait_ge(zmax_done, 2 * t + half + 1)
                zv = z[:, half * 2:half * 2 + 2, :, :].rearrange("p a n k -> p (a n) k")
                pool.tensor_tensor(zv, zv, zmax[:, half * HALF:(half + 1) * HALF].unsqueeze(2).broadcast_to([P, HALF, SEQ]),
                                   ALU.subtract).then_inc(z_shifted, 1)

            def moe_rows(t):
                pool.wait_ge(meansq2_done, t + 1)
                pool.tensor_tensor(shifted2[:, :], meansq2[:, :], cst[:, C_EPS:C_EPS + 1], ALU.add).then_inc(shifted2_done, 1)
                pool.wait_ge(shifted2_done, t + 1)
                pool.tensor_tensor(rstd2[:, :], shifted2[:, :], cst[:, C_EXP:C_EXP + 1], ALU.pow).then_inc(rstd2_done, 1)
                pool.wait_ge(rstd2_done, t + 1)
                if not (isinstance(t, int) and t == 0):
                    pool.wait_ge(kl_full, t + 4)
                pool.tensor_tensor(hrow[:, 0, :], resid[:, t, :], rstd2[:, 0:1].broadcast_to([P, D]),
                                   ALU.mult).then_inc(h2_ready, 1)

            attention_rows(0)
            attention_rows(1)
            pool.wait_ge(act_used, MH * NG - 4)
            pool.memset(kT_blk[:, :, :, :, :, :].rearrange("p a s x j k -> p (a s x j k)").bitcast(F32), 0.0).then_inc(kT_zero, 1)
            pool.wait_ge(act_used, MH * NG - 1)
            pool.memset(v_blk[:, 1, :, :, :].rearrange("p h s d -> p (h s d)").bitcast(F32), 0.0).then_inc(blocks_zero, 1)
            rope_add(0, 0)
            rope_add(0, 1)
            rope_add(0, 2)
            row_scales(1)
            rope_add(0, 3)
            rope_add(0, 4)
            pool.wait_ge(rstd1_done, NG)

            def attend(t, moe=True, rows=True, attn=True, wo=False):
                if rows:
                    attention_rows(t + 2)
                if moe:
                    moe_rows(t - 2)
                for half in range(2):
                    shift(t, half)
                if attn:
                    for c in range(QKC):
                        rope_add(t + 1, c)
                        if wo and c < OCHUNKS:
                            load_hi(FIRST_WO + c)

            attend(0, moe=False, wo=True)
            for n in range(FIRST_WO, NCH):
                split(n)
            attend(1, moe=False)
            attend(2)
            with pool.Fori(3, NT - 2) as t:
                attend(t)
            attend(NT - 2, rows=False)
            attend(NT - 1, rows=False, attn=False)

            def expert_load(part, e, b, first=False):
                if not first:
                    pool.wait_ge(*((m_full, 4 * (e - 1)) if part == 0 else (m_used, 4 * (e - 1))))
                cols = EPARTS[part]
                pool.dma_start(ew_hi[:, b, cols], expert_w[bass.ds(e, 1), :, cols].rearrange("o p n -> (o p) n")
                               ).then_inc(ew_hi_in[b][part], 16)

            def expert_lo(part, b, i):
                cols = EPARTS[part]
                pool.wait_ge(ew_hi_in[b][part], 16 * (i + 1))
                pool.wait_ge(ew_raw_in[b], 16 * (i + 1))
                pool.tensor_tensor(**lo_part(ew_lo[:, b, cols], ew_raw[:, b, cols], ew_hi[:, b, cols])).then_inc(ew_lo_done, 1)

            def experts(i, first=False, last=False):
                for b in range(2):
                    e = i * 2 + b
                    if not (last and b == 1) and not (first and b == 0):
                        for part in range(2):
                            expert_load(part, e + 1, 1 - b)
                            expert_lo(part, 1 - b, i + b)

            pool.wait_ge(v_full, NT)
            for b in range(2):
                for part in range(2):
                    expert_load(part, b, b, True)
            for b in range(2):
                for part in range(2):
                    expert_lo(part, b, 0)
            moe_rows(NT - 2)
            moe_rows(NT - 1)
            experts(0, first=True)
            with pool.Fori(1, NE // 2 - 1) as i:
                experts(i)
            experts(NE // 2 - 1, last=True)

        @block.scalar
        def _(act_e):
            def copy(out, in_, scale=None):
                if scale is None:
                    return act_e.activation(out, in_, ACT.Copy)
                return act_e.activation(out, in_, ACT.Copy, scale=scale)

            def x_hi(g, k):
                act_e.wait_ge(xT_full, KD * g + k + 1)
                copy(xT[g][0][:, k, :], xT_bank(g, k)).then_inc(xT_hi_done, 1)

            def xa_hi(g, i):
                act_e.wait_ge(xa_masked, 2 * g + i + 1)
                copy(xa_parts[g][0][:, i, :], xa[:, i, :]).then_inc(xa_hi_done, 1)

            def down_a_hi(g):
                act_e.wait_ge(da_masked, g + 1)
                copy(da_hi[:, :], xa[:, 1, :]).then_inc(da_hi_done, 1)

            def hidden(s):
                act_e.wait_ge(pair_full, s + 1)
                wait(act_e, act_done, s - 1)
                act_e.activation(silu_g[:, s % 2, :], gu[s % 2][0], ACT.Silu).then_inc(silu_done, 1)
                act_e.wait_ge(act_done, s + 1)
                wait(act_e, act_used, s - 1)
                copy(act_hi[:, s % 2, :], act[:, s % 2, :]).then_inc(act_hi_done, 1)

            def rows_out(g):
                act_e.wait_ge(c_full, g + 1)
                for i in range(TPG):
                    rows = wide[:, i // 2, (i % 2) * D:(i % 2 + 1) * D]
                    copy(resid[:, g * TPG + i, :], rows)
                    wait(act_e, meansq1_done, g * TPG + i)
                    act_e.activation(xa[:, 1, 0:D], rows, ACT.Square, scale=D ** -0.5,
                                     accum_out=meansq1[:, g * TPG + i:g * TPG + i + 1]).then_inc(meansq1_done, 1)

            def kl_hi(moe, attn):
                if moe is not None:
                    for k in range(KD):
                        last = copy(h2T_hi[:, k, bass.ds(moe * P, P)], kl_bank(moe)[:, k * P:(k + 1) * P],
                                    cst[:, C_FF + k:C_FF + k + 1])
                    last.then_inc(h2T_hi_done, 1)
                if attn is not None:
                    for k in range(KD):
                        last = copy(hT_hi[:, k, :], attn_bank(attn)[:, k * P:(k + 1) * P],
                                    cst[:, C_LN + k:C_LN + k + 1])
                    last.then_inc(hT_hi_done, 1)

            def v_part(t):
                act_e.wait_ge(v_full, t + 1)
                wait(act_e, zsum_done, t)
                wait(act_e, v_spread, 16 * SPT * t)
                copy(v[:, 0, :], ringA[:, 1, :]).then_inc(v_hi_done, 1)

            def residual_square(t):
                act_e.wait_ge(x1_done, t + 1)
                wait(act_e, shifted2_done, t)
                act_e.wait_ge(meansq1_done, NT) if isinstance(t, int) and t == 0 else wait(act_e, meansq2_done, t)
                act_e.activation(hrow[:, 0, :], resid[:, t, :], ACT.Square, scale=D ** -0.5,
                                 accum_out=meansq2[:, :]).then_inc(meansq2_done, 1)

            def turned_hi(t, chunks_):
                for c in chunks_:
                    act_e.wait_ge(qkT_full, QKC * t + c + 1)
                    for dst, src in turned(c, 0, qT_hi):
                        last = copy(dst, src)
                    last.then_inc(qkT_hi_done, 1)

            def outputs_hi(t, a):
                act_e.wait_ge(oT_full, KVP * t + a + 1)
                copy(*o_turned(a, oT_hi)).then_inc(oT_hi_done, 1)

            def exponentials(t):
                for half in range(2):
                    act_e.wait_ge(z_shifted, 2 * t + half + 1)
                    zv = z[:, half * 2:half * 2 + 2, :, :].rearrange("p a n k -> p (a n k)")
                    act_e.activation(zv, zv, ACT.Exp).then_inc(prob_done, 1)

            def probs_hi(t, j):
                act_e.wait_ge(pT_full, 2 * t + j + 1)
                copy(pT_hi[:, j * 4:(j + 1) * 4, :].rearrange("p a n -> p (a n)"), ringT[:, j, :]).then_inc(pT_hi_done, 1)

            def attend(t, before=True, moe=True, rows=True):
                if moe:
                    residual_square(t - 2)
                if before:
                    for a in range(1, KVP):
                        outputs_hi(t - 1, a)
                exponentials(t)
                for j in range(2):
                    probs_hi(t, j)
                first_turned = 1 if before else 3
                turned_hi(t + 1, range(first_turned))
                v_part(t + 1)
                turned_hi(t + 1, range(first_turned, QKC))
                if rows or moe:
                    act_e.wait_ge(kl_full, t + 3)
                    kl_hi(t - 2 if moe else None, t + 2 if rows else None)
                outputs_hi(t, 0)

            for k in range(KD):
                x_hi(0, k)
            for i in range(2):
                xa_hi(0, i)
            for s in range(MH * NG):
                hidden(s)
                if X_STEP <= s < X_STEP + KD:
                    x_hi(1, s - X_STEP)
                elif XA_STEP <= s < XA_STEP + 2:
                    xa_hi(1, s - XA_STEP)
                elif s % MH == 0 and s > 0:
                    down_a_hi(s // MH - 1)
                elif s == MH + 1:
                    rows_out(0)
                elif s == ROWS_STEP:
                    act_e.wait_ge(cst_in, 32)
                    act_e.wait_ge(kl_full, 1)
                    kl_hi(None, 0)
            down_a_hi(1)
            rows_out(1)
            act_e.wait_ge(meansq1_done, NT)
            act_e.wait_ge(kT_zero, 1)
            v_part(0)
            turned_hi(0, range(QKC))
            act_e.wait_ge(kl_full, 2)
            kl_hi(None, 1)
            attend(0, before=False, moe=False)
            attend(1, moe=False)
            attend(2)
            with act_e.Fori(3, NT - 2) as t:
                attend(t)
            attend(NT - 2, rows=False)
            def route_exp(g):
                ts = slice(ROUTE[g], ROUTE[g + 1])
                act_e.wait_ge(route_step, ROUTE_STEPS * g + 2)
                act_e.activation(tope[:, ts, :].rearrange("p t k -> p (t k)"), gate[:, ts, :].rearrange("p t k -> p (t k)"),
                                 ACT.Exp).then_inc(top_exp, 1)

            def silu(step, s):
                act_e.wait_ge(m_full, step + 1)
                wait(act_e, m_gated, step - 1)
                act_e.activation(msilu[:, s % 2, :], gu[1 - s % 2][0], ACT.Silu).then_inc(m_silu, 1)

            t = NT - 1
            residual_square(t - 2)
            for a in range(1, KVP):
                outputs_hi(t - 1, a)
            exponentials(t)
            for j in range(2):
                probs_hi(t, j)
            act_e.wait_ge(kl_full, NT + 2)
            kl_hi(t - 2, None)
            for a in range(KVP):
                outputs_hi(t, a)
            residual_square(t - 1)
            route_exp(0)
            act_e.wait_ge(kl_full, NT + 3)
            kl_hi(t - 1, None)
            residual_square(t)
            act_e.wait_ge(kl_full, NT + 4)
            kl_hi(t, None)
            route_exp(1)
            silu(0, 0)
            act_e.wait_ge(wT_full, 1)
            copy(wT[:, :], wide[:, 3, 0:P]).then_inc(wT_done, 1)
            for n in range(2):
                act_e.wait_ge(w0_full, n + 1)
                copy(wbc[:, 0, n * GROUP:(n + 1) * GROUP], wide[:, 2 + n, :]).then_inc(w0_done, 1)

            def experts(i):
                for b in range(2):
                    for s in range(4):
                        step = i * 8 + (4 * b + s)
                        if not (isinstance(step, int) and step == 0):
                            silu(step, s)
                        act_e.wait_ge(m_act, step + 1)
                        wait(act_e, m_used, step - 1)
                        copy(mact_hi[:, s % 2, :], mact[:, s % 2, :]).then_inc(m_hi, 1)

            experts(0)
            with act_e.Fori(1, NE // 2) as i:
                experts(i)

        @block.vector
        def _(dve):
            def first_split(n):
                _src, hi, lo = chunks[n]
                dve.wait_ge(raw_in[n], 16)
                dve.wait_ge(hi_in[n], 16)
                dve.tensor_tensor(**lo_part(lo, staging[:, n, 0:hi.shape[-1]], hi)).then_inc(lo_done, 1)

            def x_low(g, k):
                dve.wait_ge(xT_hi_done, KD * g + k + 1)
                dve.tensor_tensor(**lo_part(xT[g][1][:, k, :], xT_bank(g, k), xT[g][0][:, k, :])).then_inc(xT_lo_done, 1)

            x_low(0, 0)
            first_split(0)
            x_low(0, 1)
            dve.wait_ge(ids_in, 16)
            dve.wait_ge(mask_step, 1)
            dve.tensor_copy(part_f[:, :], part_id[:, :]).then_inc(mask_done, 1)
            dve.wait_ge(mask_done, 1)
            dve.tensor_scalar(row_off[:, :], seq_ids[:, :], -float(RANK), part_f[:, 0:1], ALU.mult, ALU.add).then_inc(mask_done, 1)
            dve.wait_ge(mask_done, 2)
            dve.tensor_scalar(below[:, :], row_off[:, :], RANK - 0.5, None, ALU.is_le).then_inc(mask_done, 1)
            dve.wait_ge(mask_done, 3)
            dve.scalar_tensor_tensor(out=amask[:, :], in0=row_off[:, :], scalar=0.0, in1=below[:, :],
                                     op0=ALU.is_ge, op1=ALU.mult).then_inc(mask_done, 1)
            dve.wait_ge(mask_done, 4)

            dve.wait_ge(eidx_done, 1)
            dve.tensor_copy(eidx_f[:, :], eidx[:, :]).then_inc(eidx_f_done, 1)
            first_split(1)

            def masked(dst, g, src):
                picked = amask[:, g * TPG * SPT:(g + 1) * TPG * SPT].unsqueeze(2).broadcast_to([P, TPG * SPT, SEQ])
                return dve.tensor_tensor(dst.rearrange("p (s n) -> p s n", n=SEQ), src.rearrange("p (s n) -> p s n", n=SEQ),
                                         picked, ALU.mult)

            def xa_mask(g, i):
                dve.wait_ge(xa_full, 2 * g + i + 1)
                masked(xa[:, i, :], g, xa_bank(g, i)).then_inc(xa_masked, 1)

            def xa_low(g, i):
                dve.wait_ge(xa_hi_done, 2 * g + i + 1)
                dve.tensor_tensor(**lo_part(xa_parts[g][1][:, i, :], xa[:, i, :], xa_parts[g][0][:, i, :])).then_inc(xa_lo_done, 1)

            def down_a(g):
                dve.wait_ge(act_used, MH * (g + 1))
                wait(dve, meansq1_done, TPG * g)
                masked(xa[:, 1, :], g, wide[:, 2, :]).then_inc(da_masked, 1)
                dve.wait_ge(da_hi_done, g + 1)
                dve.tensor_tensor(**lo_part(da_lo[:, :], xa[:, 1, :], da_hi[:, :])).then_inc(da_lo_done, 1)

            def hidden(s):
                dve.wait_ge(silu_done, s + 1)
                dve.tensor_tensor(act[:, s % 2, :], silu_g[:, s % 2, :], gu[s % 2][1], ALU.mult).then_inc(act_done, 1)
                dve.wait_ge(act_hi_done, s + 1)
                dve.tensor_tensor(**lo_part(act_lo[:, s % 2, :], act[:, s % 2, :], act_hi[:, s % 2, :])).then_inc(act_lo_done, 1)

            def kl_lo(moe, attn):
                if moe is not None:
                    for k in range(KD):
                        last = dve.scalar_tensor_tensor(
                            out=h2T_lo[:, k, bass.ds(moe * P, P)], in0=kl_bank(moe)[:, k * P:(k + 1) * P],
                            scalar=cst[:, C_FF + k:C_FF + k + 1], in1=h2T_hi[:, k, bass.ds(moe * P, P)].bitcast(F32),
                            op0=ALU.mult, op1=ALU.subtract)
                    last.then_inc(h2T_lo_done, 1)
                if attn is not None:
                    for k in range(KD):
                        last = dve.scalar_tensor_tensor(
                            out=hT_lo[:, k, :], in0=attn_bank(attn)[:, k * P:(k + 1) * P],
                            scalar=cst[:, C_LN + k:C_LN + k + 1], in1=hT_hi[:, k, :].bitcast(F32),
                            op0=ALU.mult, op1=ALU.subtract)
                    last.then_inc(hT_lo_done, 1)

            def rope_products(t, c):
                dve.wait_ge(qk_full, QKC * t + c + 1)
                wait(dve, qk_roped, QKC * t + c - 1)
                heads = GROUP // HD
                src = ringA[:, c % 2, :].rearrange("p (h d) -> p h d", d=HD)
                for dst, col in ((qc, C_COS), (qs, C_SIN)):
                    table = cst[:, col:col + HD].unsqueeze(1).broadcast_to([P, heads, HD])
                    last = dve.tensor_tensor(dst[:, c % 2, :].rearrange("p (h d) -> p h d", d=HD), src, table, ALU.mult)
                last.then_inc(qk_read, 1)

            def residual(t):
                dve.wait_ge(y_full, t + 1)
                dve.tensor_tensor(resid[:, t, :], ringA[:, 0, 0:D], resid[:, t, :], ALU.add).then_inc(x1_done, 1)

            def v_low(t):
                dve.wait_ge(v_hi_done, t + 1)
                dve.tensor_tensor(**lo_part(v[:, 1, :], ringA[:, 1, :], v[:, 0, :])).then_inc(v_lo_done, 1)

            def turned_low(t, c):
                dve.wait_ge(qkT_hi_done, QKC * t + c + 1)
                for (hi, src), (lo, _src) in zip(turned(c, 0, qT_hi), turned(c, 1, qT_lo)):
                    last = dve.tensor_tensor(**lo_part(lo, src, hi))
                last.then_inc(qkT_lo_done, 1)

            def rows_low(moe, attn):
                if moe is not None:
                    dve.wait_ge(h2T_hi_done, moe + 1)
                if attn is not None:
                    dve.wait_ge(hT_hi_done, attn + 1)
                kl_lo(moe, attn)

            for i in range(2):
                xa_mask(0, i)
            for i in range(2):
                xa_low(0, i)
            for s in range(MH * NG):
                hidden(s)
                if X_STEP <= s < X_STEP + KD:
                    x_low(1, s - X_STEP)
                elif XA_STEP <= s < XA_STEP + 2:
                    xa_mask(1, s - XA_STEP)
                    xa_low(1, s - XA_STEP)
                elif s % MH == 0 and s > 0:
                    down_a(s // MH - 1)
                elif s == ROWS_STEP:
                    dve.wait_ge(cst_in, 32)
                    dve.wait_ge(hT_hi_done, 1)
                    kl_lo(None, 0)
                elif s == MH * NG - 2:
                    dve.wait_ge(act_used, s - 1)
                    dve.memset(v_blk[:, 0, :, :, :].rearrange("p h s d -> p (h s d)").bitcast(F32), 0.0).then_inc(blocks_zero, 1)
            rope_products(0, 0)
            down_a(1)
            rope_products(0, 1)
            rope_products(0, 2)
            v_low(0)
            for c in range(3, QKC):
                turned_low(0, c - 3)
                rope_products(0, c)
            for c in range(2, QKC):
                turned_low(0, c)
            rows_low(None, 1)

            def outputs_low(t, a):
                dve.wait_ge(oT_hi_done, KVP * t + a + 1)
                dve.tensor_tensor(**lo_part(o_turned(a, oT_lo)[0], o_turned(a, oT_hi)[1], o_turned(a, oT_hi)[0])
                                  ).then_inc(oT_lo_done, 1)

            def probs_low(t, j):
                dve.wait_ge(pT_hi_done, 2 * t + j + 1)
                half = slice(j * 4, (j + 1) * 4)
                dve.tensor_tensor(**lo_part(pT_lo[:, half, :].rearrange("p a n -> p (a n)"), ringT[:, j, :],
                                            pT_hi[:, half, :].rearrange("p a n -> p (a n)"))).then_inc(pT_lo_done, 1)

            def mask_scores(t, half):
                dve.wait_ge(s_full, 2 * t + half + 1)
                dve.wait_ge(v_spread, 16 * SPT * (t + 1))
                pairs = slice(half * 2, half * 2 + 2)
                mask = cst[:, C_MASK:C_MASK + 2 * P].unsqueeze(1).broadcast_to([P, 2, 2 * P])
                zv = z[:, pairs, :, :].rearrange("p a n k -> p a (n k)")
                for part, more in ((0, mask), (1, zv)):
                    if part:
                        dve.wait_ge(z_masked, 4 * t + (2 * half + 1))
                    src = wide[:, pairs, part * 2 * P:(part + 1) * 2 * P]
                    dve.scalar_tensor_tensor(out=zv, in0=src, scalar=SCALE, in1=more,
                                             op0=ALU.mult, op1=ALU.add).then_inc(z_masked, 1)
                dve.wait_ge(z_masked, 4 * t + (2 * half + 2))
                dve.tensor_reduce(zmax[:, half * HALF:(half + 1) * HALF], z[:, pairs, :, :].rearrange("p a n k -> p (a n) k"),
                                  AX.X, ALU.max).then_inc(zmax_done, 1)

            def sums(t):
                dve.wait_ge(prob_done, 2 * t + 2)
                dve.tensor_reduce(zsum[:, :], z[:, :, :, :].rearrange("p a n k -> p (a n) k"), AX.X, ALU.add).then_inc(zsum_done, 1)
                dve.wait_ge(zsum_done, t + 1)
                dve.reciprocal(zinv[:, :, :, :].rearrange("p a j s -> p (a j s)"), zsum[:, :]).then_inc(zinv_done, 1)

            def norm(t, pairs):
                dve.wait_ge(o_full, t + 1)
                dve.wait_ge(zinv_done, t + 1)
                for a in pairs:
                    inv = zinv[:, a, :, :].unsqueeze(3).broadcast_to([P, 2, SPT, HD])
                    dve.tensor_tensor(o_rows[:, :, a, :].rearrange("p s (j d) -> p j s d", j=2),
                                      wide[:, a, :].rearrange("p (j s d) -> p j s d", j=2, s=SPT), inv, ALU.mult).then_inc(o_normed, 1)

            def attend(t, before=True, moe=True, rows=True):
                mask_scores(t, 0)
                if before:
                    outputs_low(t - 1, 1)
                mask_scores(t, 1)
                rope_products(t + 1, 0)
                if before:
                    outputs_low(t - 1, 2)
                    outputs_low(t - 1, 3)
                rope_products(t + 1, 1)
                probs_low(t, 0)
                probs_low(t, 1)
                rope_products(t + 1, 2)
                rope_products(t + 1, 3)
                sums(t)
                rope_products(t + 1, 4)
                turned_low(t + 1, 0)
                norm(t, (0,))
                turned_low(t + 1, 1)
                norm(t, (1,))
                turned_low(t + 1, 2)
                v_low(t + 1)
                norm(t, (2,))
                turned_low(t + 1, 3)
                norm(t, (3,))
                turned_low(t + 1, 4)
                if rows or moe:
                    rows_low(t - 2 if moe else None, t + 2 if rows else None)
                outputs_low(t, 0)
                if before:
                    residual(t - 1)

            attend(0, before=False, moe=False)
            attend(1, moe=False)
            attend(2)
            with dve.Fori(3, NT - 2) as t:
                attend(t)
            attend(NT - 2, rows=False)
            def route(g):
                ts, n = slice(ROUTE[g], ROUTE[g + 1]), ROUTE[g + 1] - ROUTE[g]
                done = ROUTE_STEPS * g
                dve.wait_ge(logit_full, g + 1)
                dve.tensor_copy(logit[:, ts, :].rearrange("p t e -> p (t e)"), logit_bank(ROUTE[g])[:, ROUTE[g] * NE:ROUTE[g + 1] * NE]
                                ).then_inc(logit_done, 1)
                dve.wait_ge(logit_done, g + 1)
                for t in range(ROUTE[g], ROUTE[g + 1]):
                    last = dve.max(top8[:, t, :], logit[:, t, :])
                last.then_inc(route_step, 1)
                dve.wait_ge(route_step, done + 1)
                dve.tensor_tensor(gate[:, ts, :], top8[:, ts, 0:TOPK], top8[:, ts, 0:1].broadcast_to([P, n, TOPK]),
                                  ALU.subtract).then_inc(route_step, 1)
                for t in range(ROUTE[g], ROUTE[g + 1]):
                    last = dve.max_index(topi[:, t, :], top8[:, t, :], logit[:, t, :])
                last.then_inc(route_step, 1)
                dve.wait_ge(route_step, done + 3)
                dve.tensor_copy(topi_f[:, ts, :], topi[:, ts, 0:TOPK]).then_inc(route_step, 1)
                dve.wait_ge(route_step, done + 4)
                hits = hit[:, ts, :, :].rearrange("p t k e -> p (t k) e")
                dve.tensor_tensor(hits, topi_f[:, ts, :].rearrange("p t k -> p (t k)").unsqueeze(2).broadcast_to([P, n * TOPK, NE]),
                                  eidx_f[:, :].unsqueeze(1).broadcast_to([P, n * TOPK, NE]), ALU.is_equal).then_inc(route_step, 1)
                dve.wait_ge(top_exp, g + 1)
                dve.tensor_reduce(gsum[:, ts], tope[:, ts, :], AX.X, ALU.add).then_inc(route_step, 1)
                dve.wait_ge(route_step, done + 6)
                dve.reciprocal(ginv[:, ts], gsum[:, ts]).then_inc(route_step, 1)
                dve.wait_ge(route_step, done + 7)
                dve.tensor_tensor(gate[:, ts, :], tope[:, ts, :], ginv[:, ts].unsqueeze(2).broadcast_to([P, n, TOPK]),
                                  ALU.mult).then_inc(route_step, 1)
                dve.wait_ge(route_step, done + 8)
                dve.tensor_tensor(hits, hits, gate[:, ts, :].rearrange("p t k -> p (t k)").unsqueeze(2).broadcast_to(
                    [P, n * TOPK, NE]), ALU.mult).then_inc(route_step, 1)
                dve.wait_ge(route_step, done + 9)
                dve.tensor_reduce(wtok[:, ts, :], hit[:, ts, :, :].rearrange("p t k e -> p t e k"), AX.X, ALU.add).then_inc(route_step, 1)

            dve.wait_ge(eidx_f_done, 1)
            t = NT - 1
            mask_scores(t, 0)
            outputs_low(t - 1, 1)
            mask_scores(t, 1)
            outputs_low(t - 1, 2)
            outputs_low(t - 1, 3)
            for j in range(2):
                probs_low(t, j)
            rows_low(t - 2, None)
            sums(t)
            norm(t, range(KVP))
            for a in range(KVP - 1):
                outputs_low(t, a)
            residual(t - 1)
            outputs_low(t, KVP - 1)
            route(0)
            rows_low(t - 1, None)
            residual(t)
            rows_low(t, None)
            route(1)

            def experts(i):
                for b in range(2):
                    for s in range(4):
                        step = i * 8 + (4 * b + s)
                        dve.wait_ge(m_silu, step + 1)
                        n = s // 2
                        if b == 0 and isinstance(i, int) and i == 0:
                            dve.wait_ge(w0_done, n + 1)
                        elif s == 0:
                            dve.wait_ge(wbc_in[b], (i + b) * 16)
                        dve.tensor_tensor(mgated[:, s % 2, :], msilu[:, s % 2, :], wbc[:, b, n * GROUP:(n + 1) * GROUP],
                                          ALU.mult).then_inc(m_gated, 1)
                        dve.wait_ge(m_gated, step + 1)
                        dve.tensor_tensor(mact[:, s % 2, :], mgated[:, s % 2, :], gu[1 - s % 2][1], ALU.mult).then_inc(m_act, 1)
                        dve.wait_ge(m_hi, step + 1)
                        dve.tensor_tensor(**lo_part(mact_lo[:, s % 2, :], mact[:, s % 2, :], mact_hi[:, s % 2, :])).then_inc(m_lo, 1)

            experts(0)
            with dve.Fori(1, NE // 2) as i:
                experts(i)
            dve.wait_ge(x_again, 16)
            for h in range(4):
                dve.wait_ge(m_used, 4 * NE - (2 if h < 2 else 0))
                dve.tensor_tensor(resid[:, 2 * h:2 * h + 2, :].rearrange("p t d -> p (t d)"), wide[:, h, :],
                                  x_fin[:, 2 * h:2 * h + 2, :].rearrange("p t d -> p (t d)"), ALU.add).then_inc(out_rows, 1)

        @block.tensor
        def _(pe):
            def product(out, st, mv, first, last):
                terms = ((st[0], mv[0]), (st[0], mv[1]), (st[1], mv[0]))
                for i, (a, b) in enumerate(terms):
                    mm = pe.matmul(out, a, b, start=first and i == 0, stop=last and i == 2, skip_group_check=True)
                return mm

            def turn_x(g, k):
                pe.wait_ge(x_in, 16 * (g + 1))
                if g > 0 and k > 0:
                    pe.wait_ge(xT_lo_done, KD * g + k)
                for i in range(TPG):
                    mm = pe.transpose(xT_bank(g, k)[:, i * P:(i + 1) * P], x_rows[:, i, k * P:(k + 1) * P], ident[:, :])
                mm.then_inc(xT_full, 1)

            def x_adapters(g, i):
                pe.wait_ge(lo_done, 1)
                if g > 0:
                    pe.wait_ge(*((xT_lo_done, KD * (g + 1)) if i == 0 else (xa_masked, 2 * g + i)))
                for k in range(KD):
                    pe.wait_ge(xT_lo_done, KD * g + k + 1)
                    c = (AG, AU)[i] + k * P
                    mm = product(xa_bank(g, i), (head_hi[:, c:c + P], head_lo[:, c:c + P]),
                                 (xT[g][0][:, k, :], xT[g][1][:, k, :]), k == 0, k == KD - 1)
                mm.then_inc(xa_full, 1)

            def gate_up(s):
                g, m = s // MH, s % MH
                pe.wait_ge(lo_done, 2 + m)
                pe.wait_ge(xT_lo_done, KD * (g + 1))
                if s == 1:
                    pe.wait_ge(xa_masked, 2)
                wait(pe, act_done, s - 1)
                for i, w in enumerate((WG, WU)):
                    for k in range(KD):
                        c = w + k * P
                        product(gu[m % 2][i], (cw_hi[:, m, c:c + P], cw_lo[:, m, c:c + P]),
                                (xT[g][0][:, k, :], xT[g][1][:, k, :]), k == 0, False)
                for i, c in enumerate((BG, BU)):
                    pe.wait_ge(xa_lo_done, 2 * g + i + 1)
                    mm = product(gu[m % 2][i], (cw_hi[:, m, c:c + P], cw_lo[:, m, c:c + P]),
                                 (xa_parts[g][0][:, i, :], xa_parts[g][1][:, i, :]), False, True)
                mm.then_inc(pair_full, 1)

            def down(s):
                g, m, h = s // MH, s % MH, s % 2
                pe.wait_ge(act_lo_done, s + 1)
                if m == 0:
                    wait(pe, meansq1_done, TPG * g)
                for i in range(TPG):
                    tok = slice(i * P, (i + 1) * P)
                    product(wide[:, i // 2, (i % 2) * D:(i % 2 + 1) * D], (act_hi[:, h, tok], act_lo[:, h, tok]),
                            (cw_hi[:, m, WD:WD + D], cw_lo[:, m, WD:WD + D]), m == 0 and i % 2 == 0, False)
                mm = product(wide[:, 2, :], (cw_hi[:, m, AD:AD + P], cw_lo[:, m, AD:AD + P]),
                             (act_hi[:, h, :], act_lo[:, h, :]), m == 0, m == MH - 1)
                mm.then_inc(act_used, 1)

            def down_b(g):
                pe.wait_ge(da_lo_done, g + 1)
                for i in range(TPG):
                    tok = slice(i * P, (i + 1) * P)
                    mm = product(wide[:, i // 2, (i % 2) * D:(i % 2 + 1) * D], (da_hi[:, tok], da_lo[:, tok]),
                                 (head_hi[:, BD:BD + D], head_lo[:, BD:BD + D]), False, i % 2 == 1)
                mm.then_inc(c_full, 1)

            def rows_turned(moe, attn):
                if moe is not None:
                    pe.wait_ge(h2_ready, moe + 1)
                    for k in range(KD):
                        mm = pe.transpose(kl_bank(moe)[:, k * P:(k + 1) * P], hrow[:, 0, k * P:(k + 1) * P], ident[:, :])
                if attn is not None:
                    pe.wait_ge(h_ready, attn + 1)
                    for k in range(KD):
                        mm = pe.transpose(attn_bank(attn)[:, k * P:(k + 1) * P], hrow[:, 1, k * P:(k + 1) * P], ident[:, :])
                mm.then_inc(kl_full, 1)

            def project(t, c):
                if isinstance(t, int) and t == 0:
                    pe.wait_ge(lo_done, FIRST_QKV + c + 1)
                if c == 0:
                    pe.wait_ge(hT_lo_done, t + 1)
                    wait(pe, x1_done, t - 2)
                    if isinstance(t, int) and t == 0:
                        pe.wait_ge(act_done, MH * NG - 1)
                elif c == 1:
                    wait(pe, v_lo_done, t)
                elif isinstance(t, int) and t == 0 and c in (3, QKC):
                    pe.wait_ge(*((v_lo_done, 1) if c == 3 else (qk_read, 2)))
                else:
                    pe.wait_ge(qk_read, QKC * t + c - 1)
                for k in range(KD):
                    mm = product(ringA[:, c % 2, :], (hT_hi[:, k, :], hT_lo[:, k, :]),
                                 (qkvw_hi[:, c, k, :], qkvw_lo[:, c, k, :]), k == 0, k == KD - 1)
                mm.then_inc(qk_full if c < QKC else v_full, 1)

            def turn_qk(t, c):
                pe.wait_ge(qk_roped, QKC * t + c + 1)
                if isinstance(t, int) and t == 0 and c == 0:
                    pe.wait_ge(act_done, MH * NG)
                if c < 2:
                    wait(pe, pT_lo_done, 2 * (t - 1) + c + 1)
                else:
                    pe.wait_ge(qkT_lo_done, QKC * t + c - 1)
                for n in range(GROUP // P):
                    mm = pe.transpose(ringT[:, c % 2, n * P:(n + 1) * P], qr[:, c, n * P:(n + 1) * P], ident[:, :])
                mm.then_inc(qkT_full, 1)

            def scores(t, half):
                if isinstance(t, int) and t == 0:
                    pe.wait_ge(meansq1_done, NT)
                wait(pe, o_normed, KVP * t)
                for a in range(2 * half, 2 * half + 2):
                    pe.wait_ge(qkT_lo_done, QKC * t + a + 2)
                    bank = wide[:, a, :].rearrange("p (x s k) -> p x s k", x=4, s=SPT)
                    for s in range(SPT):
                        k_ = kT_blk[:, a, s, :, :, :].rearrange("p x j k -> p (x j k)")
                        for i, qT in enumerate((qT_hi, qT_lo)):
                            mm = pe.matmul(bank[:, :, s, :], qT[:, a, s, :], k_, start=i == 0, stop=i == 1, skip_group_check=True)
                mm.then_inc(s_full, 1)

            def turn_p(t, j, before):
                pe.wait_ge(prob_done, 2 * t + j + 1)
                if before:
                    pe.wait_ge(oT_lo_done, KVP * (t - 1) + 3 + j)
                elif j == 0:
                    pe.wait_ge(qkT_lo_done, QKC)
                else:
                    pe.wait_ge(hT_lo_done, 2)
                for a in range(KVP):
                    n = j * 4 + a
                    rows = z[:, n // 2, (n % 2) * SPT:(n % 2 + 1) * SPT, :].rearrange("p s k -> p (s k)")
                    mm = pe.transpose(ringT[:, j, a * P:(a + 1) * P], rows, ident[:, :])
                mm.then_inc(pT_full, 1)

            def heads_out(t):
                pe.wait_ge(v_lo_done, t + 1)
                pe.wait_ge(v_spread, 16 * SPT * (t + 1))
                for h in range(KVH):
                    if h % 4 == 0:
                        pe.wait_ge(pT_lo_done, 2 * t + h // 4 + 1)
                    v_ = [v_blk[:, part, h, :, :].rearrange("p s d -> p (s d)") for part in range(2)]
                    mm = product(wide[:, h // 2, (h % 2) * D:(h % 2 + 1) * D], (pT_hi[:, h, :], pT_lo[:, h, :]), v_, True, True)
                mm.then_inc(o_full, 1)

            def turn_o(t, a):
                pe.wait_ge(o_normed, KVP * t + a + 1)
                if a < 2 and isinstance(t, int) and t == NT - 1:
                    pe.wait_ge(*((pT_lo_done, 2 * NT) if a == 0 else (h2T_lo_done, NT - 2)))
                elif a == 0:
                    pe.wait_ge(qkT_lo_done, QKC * (t + 2))
                elif a == 1:
                    if not isinstance(t, int) or t + 2 < NT:
                        pe.wait_ge(hT_lo_done, t + 3)
                    if isinstance(t, int):
                        wait(pe, h2T_lo_done, t - 1)
                else:
                    pe.wait_ge(oT_lo_done, KVP * t + a - 1)
                for s in range(SPT):
                    mm = pe.transpose(ringT[:, a % 2, s * P:(s + 1) * P], o_rows[:, s, a, :], ident[:, :])
                mm.then_inc(oT_full, 1)

            def attention_out(t, part, attn=True):
                if part == 0:
                    pe.wait_ge(oT_lo_done, KVP * (t + 1))
                    if isinstance(t, int) and t == 0:
                        pe.wait_ge(lo_done, FIRST_WO + OCHUNKS)
                    if attn:
                        pe.wait_ge(qk_read, QKC * (t + 3))
                    else:
                        pe.wait_ge(x1_done, t)
                for n in range(2 * part, 2 * part + 2):
                    mm = product(ringA[:, 0, 0:D], (oT_hi[:, n, :], oT_lo[:, n, :]), (wo_hi[:, n, :], wo_lo[:, n, :]),
                                 n == 0, n == KVP * QPK - 1)
                if part == OPARTS - 1:
                    mm.then_inc(y_full, 1)

            pe.wait_ge(ident_done, 1)
            for k in range(KD):
                turn_x(0, k)
            for i in range(2):
                x_adapters(0, i)
            for s in range(MH * NG):
                gate_up(s)
                if s == MH + 1:
                    down_b(0)
                elif s == MH + 2:
                    down(s - 2)
                    down(s - 1)
                elif s > 0:
                    down(s - 1)
                if X_STEP <= s < X_STEP + KD:
                    turn_x(1, s - X_STEP)
                elif XA_STEP <= s < XA_STEP + 2:
                    x_adapters(1, s - XA_STEP)
                elif s == ROWS_STEP:
                    rows_turned(None, 0)
            project(0, 0)
            down(MH * NG - 1)
            project(0, 1)
            down_b(1)
            project(0, 2)
            project(0, QKC)
            turn_qk(0, 0)
            turn_qk(0, 1)
            project(0, 3)
            project(0, 4)
            for c in range(2, QKC):
                turn_qk(0, c)
            pe.wait_ge(qkT_lo_done, 4)
            rows_turned(None, 1)

            def logits(tiles, last=False):
                for t in tiles:
                    pe.wait_ge(h2T_lo_done, t + 1)
                    for k in range(KD):
                        tok = slice(t * P, (t + 1) * P)
                        mm = product(logit_bank(t)[:, t * NE:(t + 1) * NE], (h2T_hi[:, k, tok], h2T_lo[:, k, tok]),
                                     (wg_hi[:, k, :], wg_lo[:, k, :]), k == 0, k == KD - 1)
                if last:
                    mm.then_inc(logit_full, 1)

            def attend(t, before=True, moe=True, rows=True):
                scores(t, 0)
                if before:
                    turn_o(t - 1, 1)
                scores(t, 1)
                project(t + 1, 0)
                if before:
                    turn_o(t - 1, 2)
                    turn_o(t - 1, 3)
                project(t + 1, 1)
                project(t + 1, 2)
                turn_p(t, 0, before)
                turn_p(t, 1, before)
                project(t + 1, 3)
                heads_out(t)
                if before:
                    project(t + 1, 4)
                    turn_qk(t + 1, 0)
                    project(t + 1, QKC)
                    turn_qk(t + 1, 1)
                    attention_out(t - 1, 0)
                    for c in range(2, QKC):
                        attention_out(t - 1, c - 1)
                        turn_qk(t + 1, c)
                    attention_out(t - 1, QKC - 1)
                    attention_out(t - 1, QKC)
                else:
                    turn_qk(t + 1, 0)
                    turn_qk(t + 1, 1)
                    project(t + 1, 4)
                    turn_qk(t + 1, 2)
                    project(t + 1, QKC)
                    turn_qk(t + 1, 3)
                    turn_qk(t + 1, 4)
                if rows or moe:
                    pe.wait_ge(qkT_lo_done, QKC * (t + 1) + 4)
                    rows_turned(t - 2 if moe else None, t + 2 if rows else None)
                if before:
                    attention_out(t - 1, QKC + 1)
                turn_o(t, 0)
                if before:
                    attention_out(t - 1, QKC + 2)

            attend(0, before=False, moe=False)
            attend(1, moe=False)
            attend(2)
            with pe.Fori(3, NT - 2) as t:
                attend(t)
            attend(NT - 2, rows=False)
            def gate_up_e(e, b, n, j):
                step = e * 4 + (2 * n + j)
                if n == 0 and j == 0:
                    pe.wait_ge(ew_lo_done, 2 * e + 1)
                wait(pe, m_act, step - 1)
                if isinstance(e, int) and step == 1:
                    pe.wait_ge(logit_done, 1)
                    pe.wait_ge(x1_done, NT)
                for i in range(2):
                    for k in range(KD):
                        c = (i * KD + k) * D + j * P
                        tok = slice(n * GROUP, (n + 1) * GROUP)
                        mm = product(gu[1 - j][i], (ew_hi[:, b, c:c + P], ew_lo[:, b, c:c + P]),
                                     (h2T_hi[:, k, tok], h2T_lo[:, k, tok]), k == 0, k == KD - 1)
                mm.then_inc(m_full, 1)

            def down_e(e, b, n, j, last=False):
                pe.wait_ge(m_lo, e * 4 + (2 * n + j + 1))
                if n == 0 and j == 0:
                    pe.wait_ge(ew_lo_done, 2 * e + 2)
                c = (2 * KD + j) * D
                for i in range(TPG):
                    tile = n * TPG + i
                    tok = slice(i * P, (i + 1) * P)
                    mm = product(wide[:, tile // 2, (tile % 2) * D:(tile % 2 + 1) * D], (mact_hi[:, j, tok], mact_lo[:, j, tok]),
                                 (ew_hi[:, b, c:c + D], ew_lo[:, b, c:c + D]), False, last)
                mm.then_inc(m_used, 1)

            def seed(tiles):
                for tile in tiles:
                    pe.matmul(wide[:, tile // 2, (tile % 2) * D:(tile % 2 + 1) * D], ident[:, :], resid[:, tile, :],
                              start=tile % 2 == 0, stop=False, skip_group_check=True)

            STEPS = [(b, n, j) for b in range(2) for n in range(2) for j in range(2)]

            t = NT - 1
            scores(t, 0)
            turn_o(t - 1, 1)
            scores(t, 1)
            turn_o(t - 1, 2)
            turn_o(t - 1, 3)
            pe.wait_ge(lo_done, NCH)
            pe.wait_ge(v_lo_done, NT)
            logits(range(3))
            for j in range(2):
                turn_p(t, j, True)
            attention_out(t - 1, 0, False)
            attention_out(t - 1, 1, False)
            pe.wait_ge(pT_lo_done, 2 * NT)
            rows_turned(t - 2, None)
            heads_out(t)
            attention_out(t - 1, 2, False)
            attention_out(t - 1, 3, False)
            turn_o(t, 0)
            turn_o(t, 1)
            for a in range(2, KVP):
                logits([a + 1])
                attention_out(t - 1, 2 * a, False)
                attention_out(t - 1, 2 * a + 1, False)
                turn_o(t, a)
            logits([t - 2], True)
            seed(range(4))
            for part in range(OPARTS):
                attention_out(t, part, False)
                if part == OPARTS // 2 - 1:
                    rows_turned(t - 1, None)
            logits([NT - 2])
            gate_up_e(0, 0, 0, 0)
            rows_turned(NT - 1, None)
            logits([NT - 1], True)
            gate_up_e(0, *STEPS[1])
            pe.wait_ge(route_step, ROUTE_STEPS * 2)
            pe.transpose(wide[:, 3, 0:P], wtok[:, :, :].rearrange("p t e -> p (t e)"), ident[:, :]).then_inc(wT_full, 1)
            pe.wait_ge(wT_done, 1)
            for t in range(NT):
                mm = pe.matmul(wide[:, 2 + t // TPG, (t % TPG) * P:(t % TPG + 1) * P],
                               ident[:, t * NE:t * NE + 1].broadcast_to([P, P]), wT[:, :], start=True, stop=True, skip_group_check=True)
                if t % TPG == TPG - 1:
                    mm.then_inc(w0_full, 1)
            pe.wait_ge(x1_done, NT)
            for n in range(2):
                pe.wait_ge(w0_done, n + 1)
                seed(range(TPG + 2 * n, TPG + 2 * n + 2))

            def experts(i, last=False):
                for s, (b, n, j) in enumerate(STEPS):
                    if s + 2 < len(STEPS):
                        b2, n2, j2 = STEPS[s + 2]
                        gate_up_e(i * 2 + b2, b2, n2, j2)
                    elif not last:
                        gate_up_e(i * 2 + 2, *STEPS[s + 2 - len(STEPS)])
                    down_e(i * 2 + b, b, n, j, last and b == 1)

            experts(0)
            with pe.Fori(1, NE // 2 - 1) as i:
                experts(i)
            experts(NE // 2 - 1, last=True)


_INPUTS = ["x", "seq_adapter", "cond_head", "cond_w", "qkv_w", "wo_w", "gate_w", "expert_w", "norms", "consts"]


def lay_out(inputs):
    def ktiles(w):
        return w.reshape(-1, P, w.shape[-1]).transpose(1, 0, 2)

    i = {k: np.asarray(v) for k, v in inputs.items()}

    def adapters(w):
        return w.transpose(1, 0, 2).reshape(w.shape[1], NAD * RANK)

    ag, au, ad = (ktiles(adapters(i["L0_cond_A" + c])) for c in "gud")
    bg, bu, bd = (i["L0_cond_B" + c].reshape(NAD * RANK, -1) for c in "gud")
    wg, wu, wd = (ktiles(i["L0_cond_W" + c]) for c in "gud")
    head = np.concatenate([ag.reshape(P, -1), au.reshape(P, -1), bd], 1)

    def hid(w):
        return w.reshape(P, KD, MH, P).transpose(0, 2, 1, 3).reshape(P, MH, KD * P)

    cond = np.concatenate([hid(wg), hid(wu), bg.reshape(P, MH, P), bu.reshape(P, MH, P), wd, ad], 2)
    q = ktiles(i["L0_ffn_wq"]).reshape(P, KD, KVP, 2, QPK, HD).transpose(0, 1, 2, 4, 3, 5).reshape(P, KD, KVP, GROUP)
    k, v = (ktiles(i["L0_ffn_w" + c])[:, :, None, :] for c in "kv")
    qkv = np.concatenate([k, q, v], 2).transpose(0, 2, 1, 3).reshape(P, QCHUNKS, KD * GROUP)
    wo = i["L0_ffn_wo"].reshape(KVP, 2, QPK, HD, D).transpose(1, 3, 0, 2, 4).reshape(P, KVP * QPK, D)
    gate = ktiles(i["L0_ffn_wg"]).reshape(P, KD * NE)
    ew = np.stack([i["L0_ffn_" + n].reshape(NE, KD, P, D) for n in ("w1", "w3", "w2")], 1)
    ew = ew.transpose(0, 3, 1, 2, 4).reshape(NE, P, ECOLS)
    norms = np.concatenate([i["L0_ffn_ln_w"].reshape(KD, P).T, i["L0_ffn_ff_ln_w"].reshape(KD, P).T], 1)
    half = HD // 2
    inv = (1.0 / np.float32(150000.0) ** (np.arange(half, dtype=np.float32) / np.float32(half))).astype(np.float32)
    ang = (np.arange(SEQ, dtype=np.float32)[:, None] * inv).astype(np.float32)
    cos, sin = np.cos(ang), np.sin(ang)
    rope = np.tile(np.concatenate([cos, cos, sin, -sin], 1), (SPT, 1))
    pos = np.arange(P) % SEQ
    mask = np.tile(np.where(np.arange(SEQ)[None, :] <= pos[:, None], 0.0, -1e30), (1, 2 * SPT)).astype(np.float32)
    consts = np.concatenate([rope, mask], 1).astype(np.float32)
    arrays = dict(x=i["x"], seq_adapter=i["itok_B_0_7"], cond_head=head, cond_w=cond, qkv_w=qkv, wo_w=wo,
                  gate_w=gate, expert_w=ew, norms=norms, consts=consts)
    return {k: np.ascontiguousarray(v) for k, v in arrays.items()}


def kernel(**inputs):
    import concourse.bacc as bacc
    from concourse.bass_utils import run_bass_kernel_spmd

    nc = bacc.Bacc("TRN2", target_bir_lowering=False, num_devices=1)
    laid = lay_out(inputs)
    args = [nc.dram_tensor(f"in_{n}", laid[n].shape, mybir.dt.from_np(laid[n].dtype), kind="ExternalInput").ap() for n in _INPUTS]
    out = nc.dram_tensor("out_0", inputs["x"].shape, F32, kind="ExternalOutput").ap()
    build(nc, *args, out)
    result = run_bass_kernel_spmd(nc, [{f"in_{n}": laid[n] for n in _INPUTS}], core_ids=[0])
    return result.results[0]["out_0"]
```
